# Optimizing a Trainium2 kernel written in Bass

```python
import numpy as np
import jax
import jax.numpy as jnp

def _softmax(x, axis=-1):
    return jax.nn.softmax(x, axis=axis)

def _gelu(x):
    return jax.nn.gelu(x, approximate=True)

def _silu(x):
    return jax.nn.silu(x)

def _sigmoid(x):
    return jax.nn.sigmoid(x)

def _layernorm(x, axis=-1, eps=1e-05):
    m = jnp.mean(x, axis=axis, keepdims=True)
    v = jnp.var(x, axis=axis, keepdims=True)
    return (x - m) / jnp.sqrt(v + eps)

def _scatter_add(tgt, idx, src, axis=0):
    return tgt.at[idx].add(src)

def _segment_sum(src, seg, n):
    return jax.ops.segment_sum(src, seg, n)
kernel_name = 'mk_xattn_ffn_d2_seqx_r4_781757'

def setup_inputs(seed: int=0):
    np.random.seed(seed)
    _w = jnp.asarray

    def _rec_inputs():
        import jax
        import jax.numpy as jnp
        _rk = jax.random.key(seed)
        x = 7.22e-05 + 1 * jax.random.normal(jax.random.fold_in(_rk, 1), (8, 256, 512), jnp.float32)
        _lenS = 256 - jax.random.randint(jax.random.fold_in(_rk, 7), (8,), 0, max(1, 256 // 4) + 1, jnp.int32)
        _lenS2 = 256 - jax.random.randint(jax.random.fold_in(_rk, 8), (8,), 0, max(1, 256 // 4) + 1, jnp.int32)
        _ctx_2048P = jax.random.normal(jax.random.fold_in(_rk, 11), (8, 16, 512), jnp.float32)
        _ctx_2048c = jax.random.dirichlet(jax.random.fold_in(_rk, 511), 0.3 * jnp.ones((16,), jnp.float32), (8, 256))
        _ctx_2048t = jnp.einsum('bsk,bkd->bsd', _ctx_2048c, _ctx_2048P)
        _ctx_2048t = _ctx_2048t * jax.lax.rsqrt(jnp.mean(jnp.square(_ctx_2048t)) + 1e-12) * 0.953939
        ctx_2048 = 4.13588e-05 + 0.999923 * (_ctx_2048t + 0.3 * jax.random.normal(jax.random.fold_in(_rk, 611), (8, 256, 512), jnp.float32))
        return (x, ctx_2048)
    x, ctx_2048 = _rec_inputs()

    def _L0_xattn_setup():
        import jax, jax.numpy as jnp
        import numpy as np
        B, S, DIM, HD = (4, 256, 512, 128)
        H = DIM // HD
        GN_EPS = 0.001

        def _decay_masks(n_heads, seq_len):
            gam = 1.0 - 2.0 ** (-5.0 - jnp.arange(n_heads, dtype=jnp.float32))
            idx = jnp.arange(seq_len, dtype=jnp.float32)
            expo = idx[None, :] - idx[:, None]
            D = jnp.where(expo[None, :, :] <= 0, gam[:, None, None] ** expo[None, :, :], 0.0)
            return D / jnp.sqrt(D.sum(axis=-1))[:, None, :]
        key = jax.random.key(seed)
        ks = jax.random.split(key, 8)
        x = jax.random.normal(ks[0], (B, S, DIM), dtype=jnp.float32)
        k = jax.random.normal(ks[1], (B, S, DIM), dtype=jnp.float32)
        v = jax.random.normal(ks[2], (B, S, DIM), dtype=jnp.float32)
        Wh = jax.random.normal(ks[3], (H, HD, HD), dtype=jnp.float32) / np.sqrt(HD)
        wg_w = jax.random.normal(ks[4], (DIM, DIM), dtype=jnp.float32) / np.sqrt(DIM)
        wo_w = jax.random.normal(ks[5], (DIM, DIM), dtype=jnp.float32) / np.sqrt(DIM)
        gn_gamma = jnp.ones((DIM,), dtype=jnp.float32)
        gn_beta = jnp.zeros((DIM,), dtype=jnp.float32)
        return {'x': x, 'k': k, 'v': v, 'Wh': Wh, 'wg_w': wg_w, 'wo_w': wo_w, 'gn_gamma': gn_gamma, 'gn_beta': gn_beta}
    _L0_xattn_all = _L0_xattn_setup()
    _L0_xattn_in = {k: v for k, v in _L0_xattn_all.items() if k in ('Wh', 'wg_w', 'wo_w', 'gn_gamma', 'gn_beta')}
    del _L0_xattn_all

    def _L0_ffn_setup():
        import jax, jax.numpy as jnp
        import numpy as np
        EPS = 1e-05

        def act_quant(x):
            scale = 127.0 / jnp.clip(jnp.max(jnp.abs(x), axis=-1, keepdims=True), EPS)
            return jnp.clip(jnp.round(x * scale), -128.0, 127.0) / scale

        def weight_quant(w):
            scale = 1.0 / jnp.clip(jnp.mean(jnp.abs(w)), EPS)
            return jnp.clip(jnp.round(w * scale), -1.0, 1.0) / scale

        def bitlinear(x, w):
            return jnp.einsum('bsd,hd->bsh', act_quant(x), weight_quant(w))
        key = jax.random.key(seed)
        k0, k1, k2, k3 = jax.random.split(key, 4)
        d_model, hidden_dim = (512, 1408)
        B, S = (4, 512)
        x = jax.random.normal(k0, (B, S, d_model), dtype=jnp.float32)
        std = 0.02
        w1 = jax.random.normal(k1, (hidden_dim, d_model), dtype=jnp.float32) * std
        w2 = jax.random.normal(k2, (d_model, hidden_dim), dtype=jnp.float32) * std
        w3 = jax.random.normal(k3, (hidden_dim, d_model), dtype=jnp.float32) * std
        return {'x': x, 'w1': w1, 'w2': w2, 'w3': w3}
    _L0_ffn_all = _L0_ffn_setup()
    _L0_ffn_in = {k: v for k, v in _L0_ffn_all.items() if k in ('w1', 'w2', 'w3')}
    del _L0_ffn_all

    def _L1_xattn_setup():
        import jax, jax.numpy as jnp
        import numpy as np
        B, S, E, NH = (2, 256, 512, 16)
        DH = E // NH
        EPS = 1e-06

        def _mlstm_forward(q, k, v, Wi, bi, Wf, bf, ln_scale):
            b, s, e = q.shape
            nh = Wi.shape[1]
            dh = e // nh
            x = jnp.concatenate([q, k, v], axis=-1)
            ig = (x @ Wi + bi).transpose(0, 2, 1)[..., None]
            fg = (x @ Wf + bf).transpose(0, 2, 1)[..., None]
            split = lambda t: t.reshape(b, s, nh, dh).transpose(0, 2, 1, 3)
            qh, kh, vh = (split(q), split(k), split(v))
            log_f = jax.nn.log_sigmoid(fg)
            log_f_cum = jnp.concatenate([jnp.zeros((b, nh, 1, 1), q.dtype), jnp.cumsum(log_f, axis=2)], axis=2)
            fg_mat = log_f_cum - jnp.transpose(log_f_cum, (0, 1, 3, 2))
            ltr = jnp.tril(jnp.ones((s, s), dtype=bool))
            log_fg = jnp.where(ltr, fg_mat[:, :, 1:, 1:], -jnp.inf)
            log_D = log_fg + jnp.transpose(ig, (0, 1, 3, 2))
            max_log_D = jnp.max(log_D, axis=-1, keepdims=True)
            D = jnp.exp(log_D - max_log_D)
            qk = jnp.einsum('bhsd,bhtd->bhst', qh, kh) / jnp.sqrt(jnp.asarray(dh, q.dtype))
            C = qk * D
            normalizer = jnp.maximum(jnp.abs(C.sum(-1, keepdims=True)), jnp.exp(-max_log_D))
            Cn = C / (normalizer + EPS)
            h = jnp.einsum('bhst,bhtd->bhsd', Cn, vh)
            mu = h.mean(-1, keepdims=True)
            var = ((h - mu) ** 2).mean(-1, keepdims=True)
            hn = (h - mu) * jax.lax.rsqrt(var + EPS)
            hn = hn * ln_scale.reshape(1, nh, 1, dh)
            return hn.transpose(0, 2, 1, 3).reshape(b, s, e)
        key = jax.random.key(seed)
        ks = jax.random.split(key, 6)
        q = jax.random.normal(ks[0], (B, S, E), dtype=jnp.float32)
        k = jax.random.normal(ks[1], (B, S, E), dtype=jnp.float32)
        v = jax.random.normal(ks[2], (B, S, E), dtype=jnp.float32)
        Wi = jax.random.normal(ks[3], (3 * E, NH), dtype=jnp.float32) * 0.02
        bi = jax.random.normal(ks[4], (NH,), dtype=jnp.float32) * 0.1
        Wf = jax.random.normal(ks[5], (3 * E, NH), dtype=jnp.float32) * 0.02
        bf = jnp.linspace(3.0, 6.0, NH, dtype=jnp.float32)
        ln_scale = jnp.ones((E,), dtype=jnp.float32)
        return {'q': q, 'k': k, 'v': v, 'Wi': Wi, 'bi': bi, 'Wf': Wf, 'bf': bf, 'ln_scale': ln_scale}
    _L1_xattn_all = _L1_xattn_setup()
    _L1_xattn_in = {k: v for k, v in _L1_xattn_all.items() if k in ('Wi', 'bi', 'Wf', 'bf', 'ln_scale')}
    del _L1_xattn_all

    def _L1_ffn_setup():
        import jax, jax.numpy as jnp
        import numpy as np
        H = 512
        I = 256
        E = 32
        K = 4
        N_SHARED = 1
        EPS = 1e-06

        def _rmsnorm(x, w, eps=EPS):
            var = jnp.mean(jnp.square(x), axis=-1, keepdims=True)
            return x * jax.lax.rsqrt(var + eps) * w

        def _moe_core(x, gate_w, w13, w2):
            T = x.shape[0]
            N = T * K
            C = 2 * N // E
            logits = jnp.einsum('th,eh->te', x.astype(jnp.float32), gate_w.astype(jnp.float32))
            scores = jax.nn.softmax(logits, axis=-1)
            topk_w, topk_ids = jax.lax.top_k(scores, K)
            topk_w = topk_w / jnp.sum(topk_w, axis=-1, keepdims=True)
            flat_ids = topk_ids.reshape(-1)
            flat_w = topk_w.reshape(-1)
            order = jnp.argsort(flat_ids)
            sorted_eid = flat_ids[order]
            tok = order // K
            counts = jnp.zeros((E,), jnp.int32).at[flat_ids].add(1)
            starts = jnp.cumsum(counts) - counts
            pos = jnp.arange(N) - starts[sorted_eid]
            buf = jnp.zeros((E, C, x.shape[1]), x.dtype).at[sorted_eid, pos].set(x[tok], mode='drop')
            gu = jnp.einsum('ech,ehf->ecf', buf, w13)
            g, u = jnp.split(gu, 2, axis=-1)
            act = jax.nn.silu(g) * u
            eo = jnp.einsum('eci,eih->ech', act, w2)
            out_slots = eo[sorted_eid, pos]
            routed = jnp.zeros_like(x).at[tok].add(out_slots * flat_w[order][:, None])
            return routed
        key = jax.random.key(seed)
        ks = jax.random.split(key, 8)
        s = 1.0 / np.sqrt(H)
        si = 1.0 / np.sqrt(I)
        return {'hidden_states': jax.random.normal(ks[0], (1, 1024, H), jnp.float32), 'norm_w': jnp.ones((H,), jnp.float32), 'gate_w': jax.random.normal(ks[1], (E, H), jnp.float32) * s, 'w13': jax.random.normal(ks[2], (E, H, 2 * I), jnp.float32) * s, 'w2': jax.random.normal(ks[3], (E, I, H), jnp.float32) * si, 'shared_gate_w': jax.random.normal(ks[4], (H, I * N_SHARED), jnp.float32) * s, 'shared_up_w': jax.random.normal(ks[5], (H, I * N_SHARED), jnp.float32) * s, 'shared_down_w': jax.random.normal(ks[6], (I * N_SHARED, H), jnp.float32) * si}
    _L1_ffn_all = _L1_ffn_setup()
    _L1_ffn_in = {k: v for k, v in _L1_ffn_all.items() if k in ('norm_w', 'gate_w', 'w13', 'w2', 'shared_gate_w', 'shared_up_w', 'shared_down_w')}
    del _L1_ffn_all
    return {'x': x, 'ctx_2048': ctx_2048, 'L0_xattn_Wh': _L0_xattn_in['Wh'], 'L0_xattn_wg_w': _L0_xattn_in['wg_w'], 'L0_xattn_wo_w': _L0_xattn_in['wo_w'], 'L0_xattn_gn_gamma': _L0_xattn_in['gn_gamma'], 'L0_xattn_gn_beta': _L0_xattn_in['gn_beta'], 'L0_ffn_w1': _L0_ffn_in['w1'], 'L0_ffn_w2': _L0_ffn_in['w2'], 'L0_ffn_w3': _L0_ffn_in['w3'], 'L1_xattn_Wi': _L1_xattn_in['Wi'], 'L1_xattn_bi': _L1_xattn_in['bi'], 'L1_xattn_Wf': _L1_xattn_in['Wf'], 'L1_xattn_bf': _L1_xattn_in['bf'], 'L1_xattn_ln_scale': _L1_xattn_in['ln_scale'], 'L1_ffn_norm_w': _L1_ffn_in['norm_w'], 'L1_ffn_gate_w': _L1_ffn_in['gate_w'], 'L1_ffn_w13': _L1_ffn_in['w13'], 'L1_ffn_w2': _L1_ffn_in['w2'], 'L1_ffn_shared_gate_w': _L1_ffn_in['shared_gate_w'], 'L1_ffn_shared_up_w': _L1_ffn_in['shared_up_w'], 'L1_ffn_shared_down_w': _L1_ffn_in['shared_down_w']}

def reference(x, ctx_2048, L0_xattn_Wh, L0_xattn_wg_w, L0_xattn_wo_w, L0_xattn_gn_gamma, L0_xattn_gn_beta, L0_ffn_w1, L0_ffn_w2, L0_ffn_w3, L1_xattn_Wi, L1_xattn_bi, L1_xattn_Wf, L1_xattn_bf, L1_xattn_ln_scale, L1_ffn_norm_w, L1_ffn_gate_w, L1_ffn_w13, L1_ffn_w2, L1_ffn_shared_gate_w, L1_ffn_shared_up_w, L1_ffn_shared_down_w):
    import jax
    import jax.numpy as jnp

    def _L0_xattn_ref(x, k, v, Wh, wg_w, wo_w, gn_gamma, gn_beta):
        import jax, jax.numpy as jnp
        import numpy as np
        B, S, DIM, HD = (4, 256, 512, 128)
        H = DIM // HD
        GN_EPS = 0.001

        def _decay_masks(n_heads, seq_len):
            gam = 1.0 - 2.0 ** (-5.0 - jnp.arange(n_heads, dtype=jnp.float32))
            idx = jnp.arange(seq_len, dtype=jnp.float32)
            expo = idx[None, :] - idx[:, None]
            D = jnp.where(expo[None, :, :] <= 0, gam[:, None, None] ** expo[None, :, :], 0.0)
            return D / jnp.sqrt(D.sum(axis=-1))[:, None, :]
        b, s, dim = x.shape
        h, hd, _ = Wh.shape
        xh = x.reshape(b, s, h, hd)
        kh = k.reshape(b, s, h, hd)
        vh = v.reshape(b, s, h, hd)
        Q = jnp.einsum('bshd,hde->bshe', xh, Wh)
        K = jnp.einsum('bshd,hde->bshe', kh, Wh)
        V = jnp.einsum('bshd,hde->bshe', vh, Wh)
        scores = jnp.einsum('bshe,bthe->bhst', Q, K) / jnp.sqrt(jnp.float32(hd))
        Dn = _decay_masks(h, s)
        masked = scores * Dn[None, :, :, :]
        A = jnp.maximum(jnp.abs(masked.sum(axis=0)), 1.0)
        O = jnp.einsum('hst,bthe->bshe', A, V).reshape(b, s, dim)
        mu = O.mean(axis=-1, keepdims=True)
        var = O.var(axis=-1, keepdims=True)
        Y = (O - mu) / jnp.sqrt(var + GN_EPS) * gn_gamma + gn_beta
        W = jax.nn.relu(x @ wg_w)
        return W * Y @ wo_w

    def _L0_ffn_ref(x, w1, w2, w3):
        import jax, jax.numpy as jnp
        import numpy as np
        EPS = 1e-05

        def act_quant(x):
            scale = 127.0 / jnp.clip(jnp.max(jnp.abs(x), axis=-1, keepdims=True), EPS)
            return jnp.clip(jnp.round(x * scale), -128.0, 127.0) / scale

        def weight_quant(w):
            scale = 1.0 / jnp.clip(jnp.mean(jnp.abs(w)), EPS)
            return jnp.clip(jnp.round(w * scale), -1.0, 1.0) / scale

        def bitlinear(x, w):
            return jnp.einsum('bsd,hd->bsh', act_quant(x), weight_quant(w))
        h = jax.nn.silu(bitlinear(x, w1)) * bitlinear(x, w3)
        return bitlinear(h, w2)

    def _L1_xattn_ref(q, k, v, Wi, bi, Wf, bf, ln_scale):
        import jax, jax.numpy as jnp
        import numpy as np
        B, S, E, NH = (2, 256, 512, 16)
        DH = E // NH
        EPS = 1e-06

        def _mlstm_forward(q, k, v, Wi, bi, Wf, bf, ln_scale):
            b, s, e = q.shape
            nh = Wi.shape[1]
            dh = e // nh
            x = jnp.concatenate([q, k, v], axis=-1)
            ig = (x @ Wi + bi).transpose(0, 2, 1)[..., None]
            fg = (x @ Wf + bf).transpose(0, 2, 1)[..., None]
            split = lambda t: t.reshape(b, s, nh, dh).transpose(0, 2, 1, 3)
            qh, kh, vh = (split(q), split(k), split(v))
            log_f = jax.nn.log_sigmoid(fg)
            log_f_cum = jnp.concatenate([jnp.zeros((b, nh, 1, 1), q.dtype), jnp.cumsum(log_f, axis=2)], axis=2)
            fg_mat = log_f_cum - jnp.transpose(log_f_cum, (0, 1, 3, 2))
            ltr = jnp.tril(jnp.ones((s, s), dtype=bool))
            log_fg = jnp.where(ltr, fg_mat[:, :, 1:, 1:], -jnp.inf)
            log_D = log_fg + jnp.transpose(ig, (0, 1, 3, 2))
            max_log_D = jnp.max(log_D, axis=-1, keepdims=True)
            D = jnp.exp(log_D - max_log_D)
            qk = jnp.einsum('bhsd,bhtd->bhst', qh, kh) / jnp.sqrt(jnp.asarray(dh, q.dtype))
            C = qk * D
            normalizer = jnp.maximum(jnp.abs(C.sum(-1, keepdims=True)), jnp.exp(-max_log_D))
            Cn = C / (normalizer + EPS)
            h = jnp.einsum('bhst,bhtd->bhsd', Cn, vh)
            mu = h.mean(-1, keepdims=True)
            var = ((h - mu) ** 2).mean(-1, keepdims=True)
            hn = (h - mu) * jax.lax.rsqrt(var + EPS)
            hn = hn * ln_scale.reshape(1, nh, 1, dh)
            return hn.transpose(0, 2, 1, 3).reshape(b, s, e)
        return _mlstm_forward(q, k, v, Wi, bi, Wf, bf, ln_scale)

    def _L1_ffn_ref(hidden_states, norm_w, gate_w, w13, w2, shared_gate_w, shared_up_w, shared_down_w):
        import jax, jax.numpy as jnp
        import numpy as np
        H = 512
        I = 256
        E = 32
        K = 4
        N_SHARED = 1
        EPS = 1e-06

        def _rmsnorm(x, w, eps=EPS):
            var = jnp.mean(jnp.square(x), axis=-1, keepdims=True)
            return x * jax.lax.rsqrt(var + eps) * w

        def _moe_core(x, gate_w, w13, w2):
            T = x.shape[0]
            N = T * K
            C = 2 * N // E
            logits = jnp.einsum('th,eh->te', x.astype(jnp.float32), gate_w.astype(jnp.float32))
            scores = jax.nn.softmax(logits, axis=-1)
            topk_w, topk_ids = jax.lax.top_k(scores, K)
            topk_w = topk_w / jnp.sum(topk_w, axis=-1, keepdims=True)
            flat_ids = topk_ids.reshape(-1)
            flat_w = topk_w.reshape(-1)
            order = jnp.argsort(flat_ids)
            sorted_eid = flat_ids[order]
            tok = order // K
            counts = jnp.zeros((E,), jnp.int32).at[flat_ids].add(1)
            starts = jnp.cumsum(counts) - counts
            pos = jnp.arange(N) - starts[sorted_eid]
            buf = jnp.zeros((E, C, x.shape[1]), x.dtype).at[sorted_eid, pos].set(x[tok], mode='drop')
            gu = jnp.einsum('ech,ehf->ecf', buf, w13)
            g, u = jnp.split(gu, 2, axis=-1)
            act = jax.nn.silu(g) * u
            eo = jnp.einsum('eci,eih->ech', act, w2)
            out_slots = eo[sorted_eid, pos]
            routed = jnp.zeros_like(x).at[tok].add(out_slots * flat_w[order][:, None])
            return routed
        B, S, Hd = hidden_states.shape
        residual = hidden_states
        h = _rmsnorm(hidden_states, norm_w)
        x = h.reshape(-1, Hd)
        routed = _moe_core(x, gate_w, w13, w2)
        shared = jax.nn.silu(x @ shared_gate_w) * (x @ shared_up_w) @ shared_down_w
        out = residual + (routed + shared).reshape(B, S, Hd)
        return out
    x = x + _L0_xattn_ref(_layernorm(x, axis=-1), ctx_2048, ctx_2048, L0_xattn_Wh, L0_xattn_wg_w, L0_xattn_wo_w, L0_xattn_gn_gamma, L0_xattn_gn_beta)
    x = x + _L0_ffn_ref(_layernorm(x, axis=-1), L0_ffn_w1, L0_ffn_w2, L0_ffn_w3)
    x = x + _L1_xattn_ref(_layernorm(x, axis=-1), ctx_2048, ctx_2048, L1_xattn_Wi, L1_xattn_bi, L1_xattn_Wf, L1_xattn_bf, L1_xattn_ln_scale)
    x = x + _L1_ffn_ref(_layernorm(x, axis=-1), L1_ffn_norm_w, L1_ffn_gate_w, L1_ffn_w13, L1_ffn_w2, L1_ffn_shared_gate_w, L1_ffn_shared_up_w, L1_ffn_shared_down_w)
    return x

_drawn_inputs = setup_inputs


def setup_inputs(seed=0):
    import zlib

    import numpy as np

    out = dict(_drawn_inputs(seed))
    spreads = {'L0_xattn_gn_gamma': (1.0, 0.2),
     'L0_xattn_gn_beta': (0.0, 0.1),
     'L1_xattn_ln_scale': (1.0, 0.2),
     'L1_ffn_norm_w': (1.0, 0.2)}
    factors = {'L1_xattn_bi': 64.0}
    for name, (base, spread) in spreads.items():
        noise = np.random.default_rng([zlib.crc32(name.encode()), seed]).standard_normal(out[name].shape)
        drawn = base * np.exp(spread * noise) if base else spread * noise
        out[name] = jnp.asarray(drawn.astype(out[name].dtype))
    for name, factor in factors.items():
        out[name] = (out[name] * factor).astype(out[name].dtype)
    return out
```

```python
from contextlib import ExitStack, contextmanager

import numpy as np

import concourse.bass as bass
from concourse import mybir

ALU = mybir.AluOpType
ACT = mybir.ActivationFunctionType
AX = mybir.AxisListType
F32 = mybir.dt.float32
BF16 = mybir.dt.bfloat16
I32 = mybir.dt.int32
U32 = mybir.dt.uint32
ds = bass.ds

P = 128
B, S, D = 8, 256, 512
KD = D // P
CB = S // P
T = B * S
NT = T // P
LN_EPS = 1e-5
H0 = 4
HD = D // H0
GN_EPS = 1e-3
F0 = 1408
KF = F0 // P
Q_EPS = 1e-5
ROUND = float(1.5 * 2 ** 23)
NH = 16
DH = D // NH
HG = P // DH
NG = NH // HG
M_EPS = 1e-6
MASKED = -1e30
NE, TOPK, FI = 32, 4, 256
CAP = 2 * T * TOPK // NE
RT = CAP // P
KI = FI // P
ROUTES = NE * RT


class Steps:

    def __init__(self, eng, sem):
        self.eng, self.sem, self.n, self.base = eng, sem, 0, 0

    def did(self, ins):
        ins.then_inc(self.sem, 1)
        self.n += 1

    def settle(self):
        self.eng.wait_ge(self.sem, self.base + self.n)

    def then(self, ins):
        self.did(ins)
        self.settle()

    @contextmanager
    def loop(self, lo, hi, per):
        before = self.n
        with self.eng.Fori(lo, hi) as i:
            self.base, self.n = (i - lo) * per + before, 0
            yield i
            assert self.n == per, f"{self.sem}: {self.n} steps in a round"
        self.base, self.n = 0, before + (hi - lo) * per


def shape_constants():
    gam = 1.0 - 2.0 ** (-5.0 - np.arange(H0, dtype=np.float64))
    pos = np.arange(S, dtype=np.float64)
    expo = pos[None, :] - pos[:, None]
    dec = np.where(expo[None] <= 0, gam[:, None, None] ** np.minimum(expo, 0)[None], 0.0)
    dec = dec / np.sqrt(dec.sum(-1))[:, None, :] / np.sqrt(float(HD))
    dect = dec.transpose(2, 0, 1)
    first = dect[:P].reshape(P, H0 * S)
    second = dect[P:, :, P:].reshape(P, H0 * P)
    decay = np.concatenate([first, second], 1).astype(np.float32)
    r = np.arange(P)
    ident = np.eye(P, dtype=np.float32)
    future = np.where(r[:, None] <= r[None, :], 0.0, MASKED).astype(np.float32)
    before = (r[:, None] < r[None, :]).astype(np.float32)
    iota = np.broadcast_to(r.astype(np.float32), (P, P))
    token = (np.arange(NT)[None, :] * P + r[:, None] - T).astype(np.float32)
    return np.concatenate([decay, ident, future, before, iota, token], 1)


C_DEC, C_ID = 0, H0 * (S + P)
C_FUT, C_BEF, C_IOTA, C_TOK = C_ID + P, C_ID + 2 * P, C_ID + 3 * P, C_ID + 4 * P
C_ALL = C_TOK + NT


def program(nc, a, out, upto=99):
    with ExitStack() as top:
        held = [ExitStack(), []]

        def sem(name):
            held[1].append(held[0].enter_context(nc.semaphore(name)))
            return held[1][-1]

        def clear_semaphores():
            with nc.Block() as block:
                @block.gpsimd
                def _(pool):
                    nums = sorted(s.num for s in held[1])
                    runs = [n for n in nums if n - 1 not in nums]
                    for lo in runs:
                        hi = next(n for n in range(lo, 257) if n not in nums)
                        pool.sem_clear(range(lo, hi))
            held[0].close()
            held[:] = [ExitStack(), []]

        def scratch_dram(name, shape, dt=F32):
            return nc.dram_tensor(name, shape, dt, kind="Internal").ap()

        def psum(st, name, shape, dt=F32):
            return st.enter_context(nc.psum_tensor(name, shape, dt))

        def sbuf(st, name, shape, dt=F32):
            return st.enter_context(nc.sbuf_tensor(name, shape, dt))

        x = sbuf(top, "x_res", [P, NT, D])
        ident = sbuf(top, "ident", [P, P])
        powers = sbuf(top, "powers", [P, 2])
        x_rows = a["x"].rearrange("b (c p) d -> p (b c) d", p=P)
        eo_d = scratch_dram("eo_d", [NE * CAP, D])
        ctx_rows = a["ctx_2048"].rearrange("b (c p) d -> p (b c) d", p=P)

        with ExitStack() as st:
            tern = {n: sbuf(st, f"tern_{n}", [P, KF * D], BF16) for n in ("w1", "w3", "w2")}
            w_mean = sbuf(st, "w_mean", [P, 3])
            raw = sbuf(st, "raw", [P, KF * D])
            with ExitStack() as sr:
                retention(nc, sr, sem, sbuf, psum, a, x, x_rows, ctx_rows, ident, powers, tern, w_mean, raw, upto)
            if upto >= 2:
                bit_ffn(nc, st, sem, sbuf, psum, eo_d, x, ident, powers, tern, w_mean)
        clear_semaphores()
        if upto >= 3:
            with ExitStack() as st:
                mlstm(nc, st, sem, sbuf, psum, scratch_dram, a, x, ctx_rows, ident, powers, upto)
        if upto >= 4:
            with ExitStack() as st:
                experts(nc, st, sem, sbuf, psum, scratch_dram, eo_d, a, x, ident, powers, out)
        else:
            dumped = sem("dumped")
            with nc.Block() as block:
                @block.sync
                def _(sp):
                    sp.dma_start(out.rearrange("b (c p) d -> p (b c) d", p=P), x[:]).then_inc(dumped, 16)
                    sp.wait_ge(dumped, 16)
        held[0].close()


class Norm:

    def __init__(self, nc, st, sem, sbuf, name, lanes):
        self.nc = nc
        self.st6 = sbuf(st, f"{name}_st6", [P, lanes, 6])
        self.mv = sbuf(st, f"{name}_mv", [P, lanes, 2])
        self.ve = sbuf(st, f"{name}_ve", [P, lanes])
        self.rstd = sbuf(st, f"{name}_rstd", [P, lanes])
        self.var_ready = sem(f"{name}_var_ready")
        self.rstd_ready = sem(f"{name}_rstd_ready")

    def stats(self, steps, sources, eps):
        for c, src in enumerate(sources):
            steps.did(self.nc.vector.bn_stats(self.st6[:, c, :], src))
        steps.settle()
        self.nc.vector.tensor_copy(self.ve[:, 0:1], self.st6[:, 0, 0:1])
        for c in range(len(sources)):
            steps.did(self.nc.vector.bn_aggr(self.mv[:, c, :], self.st6[:, c, :]))
        steps.settle()
        self.nc.vector.tensor_scalar(self.ve[:, 0:len(sources)], self.mv[:, 0:len(sources), 1], eps, None,
                                     ALU.add).then_inc(self.var_ready, 1)

    def power(self, pool, powers, n, lanes):
        pool.wait_ge(self.var_ready, n)
        self.nc.gpsimd.tensor_tensor(self.rstd[:, 0:lanes], self.ve[:, 0:lanes],
                                     powers[:, 0:1].to_broadcast([P, lanes]), ALU.pow).then_inc(self.rstd_ready, 1)


def retention(nc, st, sem, sbuf, psum, a, x, x_rows, ctx_rows, ident, powers, tern, w_mean, raw, upto):
    vt = sbuf(st, "v_rows", [P, NT, D])
    wt = sbuf(st, "gate_t", [P, KD, T])
    at = sbuf(st, "a_t", [P, H0 * (S + P)])
    ones = sbuf(st, "ones", [P, P])
    rsum = sbuf(st, "rsum", [P, 3])
    wrec = sbuf(st, "wrec", [P, 3])

    raw_in = sem("raw_in")
    abs_done = sem("abs_done")
    pool_step = sem("r_pool_step")
    names = ("w1", "w3", "w2")
    ROUND_STEPS = 6

    def load_raw(eng, j):
        src = a[f"L0_ffn_{names[j]}"].rearrange("(j p) d -> p j d", p=P)
        eng.dma_start(raw[:].rearrange("p (j d) -> p j d", j=src.shape[1]), src).then_inc(raw_in, 16)

    def abs_sum(act, j):
        act.wait_ge(raw_in, 16 * (j + 1))
        nc.scalar.activation(tern[names[j]][:], raw[:], ACT.Abs, accum_out=rsum[:, j:j + 1]).then_inc(abs_done, 1)

    def ternary(pool, steps, j):
        pool.wait_ge(abs_done, j + 1)
        m = w_mean[:, j:j + 1]
        steps.then(nc.gpsimd.partition_all_reduce(m, rsum[:, j:j + 1], P, bass.bass_isa.ReduceOp.add))
        steps.then(nc.gpsimd.tensor_scalar(m, m, 1.0 / (F0 * D), Q_EPS, ALU.mult, ALU.max))
        steps.then(nc.gpsimd.tensor_tensor(wrec[:, j:j + 1], m, powers[:, 1:2], ALU.pow))
        steps.then(nc.gpsimd.tensor_scalar(raw[:], raw[:], wrec[:, j:j + 1], ROUND, ALU.mult, ALU.add))
        steps.then(nc.gpsimd.tensor_scalar(raw[:], raw[:], ROUND, 1.0, ALU.subtract, ALU.min))
        steps.then(nc.gpsimd.tensor_scalar(tern[names[j]][:], raw[:], -1.0, None, ALU.max))

    with ExitStack() as sa:
        acc = psum(sa, "acc", [P, 3, 512])
        ring = [psum(sa, f"ring{i}", [P, 512]) for i in range(5)]
        decay = sbuf(sa, "decay", [P, H0 * (S + P)])
        wh = sbuf(sa, "wh", [P, H0, HD])
        wht = sbuf(sa, "wht", [P, H0, HD])
        gram = sbuf(sa, "gram", [P, H0, HD])
        wg = sbuf(sa, "wg", [P, KD, D])
        cx = sbuf(sa, "ctx_in", [P, 2, CB, D])
        xn = sbuf(sa, "xn", [P, CB, D])
        xt = sbuf(sa, "xt", [P, KD, S])
        ct = sbuf(sa, "ct", [P, KD, S])
        qt = sbuf(sa, "qt", [P, H0, S])
        zeros = sbuf(sa, "zeros", [P, 512], BF16)
        norm = Norm(nc, sa, sem, sbuf, "ln0", CB)
        x_in = [sem(f"x_in{i}") for i in range(2)]
        c_in = [sem(f"ctx_in{i}") for i in range(2)]
        ident_in, wh_in, wg_in, decay_in = (sem(n) for n in ("ident_in", "wh_in", "wg_in", "decay_in"))
        fill_done, dve_step = sem("fill_done"), sem("r_dve_step")
        setup_ps, setup_sb = sem("setup_ps"), sem("setup_sb")
        xn_ready, xt_ps, ct_ps, xt_sb, ct_sb = (sem(n) for n in ("xn_ready", "xt_ps", "ct_ps", "xt_sb", "ct_sb"))
        q_ps, v_ps, w_ps, q_sb, v_sb, w_sb = (sem(n) for n in ("q_ps", "v_ps", "w_ps", "q_sb", "v_sb", "w_sb"))
        scored, a_ready, ctx_used = sem("scored"), sem("a_ready"), sem("ctx_used")
        block = sa.enter_context(nc.Block())

        @block.sync
        def _(sp):
            sp.dma_start(x[:, 0:CB, :], x_rows[:, 0:CB, :]).then_inc(x_in[0], 16)
            sp.dma_start(ident[:], a["consts"][:, C_ID:C_ID + P]).then_inc(ident_in, 16)
            sp.dma_start(wh[:], a["L0_xattn_Wh"].rearrange("h d e -> d h e")).then_inc(wh_in, 16)
            sp.dma_start(cx[:, 0], ctx_rows[:, 0:CB, :]).then_inc(c_in[0], 16)
            sp.dma_start(wg[:], a["L0_xattn_wg_w"].rearrange("(k p) n -> p k n", p=P)).then_inc(wg_in, 16)
            sp.dma_start(x[:, CB:2 * CB, :], x_rows[:, CB:2 * CB, :]).then_inc(x_in[1], 16)
            sp.dma_start(cx[:, 1], ctx_rows[:, CB:2 * CB, :]).then_inc(c_in[1], 16)
            load_raw(sp, 0)
            with sp.Fori(0, B // 2 - 1) as i:
                for u in range(2):
                    at_b = 2 * CB * i + CB * (2 + u)
                    sp.wait_ge(x_in[u], 16 * i + 16)
                    sp.dma_start(x[:, ds(at_b, CB), :], x_rows[:, ds(at_b, CB), :]).then_inc(x_in[u], 16)
                    sp.wait_ge(ct_ps, 4 * i + 2 * u + 2)
                    sp.dma_start(cx[:, u], ctx_rows[:, ds(at_b, CB), :]).then_inc(c_in[u], 16)
            sp.dma_start(decay[:], a["consts"][:, C_DEC:C_DEC + H0 * (S + P)]).then_inc(decay_in, 16)

        @block.gpsimd
        def _(pool):
            steps = Steps(pool, pool_step)
            nc.gpsimd.memset(zeros[:], 0.0).then_inc(fill_done, 1)
            nc.gpsimd.memset(powers[:, 0:1], -0.5).then_inc(fill_done, 1)
            nc.gpsimd.memset(powers[:, 1:2], -1.0).then_inc(fill_done, 1)
            nc.gpsimd.memset(ones[:], 1.0).then_inc(fill_done, 1)
            pool.wait_ge(fill_done, 4)
            norm.power(pool, powers, 1, CB)
            with pool.Fori(0, B - 1) as b:
                norm.power(pool, powers, b + 2, CB)
            ternary(pool, steps, 0)

        @block.vector
        def _(dve):
            steps = Steps(dve, dve_step)

            def normalise(b, i, u):
                dve.wait_ge(x_in[u], 16 * i + 16)
                norm.stats(steps, [x[:, CB * b + c, :] if isinstance(b, int) else x[:, ds(CB * b + c, 1), :]
                                   for c in range(CB)], LN_EPS)
                dve.wait_ge(norm.rstd_ready, b + 1)
                for c in range(CB):
                    nc.vector.tensor_scalar(xn[:, c, :], x[:, ds(CB * b + c, 1), :], norm.mv[:, c, 0:1],
                                            norm.rstd[:, c:c + 1], ALU.subtract, ALU.mult).then_inc(xn_ready, 1)

            def copies(b, src_sem, counts, ring_at, dst, done):
                for c in range(CB):
                    dve.wait_ge(src_sem, 2 * b + c + 1)
                    nc.vector.tensor_copy(dst(c), ring[ring_at[c]][:].rearrange("p (k n) -> p k n", n=P)).then_inc(done, 1)

            def batch(b, nxt):
                copies(b, ct_ps, None, (1, 3), lambda c: ct[:, :, c * P:(c + 1) * P], ct_sb)
                if nxt is not None:
                    normalise(b + 1, *nxt)
                for c in range(CB):
                    dve.wait_ge(v_ps, 2 * b + c + 1)
                    nc.vector.tensor_copy(vt[:, ds(CB * b + c, 1), :], ring[1 + c][:]).then_inc(v_sb, 1)

            dve.wait_ge(setup_ps, 1)
            nc.vector.tensor_copy(wht[:], ring[0][:].rearrange("p (h n) -> p h n", n=P)).then_inc(setup_sb, 1)
            dve.wait_ge(setup_ps, 2)
            nc.vector.tensor_copy(gram[:], ring[1][:].rearrange("p (h n) -> p h n", n=P)).then_inc(setup_sb, 1)
            normalise(0, 0, 0)
            with steps.loop(0, B // 2 - 1, 8) as i:
                batch(2 * i, (i, 1))
                batch(2 * i + 1, (i + 1, 0))
            batch(B - 2, (B // 2 - 1, 1))
            batch(B - 1, None)
            dve.wait_ge(scored, B)
            dve.wait_ge(decay_in, 16)
            flat = acc[:].rearrange("p n d -> p (n d)")
            steps.then(nc.vector.tensor_tensor(at[:], flat, decay[:], ALU.mult))
            steps.then(nc.vector.scalar_tensor_tensor(at[:], at[:], -1.0, at[:], ALU.mult, ALU.max))
            nc.vector.tensor_scalar(at[:], at[:], 1.0, None, ALU.max).then_inc(a_ready, 1)

        @block.scalar
        def _(act):
            def batch(b):
                for c in range(CB):
                    act.wait_ge(xt_ps, 2 * b + c + 1)
                    nc.scalar.copy(xt[:, :, c * P:(c + 1) * P],
                                   ring[2 * c][:].rearrange("p (k n) -> p k n", n=P)).then_inc(xt_sb, 1)
                for c in range(CB):
                    act.wait_ge(q_ps, 2 * b + c + 1)
                    nc.scalar.copy(qt[:, :, c * P:(c + 1) * P],
                                   ring[(4, 0)[c]][:].rearrange("p (k n) -> p k n", n=P)).then_inc(q_sb, 1)
                for c in range(2):
                    act.wait_ge(w_ps, 2 * b + c + 1)
                    nc.scalar.activation(wt[:, 2 * c:2 * c + 2, ds(S * b, S)],
                                         ring[3 + c][:].rearrange("p (k n) -> p k n", n=S), ACT.Relu).then_inc(w_sb, 1)

            with act.Fori(0, B - 1) as b:
                batch(b)
            abs_sum(act, 0)
            batch(B - 1)

        @block.tensor
        def _(pe):
            pe.wait_ge(ident_in, 16)
            pe.wait_ge(wh_in, 16)
            pe.wait_ge(fill_done, 4)
            for h in range(H0):
                last = nc.tensor.transpose(ring[0][:, h * P:(h + 1) * P], wh[:, h, :], ident[:])
            last.then_inc(setup_ps, 1)
            for n in range(3):
                nc.tensor.matmul(acc[:, n, :], zeros[:, 0:P], zeros[:], start=True, stop=False, skip_group_check=True)
            pe.wait_ge(setup_sb, 1)
            for h in range(H0):
                last = nc.tensor.matmul(ring[1][:, h * P:(h + 1) * P], wht[:, h, :], wht[:, h, :], start=True, stop=True)
            last.then_inc(setup_ps, 1)
            pe.wait_ge(setup_sb, 2)
            pe.wait_ge(wg_in, 16)

            def turn(dst, src, done):
                for k in range(KD):
                    last = nc.tensor.transpose(dst[:, k * P:(k + 1) * P], src[:, k * P:(k + 1) * P], ident[:])
                last.then_inc(done, 1)

            def batch(b, i, u, first=False):
                for c in range(CB):
                    pe.wait_ge(xn_ready, 2 * b + c + 1)
                    if not first:
                        pe.wait_ge(*((q_sb, 2 * b), (v_sb, 2 * b))[c])
                    turn(ring[2 * c], xn[:, c, :], xt_ps)
                    if c == 0:
                        pe.wait_ge(c_in[u], 16 * i + 16)
                    if not first:
                        pe.wait_ge(*((v_sb, 2 * b - 1), (w_sb, 2 * b - 1))[c])
                    turn(ring[2 * c + 1], cx[:, u, c, :], ct_ps)
                for c in range(CB):
                    pe.wait_ge(xt_sb, 2 * b + c + 1)
                    if c == 0 and not first:
                        pe.wait_ge(w_sb, 2 * b)
                    for h in range(H0):
                        last = nc.tensor.matmul(ring[(4, 0)[c]][:, h * P:(h + 1) * P], gram[:, h, :],
                                                xt[:, h, c * P:(c + 1) * P], start=True, stop=True)
                    last.then_inc(q_ps, 1)
                for c in range(CB):
                    pe.wait_ge(ct_sb, 2 * b + c + 1)
                    for h in range(H0):
                        last = nc.tensor.matmul(ring[1 + c][:, h * P:(h + 1) * P], ct[:, h, c * P:(c + 1) * P],
                                                wh[:, h, :], start=True, stop=True)
                    last.then_inc(v_ps, 1)
                for n in range(2):
                    if n == 1:
                        pe.wait_ge(q_sb, 2 * b + 1)
                    for j in range(2):
                        m = 2 * n + j
                        for k in range(KD):
                            last = nc.tensor.matmul(ring[3 + n][:, j * S:(j + 1) * S], wg[:, k, m * P:(m + 1) * P],
                                                    xt[:, k, :], start=k == 0, stop=k == KD - 1)
                    last.then_inc(w_ps, 1)
                pe.wait_ge(q_sb, 2 * b + 2)
                for h in range(H0):
                    nc.tensor.matmul(acc[:, h // 2, (h % 2) * S:(h % 2 + 1) * S], ct[:, h, 0:P], qt[:, h, :],
                                     start=False, stop=False, skip_group_check=True)
                    last = nc.tensor.matmul(acc[:, 2, h * P:(h + 1) * P], ct[:, h, P:S], qt[:, h, P:S],
                                            start=False, stop=False, skip_group_check=True)
                last.then_inc(scored, 1)

            batch(0, 0, 0, first=True)
            batch(1, 0, 1)
            with pe.Fori(1, B // 2) as i:
                batch(2 * i, i, 0)
                batch(2 * i + 1, i, 1)

    with ExitStack() as sb_:
        wo = sbuf(sb_, "wo", [P, KD, D])
        gam = sbuf(sb_, "gn_gamma", [P, KD])
        bet = sbuf(sb_, "gn_beta", [P, KD])
        y = sbuf(sb_, "gn_y", [P, CB, D])
        zt = sbuf(sb_, "z_t", [P, CB, D])
        o_bank = [psum(sb_, f"o_bank{c}", [P, D]) for c in range(CB)]
        y_bank = [psum(sb_, f"y_bank{c}", [P, D]) for c in range(CB)]
        p_bank = [psum(sb_, f"p_bank{c}", [P, D]) for c in range(CB)]
        norm = Norm(nc, sb_, sem, sbuf, "gn", CB)
        wo_in, dve_step = sem("wo_in"), sem("gn_dve_step")
        o_ps, y_ready, y_ps, y_scaled, z_ready, p_ps, x_added = (
            sem(n) for n in ("o_ps", "y_ready", "y_ps", "y_scaled", "z_ready", "p_ps", "x_added"))
        block = sb_.enter_context(nc.Block())

        @block.sync
        def _(sp):
            sp.dma_start(wo[:], a["L0_xattn_wo_w"].rearrange("(k p) n -> p k n", p=P)).then_inc(wo_in, 16)
            sp.dma_start(gam[:], a["L0_xattn_gn_gamma"].rearrange("(k p) -> p k", p=P),
                         allow_slow_non_contiguous=True).then_inc(wo_in, 16)
            sp.dma_start(bet[:], a["L0_xattn_gn_beta"].rearrange("(k p) -> p k", p=P),
                         allow_slow_non_contiguous=True).then_inc(wo_in, 16)
            load_raw(sp, 1)
            sp.wait_ge(pool_step, 2 * ROUND_STEPS)
            load_raw(sp, 2)

        @block.gpsimd
        def _(pool):
            steps = Steps(pool, pool_step)
            steps.n = ROUND_STEPS
            norm.power(pool, powers, 1, CB)
            norm.power(pool, powers, 2, CB)
            ternary(pool, steps, 1)
            with pool.Fori(2, B) as b:
                norm.power(pool, powers, b + 1, CB)
            ternary(pool, steps, 2)

        def pv(b):
            for c in range(CB):
                for h in range(H0):
                    col = c * P
                    nc.tensor.matmul(o_bank[c][:, h * P:(h + 1) * P], at[:, h * S + col:h * S + col + P],
                                     vt[:, ds(CB * b, 1), h * P:(h + 1) * P], start=True, stop=False)
                    second = ones[:] if c == 0 else at[:, H0 * S + h * P:H0 * S + (h + 1) * P]
                    last = nc.tensor.matmul(o_bank[c][:, h * P:(h + 1) * P], second,
                                            vt[:, ds(CB * b + 1, 1), h * P:(h + 1) * P], start=False, stop=True)
                last.then_inc(o_ps, 1)

        @block.tensor
        def _(pe):
            def batch(b, first=False, final=False):
                for c in range(CB):
                    pe.wait_ge(y_ready, 2 * b + c + 1)
                    if not first:
                        pe.wait_ge(y_scaled, 2 * b + c - 1)
                    for k in range(KD):
                        last = nc.tensor.transpose(y_bank[c][:, k * P:(k + 1) * P], y[:, c, k * P:(k + 1) * P], ident[:])
                    last.then_inc(y_ps, 1)
                if not final:
                    pv(b + 1)
                for c in range(CB):
                    pe.wait_ge(z_ready, 2 * b + c + 1)
                    if not first:
                        pe.wait_ge(x_added, 2 * b + c - 1)
                    for k in range(KD):
                        last = nc.tensor.matmul(p_bank[c][:], zt[:, c, k * P:(k + 1) * P], wo[:, k, :],
                                                start=k == 0, stop=k == KD - 1)
                    last.then_inc(p_ps, 1)

            pv(0)
            pe.wait_ge(wo_in, 48)
            batch(0, first=True)
            with pe.Fori(1, B - 1) as b:
                batch(b)
            batch(B - 1, final=True)

        @block.scalar
        def _(act):
            def batch(b):
                for c in range(CB):
                    act.wait_ge(y_ps, 2 * b + c + 1)
                    for k in range(KD):
                        last = nc.scalar.activation(zt[:, c, k * P:(k + 1) * P], y_bank[c][:, k * P:(k + 1) * P],
                                                    ACT.Identity, bias=bet[:, k:k + 1], scale=gam[:, k:k + 1])
                    last.then_inc(y_scaled, 1)

            act.wait_ge(wo_in, 48)
            batch(0)
            abs_sum(act, 1)
            with act.Fori(1, B) as b:
                act.wait_ge(p_ps, 2 * b)
                batch(b)
            abs_sum(act, 2)

        @block.vector
        def _(dve):
            steps = Steps(dve, dve_step)

            def normalise(b):
                dve.wait_ge(o_ps, 2 * b + CB)
                norm.stats(steps, [o_bank[c][:] for c in range(CB)], GN_EPS)
                dve.wait_ge(norm.rstd_ready, b + 1)
                for c in range(CB):
                    nc.vector.tensor_scalar(y[:, c, :], o_bank[c][:], norm.mv[:, c, 0:1], norm.rstd[:, c:c + 1],
                                            ALU.subtract, ALU.mult).then_inc(y_ready, 1)

            def gate(b):
                for c in range(CB):
                    dve.wait_ge(y_scaled, 2 * b + c + 1)
                    z = zt[:, c, :].rearrange("p (k n) -> p k n", n=P)
                    nc.vector.tensor_tensor(z, z, wt[:, :, ds(S * b + c * P, P)], ALU.mult).then_inc(z_ready, 1)

            def residual(b):
                for c in range(CB):
                    dve.wait_ge(p_ps, 2 * b + c + 1)
                    nc.vector.tensor_tensor(x[:, ds(CB * b + c, 1), :], x[:, ds(CB * b + c, 1), :], p_bank[c][:],
                                            ALU.add).then_inc(x_added, 1)

            normalise(0)
            with steps.loop(0, B - 1, 4) as b:
                gate(b)
                normalise(b + 1)
                residual(b)
            gate(B - 1)
            residual(B - 1)


def bit_ffn(nc, st, sem, sbuf, psum, eo_d, x, ident, powers, tern, w_mean):
    w1t = sbuf(st, "w1t", [P, KD, F0], BF16)
    w3t = sbuf(st, "w3t", [P, KD, F0], BF16)
    w2t = sbuf(st, "w2t", [P, KF, D], BF16)
    identb = sbuf(st, "identb", [P, P], BF16)
    xn = sbuf(st, "f_xn", [P, D])
    big = sbuf(st, "f_big", [P, 1])
    deq = sbuf(st, "f_deq", [P, 2])
    scl = sbuf(st, "f_scl", [P, 1])
    d13 = sbuf(st, "f_d13", [P, 2, 2])
    xq = sbuf(st, "f_xq", [P, D], BF16)
    xqt = sbuf(st, "f_xqt", [P, KD, P], BF16)
    sil = sbuf(st, "f_silu", [P, F0])
    hid = sbuf(st, "f_hid", [P, F0])
    hq = sbuf(st, "f_hq", [P, F0], BF16)
    hqt = sbuf(st, "f_hqt", [P, KF, P], BF16)
    hbig = sbuf(st, "f_hbig", [P, 1])
    hscl = sbuf(st, "f_hscl", [P, 1])
    hdeq = sbuf(st, "f_hdeq", [P, 2])
    hd2 = sbuf(st, "f_hd2", [P, 2])
    g_bank = psum(st, "g_bank", [P, 3, 512])
    u_bank = psum(st, "u_bank", [P, 3, 512])
    ta = psum(st, "turn_a", [P, 512])
    tb = psum(st, "turn_b", [P, 512])
    tab, tbb = (t[:].bitcast(BF16).rearrange("p (k n) -> p k n", n=P) for t in (ta, tb))
    KA = 8
    norm = Norm(nc, st, sem, sbuf, "ln1", 1)
    dve_step, act_step = sem("f_dve_step"), sem("f_act_step")
    idb_ready = sem("f_identb")
    wt_ps = sem("f_wt_ps")
    wt_sb = [sem("f_wt_sb_even"), sem("f_wt_sb_odd")]
    xq_ready, xqt_ps, xqt_sb, g_ps, u_ps, sil_ready, u_used, hq_ready, hta_ps, htb_ps, hta_sb, htb_sb, o_ps, x_added = (
        sem("f_" + n) for n in ("xq_ready", "xqt_ps", "xqt_sb", "g_ps", "u_ps", "sil_ready", "u_used", "hq_ready",
                                "hta_ps", "htb_ps", "hta_sb", "htb_sb", "o_ps", "x_added"))
    jobs = []
    for src, dst in (("w1", w1t), ("w3", w3t)):
        for k in range(KD):
            for j0 in range(0, KF, KA):
                n = min(KA, KF - j0)
                jobs.append(([tern[src][:, (j0 + j) * D + k * P:(j0 + j) * D + (k + 1) * P] for j in range(n)],
                             dst[:, k, j0 * P:(j0 + n) * P].rearrange("p (j n) -> p j n", n=P)))
    for f0 in range(0, KF, 2):
        n = min(2, KF - f0)
        jobs.append(([tern["w2"][:, m * F0 + (f0 + j) * P:m * F0 + (f0 + j + 1) * P] for j in range(n) for m in range(KD)],
                     w2t[:, f0:f0 + n, :].rearrange("p f (m n) -> p (f m) n", n=P)))
    zero_row = sbuf(st, "f_zero_row", [P, D])
    zero_ready, zeroed = sem("f_zero_ready"), sem("f_zeroed")
    FILLS = 8
    block = st.enter_context(nc.Block())

    @block.sync
    def _(sp):
        sp.wait_ge(zero_ready, 1)
        per = NE * CAP // FILLS
        for n in range(FILLS):
            sp.dma_start(eo_d[n * per:(n + 1) * per, :].rearrange("(p q) d -> p q d", p=P),
                         zero_row[:].unsqueeze(1).to_broadcast([P, per // P, D])).then_inc(zeroed, 16)
        sp.wait_ge(zeroed, 16 * FILLS)

    @block.gpsimd
    def _(pool):
        nc.gpsimd.memset(zero_row[:], 0.0).then_inc(zero_ready, 1)
        norm.power(pool, powers, 1, 1)
        with pool.Fori(1, NT) as t:
            norm.power(pool, powers, t + 1, 1)

    @block.tensor
    def _(pe):
        pe.wait_ge(idb_ready, 1)
        for n, (pieces, _) in enumerate(jobs):
            if n >= 2:
                pe.wait_ge(wt_sb[n % 2], n // 2)
            for j, piece in enumerate(pieces):
                last = nc.tensor.transpose((tab, tbb)[n % 2][:, j, :], piece, identb[:])
            last.then_inc(wt_ps, 1)
        for e in range(2):
            pe.wait_ge(wt_sb[e], (len(jobs) + 1 - e) // 2)

        def turn_x(t):
            pe.wait_ge(xq_ready, t + 1)
            for k in range(KD):
                last = nc.tensor.transpose(tbb[:, k, :], xq[:, k * P:(k + 1) * P], identb[:])
            last.then_inc(xqt_ps, 1)

        def up(t, first=False):
            pe.wait_ge(xqt_sb, t + 1)
            for bank, wgt, done, freed in ((g_bank, w1t, g_ps, sil_ready), (u_bank, w3t, u_ps, u_used)):
                if not first:
                    pe.wait_ge(freed, t)
                for n in range(3):
                    lo, hi = 512 * n, min(512 * n + 512, F0)
                    for k in range(KD):
                        last = nc.tensor.matmul(bank[:, n, 0:hi - lo], xqt[:, k, :], wgt[:, k, lo:hi],
                                                start=k == 0, stop=k == KD - 1)
                last.then_inc(done, 1)

        def down(t):
            pe.wait_ge(hq_ready, t + 1)
            for k in range(KF):
                last = nc.tensor.transpose(tab[:, k, :] if k < KA else tbb[:, k - KA, :], hq[:, k * P:(k + 1) * P], identb[:])
                if k == KA - 1:
                    last.then_inc(hta_ps, 1)
            last.then_inc(htb_ps, 1)
            pe.wait_ge(hta_sb, t + 1)
            pe.wait_ge(htb_sb, t + 1)
            for k in range(KF):
                last = nc.tensor.matmul(ta[:], hqt[:, k, :], w2t[:, k, :], start=k == 0, stop=k == KF - 1)
            last.then_inc(o_ps, 1)

        turn_x(0)
        up(0, first=True)
        turn_x(1)
        up(1)
        down(0)
        turn_x(2)
        with pe.Fori(2, NT - 1) as t:
            up(t)
            pe.wait_ge(x_added, t - 1)
            down(t - 1)
            turn_x(t + 1)
        up(NT - 1)
        for t in (NT - 2, NT - 1):
            pe.wait_ge(x_added, t)
            down(t)

    @block.scalar
    def _(act):
        for n, (pieces, dst) in enumerate(jobs):
            if n % 2:
                act.wait_ge(wt_ps, n + 1)
                nc.scalar.copy(dst, (tab, tbb)[n % 2][:, 0:len(pieces), :]).then_inc(wt_sb[n % 2], 1)

        def copy_x(t):
            act.wait_ge(xqt_ps, t + 1)
            nc.scalar.copy(xqt[:], tbb[:, 0:KD, :]).then_inc(xqt_sb, 1)

        def silu(t, d):
            act.wait_ge(g_ps, t + 1)
            if not isinstance(t, int) or t:
                act.wait_ge(u_used, t)
            nc.scalar.activation(sil[:], g_bank[:].rearrange("p n f -> p (n f)")[:, 0:F0], ACT.Silu,
                                 scale=d).then_inc(sil_ready, 1)

        def copy_h(t):
            act.wait_ge(hta_ps, t + 1)
            nc.scalar.copy(hqt[:, 0:KA, :], tab[:, 0:KA, :]).then_inc(hta_sb, 1)
            act.wait_ge(htb_ps, t + 1)
            nc.scalar.copy(hqt[:, KA:KF, :], tbb[:, 0:KF - KA, :]).then_inc(htb_sb, 1)

        copy_x(0)
        silu(0, d13[:, 0, 0:1])
        copy_x(1)
        with act.Fori(0, NT // 2 - 1) as i:
            for u in range(2):
                t = 2 * i + 1 + u
                silu(t, d13[:, (1 + u) % 2, 0:1])
                copy_h(t - 1)
                copy_x(t + 1)
        silu(NT - 1, d13[:, (NT - 1) % 2, 0:1])
        copy_h(NT - 2)
        copy_h(NT - 1)

    @block.vector
    def _(dve):
        steps = Steps(dve, dve_step)
        nc.vector.tensor_copy(identb[:], ident[:]).then_inc(idb_ready, 1)
        for n, (pieces, dst) in enumerate(jobs):
            if n % 2 == 0:
                dve.wait_ge(wt_ps, n + 1)
                nc.vector.tensor_copy(dst, (tab, tbb)[n % 2][:, 0:len(pieces), :]).then_inc(wt_sb[n % 2], 1)

        def quantise(src, bigs, scale, step, products, dst, done):
            steps.then(nc.vector.tensor_reduce(bigs[:], src[:], AX.X, ALU.max, apply_absolute_value=True))
            steps.then(nc.vector.tensor_scalar(bigs[:], bigs[:], Q_EPS, None, ALU.max))
            steps.did(nc.vector.tensor_scalar(step, bigs[:], 1.0 / 127.0, None, ALU.mult))
            steps.then(nc.vector.reciprocal(scale[:], bigs[:]))
            steps.did(nc.vector.tensor_scalar(scale[:], scale[:], 127.0, None, ALU.mult))
            for dst_p, mean in products:
                steps.did(nc.vector.tensor_scalar(dst_p, step, mean, None, ALU.mult))
            steps.settle()
            steps.then(nc.vector.tensor_scalar(src[:], src[:], scale[:], ROUND, ALU.mult, ALU.add))
            nc.vector.tensor_scalar(dst[:], src[:], ROUND, 127.0, ALU.subtract, ALU.min).then_inc(done, 1)

        def prepare(t, par):
            row = x[:, ds(t, 1), :]
            norm.stats(steps, [row], LN_EPS)
            dve.wait_ge(norm.rstd_ready, t + 1)
            steps.then(nc.vector.tensor_scalar(xn[:], row, norm.mv[:, 0, 0:1], norm.rstd[:, 0:1],
                                               ALU.subtract, ALU.mult))
            if not isinstance(t, int) or t:
                dve.wait_ge(xqt_ps, t)
            quantise(xn, big, scl, deq[:, par:par + 1],
                     [(d13[:, par, 0:1], w_mean[:, 0:1]), (d13[:, par, 1:2], w_mean[:, 1:2])], xq, xq_ready)

        def hidden(t, par):
            dve.wait_ge(u_ps, t + 1)
            dve.wait_ge(sil_ready, t + 1)
            if not isinstance(t, int) or t:
                dve.wait_ge(hq_ready, t)
            nc.vector.scalar_tensor_tensor(hid[:], u_bank[:].rearrange("p n f -> p (n f)")[:, 0:F0],
                                           d13[:, par, 1:2], sil[:], ALU.mult, ALU.mult).then_inc(u_used, 1)
            dve.wait_ge(u_used, t + 1)
            if not isinstance(t, int) or t:
                dve.wait_ge(htb_ps, t)
            quantise(hid, hbig, hscl, hdeq[:, par:par + 1], [(hd2[:, par:par + 1], w_mean[:, 2:3])], hq, hq_ready)

        def residual(t, par):
            dve.wait_ge(o_ps, t + 1)
            row = x[:, ds(t, 1), :]
            nc.vector.scalar_tensor_tensor(row, ta[:], hd2[:, par:par + 1], row, ALU.mult, ALU.add).then_inc(x_added, 1)

        prepare(0, 0)
        prepare(1, 1)
        hidden(0, 0)
        with steps.loop(0, NT // 2 - 1, 36) as i:
            for u in range(2):
                t = 2 * i + 1 + u
                prepare(t + 1, u)
                hidden(t, 1 - u)
                residual(t - 1, u)
        hidden(NT - 1, 1)
        residual(NT - 2, 0)
        residual(NT - 1, 1)


def mlstm(nc, st, sem, sbuf, psum, scratch_dram, a, x, ctx_rows, ident, powers, upto):
    BH = B * NH
    W = DH + 1
    gate_d = scratch_dram("gate_d", [2, B, NH, S])
    negm_d = scratch_dram("negm_d", [BH, S])
    qt_d = scratch_dram("qt_d", [B, P, KD * S])
    kt_d = scratch_dram("kt_d", [B, P, KD * S])
    g_t = sbuf(st, "g_t", [P, CB, BH])
    floor_t = sbuf(st, "floor_t", [P, CB, BH])

    with ExitStack() as sa:
        wraw = sbuf(sa, "m_wraw", [P, 3 * KD, 2 * NH])
        bias = sbuf(sa, "m_bias", [2 * NH, 1])
        cx = sbuf(sa, "m_cx", [P, 2, CB, D])
        xn = sbuf(sa, "m_xn", [P, CB, D])
        qt = sbuf(sa, "m_qt", [P, 2, KD, S])
        kt = sbuf(sa, "m_kt", [P, 2, KD, S])
        gts = sbuf(sa, "m_gts", [2 * NH, 2, S])
        ring = [psum(sa, f"m_ring{i}", [P, 512]) for i in range(5)]
        norm = Norm(nc, sa, sem, sbuf, "ln2", CB)
        w_in, w_sum = sem("m_w_in"), sem("m_w_sum")
        c_in = [sem(f"m_c_in{u}") for u in range(2)]
        stored = [sem(f"m_stored{u}") for u in range(2)]
        dve_step, xn_ready, xt_ps, ct_ps, xt_sb, ct_sb, g_ps, g_sb = (
            sem("m_" + n) for n in ("dve_step", "xn_ready", "xt_ps", "ct_ps", "xt_sb", "ct_sb", "g_ps", "g_sb"))
        block = sa.enter_context(nc.Block())

        @block.sync
        def _(sp):
            for u in range(2):
                sp.dma_start(cx[:, u], ctx_rows[:, CB * u:CB * u + CB, :]).then_inc(c_in[u], 16)
            for k, n in enumerate(("Wi", "Wf")):
                sp.dma_start(wraw[:, :, k * NH:(k + 1) * NH],
                             a["L1_xattn_" + n].rearrange("(k p) n -> p k n", p=P)).then_inc(w_in, 16)
            for k, n in enumerate(("bi", "bf")):
                sp.dma_start(bias[k * NH:(k + 1) * NH, :],
                             a["L1_xattn_" + n].rearrange("(p o) -> p o", o=1)).then_inc(w_in, 16)

            def store(b, u):
                sp.wait_ge(xt_sb, 2 * b + 2)
                sp.dma_start(qt_d[ds(b, 1)].rearrange("b p n -> p (b n)"),
                             qt[:, u].rearrange("p k n -> p (k n)")).then_inc(stored[u], 16)
                sp.wait_ge(ct_sb, 2 * b + 2)
                sp.dma_start(kt_d[ds(b, 1)].rearrange("b p n -> p (b n)"),
                             kt[:, u].rearrange("p k n -> p (k n)")).then_inc(stored[u], 16)
                sp.wait_ge(g_sb, b + 1)
                for k in range(2):
                    sp.dma_start(gate_d[k, ds(b, 1)].rearrange("b h s -> (b h) s"),
                                 gts[k * NH:(k + 1) * NH, u, :]).then_inc(stored[u], 16)

            with sp.Fori(0, B // 2 - 1) as i:
                for u in range(2):
                    sp.wait_ge(ct_ps, 4 * i + 2 * u + 2)
                    sp.dma_start(cx[:, u], ctx_rows[:, ds(2 * CB * i + CB * (2 + u), CB), :]).then_inc(c_in[u], 16)
                    store(2 * i + u, u)
            for u in range(2):
                store(B - 2 + u, u)
            for u in range(2):
                sp.wait_ge(stored[u], 64 * (B // 2))

        @block.gpsimd
        def _(pool):
            with pool.Fori(0, B) as b:
                norm.power(pool, powers, b + 1, CB)

        @block.vector
        def _(dve):
            steps = Steps(dve, dve_step)
            dve.wait_ge(w_in, 64)
            nc.vector.tensor_tensor(wraw[:, KD:2 * KD, :], wraw[:, KD:2 * KD, :], wraw[:, 2 * KD:3 * KD, :],
                                    ALU.add).then_inc(w_sum, 1)

            def normalise(b):
                norm.stats(steps, [x[:, ds(CB * b + c, 1), :] for c in range(CB)], LN_EPS)
                dve.wait_ge(norm.rstd_ready, b + 1)
                if not isinstance(b, int) or b:
                    dve.wait_ge(xt_ps, 2 * b)
                for c in range(CB):
                    nc.vector.tensor_scalar(xn[:, c, :], x[:, ds(CB * b + c, 1), :], norm.mv[:, c, 0:1],
                                            norm.rstd[:, c:c + 1], ALU.subtract, ALU.mult).then_inc(xn_ready, 1)

            def copies(b, u, i):
                if not isinstance(i, int) or i:
                    dve.wait_ge(stored[u], 64 * i)
                for c in range(CB):
                    dve.wait_ge(ct_ps, 2 * b + c + 1)
                    nc.vector.tensor_copy(kt[:, u, :, c * P:(c + 1) * P],
                                          ring[2 * c + 1][:].rearrange("p (k n) -> p k n", n=P)).then_inc(ct_sb, 1)

            normalise(0)
            for u in range(2):
                copies(u, u, 0)
                normalise(u + 1)
            with steps.loop(1, B // 2 - 1, 8) as i:
                for u in range(2):
                    copies(2 * i + u, u, i)
                    normalise(2 * i + u + 1)
            copies(B - 2, 0, B // 2 - 1)
            normalise(B - 1)
            copies(B - 1, 1, B // 2 - 1)

        @block.scalar
        def _(act):
            def batch(b, u, i):
                if not isinstance(i, int) or i:
                    act.wait_ge(stored[u], 64 * i)
                for c in range(CB):
                    act.wait_ge(xt_ps, 2 * b + c + 1)
                    nc.scalar.copy(qt[:, u, :, c * P:(c + 1) * P],
                                   ring[2 * c][:].rearrange("p (k n) -> p k n", n=P)).then_inc(xt_sb, 1)
                act.wait_ge(g_ps, b + 1)
                nc.scalar.activation(gts[:, u, :], ring[4][0:2 * NH, 0:S], ACT.Identity, bias=bias[:]).then_inc(g_sb, 1)

            act.wait_ge(w_in, 64)
            for u in range(2):
                batch(u, u, 0)
            with act.Fori(1, B // 2) as i:
                for u in range(2):
                    batch(2 * i + u, u, i)

        @block.tensor
        def _(pe):
            def batch(b, u, i, first=False):
                for c in range(CB):
                    pe.wait_ge(xn_ready, 2 * b + c + 1)
                    if not first:
                        pe.wait_ge(xt_sb, 2 * b + c - 1)
                    for k in range(KD):
                        last = nc.tensor.transpose(ring[2 * c][:, k * P:(k + 1) * P], xn[:, c, k * P:(k + 1) * P], ident[:])
                    last.then_inc(xt_ps, 1)
                    if c == 0:
                        pe.wait_ge(c_in[u], 16 * i + 16)
                    if not first:
                        pe.wait_ge(ct_sb, 2 * b + c - 1)
                    for k in range(KD):
                        last = nc.tensor.transpose(ring[2 * c + 1][:, k * P:(k + 1) * P], cx[:, u, c, k * P:(k + 1) * P], ident[:])
                    last.then_inc(ct_ps, 1)
                pe.wait_ge(xt_sb, 2 * b + 2)
                pe.wait_ge(ct_sb, 2 * b + 2)
                if not first:
                    pe.wait_ge(g_sb, b)
                for k in range(2 * KD):
                    last = nc.tensor.matmul(ring[4][0:2 * NH, 0:S], wraw[:, k, :],
                                            qt[:, u, k, :] if k < KD else kt[:, u, k - KD, :],
                                            start=k == 0, stop=k == 2 * KD - 1)
                last.then_inc(g_ps, 1)

            pe.wait_ge(w_sum, 1)
            batch(0, 0, 0, first=True)
            batch(1, 1, 0)
            with pe.Fori(1, B // 2) as i:
                for u in range(2):
                    batch(2 * i + u, u, i)

    with ExitStack() as sg:
        names = ("ig", "fg", "soft", "cum", "g", "m", "negm", "fl", "zero")
        ig, fg, soft, cum, g, m, negm, fl, zero = (sbuf(sg, "d_" + n, [BH, S]) for n in names)
        tg = psum(sg, "d_tg", [P, 512])
        i_in, soft_ready, fl_in, dve_step, act_step, g_ready, fl_ready, t_ps, t_sb, negm_ready, negm_out = (
            sem("d_" + n) for n in ("i_in", "soft_ready", "fl_in", "dve_step", "act_step", "g_ready", "fl_ready",
                                    "t_ps", "t_sb", "negm_ready", "negm_out"))
        block = sg.enter_context(nc.Block())

        @block.sync
        def _(sp):
            sp.dma_start(fg[:], gate_d[1].rearrange("b h s -> (b h) s")).then_inc(i_in, 16)
            sp.dma_start(ig[:], gate_d[0].rearrange("b h s -> (b h) s")).then_inc(i_in, 16)
            sp.wait_ge(negm_ready, 1)
            sp.dma_start(negm_d, negm[:]).then_inc(negm_out, 16)
            sp.wait_ge(negm_out, 16)

        @block.scalar
        def _(act):
            steps = Steps(act, act_step)
            act.wait_ge(i_in, 32)
            steps.then(nc.scalar.activation(soft[:], fg[:], ACT.Abs))
            steps.then(nc.scalar.activation(soft[:], soft[:], ACT.Exp, scale=-1.0))
            nc.scalar.activation(soft[:], soft[:], ACT.Ln, bias=1.0).then_inc(soft_ready, 1)
            act.wait_ge(fl_in, 1)
            nc.scalar.activation(fl[:], fl[:], ACT.Exp, scale=-1.0).then_inc(fl_ready, 1)

        @block.vector
        def _(dve):
            steps = Steps(dve, dve_step)
            steps.did(nc.vector.memset(zero[:], 0.0))
            dve.wait_ge(soft_ready, 1)
            steps.then(nc.vector.scalar_tensor_tensor(soft[:], fg[:], 0.0, soft[:], ALU.min, ALU.subtract))
            steps.then(nc.vector.tensor_tensor_scan(cum[:], soft[:], zero[:], 0.0, ALU.add, ALU.add))
            nc.vector.tensor_tensor(g[:], ig[:], cum[:], ALU.subtract).then_inc(g_ready, 1)
            dve.wait_ge(g_ready, 1)
            steps.then(nc.vector.tensor_tensor_scan(m[:], g[:], g[:], -3e38, ALU.max, ALU.max))
            nc.vector.tensor_scalar(negm[:], m[:], -1.0, None, ALU.mult).then_inc(negm_ready, 1)
            nc.vector.tensor_tensor(fl[:], cum[:], m[:], ALU.add).then_inc(fl_in, 1)
            dve.wait_ge(t_ps, 2)
            nc.vector.tensor_copy(g_t[:], tg[:, 0:2 * P].rearrange("p (c n) -> p c n", n=P)).then_inc(t_sb, 1)
            nc.vector.tensor_copy(floor_t[:], tg[:, 2 * P:4 * P].rearrange("p (c n) -> p c n", n=P)).then_inc(t_sb, 1)

        @block.tensor
        def _(pe):
            for n, (src, ready) in enumerate(((g, g_ready), (fl, fl_ready))):
                pe.wait_ge(ready, 1)
                for c in range(CB):
                    last = nc.tensor.transpose(tg[:, (2 * n + c) * P:(2 * n + c + 1) * P], src[:, c * P:(c + 1) * P], ident[:])
                last.then_inc(t_ps, 1)

    GR = 2 * NG
    with ExitStack() as sh:
        lns = sbuf(sh, "ln_scale", [P, D])
        future = sbuf(sh, "future", [P, P])
        qt = sbuf(sh, "h_qt", [P, 2, KD, S])
        kt = sbuf(sh, "h_kt", [P, 2, KD, S])
        cx = sbuf(sh, "h_cx", [P, 2, CB, D])
        nm = sbuf(sh, "h_negm", [P, 2, NH, 3, P])
        gst = sbuf(sh, "h_g", [P, 2, CB, NH])
        va = sbuf(sh, "h_v", [P, 2, CB, NH, W])
        dm = sbuf(sh, "h_d", [P, 2, HG, 3, P])
        cm = sbuf(sh, "h_c", [P, 2, HG, 3 * P])
        hr = sbuf(sh, "h_raw", [P, 2, CB, NH, W])
        hb = sbuf(sh, "h_b", [P, CB, NH, DH])
        sq = sbuf(sh, "h_sq", [P, CB, NH, DH])
        nrm = sbuf(sh, "h_nrm", [P, CB, NH])
        mu = sbuf(sh, "h_mu", [P, CB, NH])
        var = sbuf(sh, "h_var", [P, CB, NH])
        rs = sbuf(sh, "h_rs", [P, CB, NH])
        qk = psum(sh, "h_qk", [P, HG, 512])
        pvb = [psum(sh, f"h_pv{i}", [P, CB, HG, W]) for i in range(2)]
        cst_in = sem("h_cst_in")
        ld = [sem(f"h_ld{u}") for u in range(2)]
        (dve_step, staged, masked, d_ready, qk_ps, c_ready, pv_ps, h_sb, h_read, hc_in, hc_ready, sq_ready,
         var_ready, rs_ready, pool_step, x_added) = (
            sem("h_" + n) for n in ("dve_step", "staged", "masked", "d_ready", "qk_ps", "c_ready", "pv_ps",
                                    "h_sb", "h_read", "hc_in", "hc_ready", "sq_ready", "var_ready", "rs_ready",
                                    "pool_step", "x_added"))
        block = sh.enter_context(nc.Block())
        LOADS = 6 * 16
        OPEN_C, OPEN_D, OPEN_PV, OPEN_H, OPEN_R, OPEN_X = 2, 2, 8, 2, 2, 1

        @block.sync
        def _(sp):
            sp.dma_start(lns[:], a["L1_xattn_ln_scale"].rearrange("(o d) -> o d", o=1).partition_broadcast(P)
                         .rearrange("p o d -> p (o d)")).then_inc(cst_in, 16)
            sp.dma_start(future[:], a["consts"][:, C_FUT:C_FUT + P]).then_inc(cst_in, 16)

            def load(b, u):
                for blk, half in ((0, 0), (1, 1), (2, 1)):
                    sp.dma_start(nm[:, u, :, blk, :],
                                 negm_d[ds(b * NH, NH), half * P:(half + 1) * P].rearrange("(o h) s -> o h s", o=1)
                                 .partition_broadcast(P).rearrange("p o h s -> p (o h) s")).then_inc(ld[u], 16)
                sp.dma_start(qt[:, u].rearrange("p k n -> p (k n)"),
                             qt_d[ds(b, 1)].rearrange("b p n -> p (b n)")).then_inc(ld[u], 16)
                sp.dma_start(kt[:, u].rearrange("p k n -> p (k n)"),
                             kt_d[ds(b, 1)].rearrange("b p n -> p (b n)")).then_inc(ld[u], 16)
                sp.dma_start(cx[:, u], ctx_rows[:, ds(CB * b, CB), :]).then_inc(ld[u], 16)

            for u in range(2):
                load(u, u)
            with sp.Fori(0, B // 2 - 1) as i:
                for u in range(2):
                    sp.wait_ge(pv_ps, OPEN_PV + GR * i + NG * (u + 1))
                    load(2 * i + 2 + u, u)

        def group(i, k):
            return GR * i + k, k // NG, k % NG, k % 2

        @block.gpsimd
        def _(pool):
            steps = Steps(pool, pool_step)
            steps.did(nc.gpsimd.memset(va[:], 1.0))
            steps.settle()
            pool.wait_ge(cst_in, 32)

            def stage(i, u):
                b = 2 * i + u
                pool.wait_ge(ld[u], LOADS * i + LOADS)
                pool.wait_ge(pv_ps, OPEN_PV + 4 * (b - 2) + 4)
                nc.gpsimd.tensor_copy(gst[:, u], g_t[:, :, ds(b * NH, NH)]).then_inc(staged, 1)
                nc.gpsimd.tensor_copy(va[:, u, :, :, 0:DH], cx[:, u].rearrange("p c (h e) -> p c h e", e=DH)).then_inc(staged, 1)
                nc.gpsimd.tensor_tensor(nm[:, u, :, 0::2, :], nm[:, u, :, 0::2, :],
                                        future[:].unsqueeze(1).unsqueeze(1).to_broadcast([P, NH, 2, P]),
                                        ALU.add).then_inc(masked, 1)

            def centre(b):
                pool.wait_ge(hc_in, b + 1)
                nc.gpsimd.tensor_tensor(hb[:], hb[:], mu[:].unsqueeze(3).to_broadcast([P, CB, NH, DH]),
                                        ALU.subtract).then_inc(hc_ready, 1)

            def finish(b, u):
                pool.wait_ge(var_ready, b + 1)
                nc.gpsimd.tensor_tensor(rs[:].rearrange("p c h -> p (c h)"), var[:].rearrange("p c h -> p (c h)"),
                                        powers[:, 0:1].to_broadcast([P, CB * NH]), ALU.pow).then_inc(rs_ready, 1)
                pool.wait_ge(rs_ready, b + 1)
                steps.then(nc.gpsimd.tensor_tensor(hb[:], hb[:], rs[:].unsqueeze(3).to_broadcast([P, CB, NH, DH]), ALU.mult))
                flat = hb[:].rearrange("p c h e -> p c (h e)")
                for c in range(CB):
                    steps.did(nc.gpsimd.tensor_tensor(flat[:, c], flat[:, c], lns[:], ALU.mult))
                steps.settle()
                nc.gpsimd.tensor_tensor(x[:, ds(CB * b, CB), :], x[:, ds(CB * b, CB), :], flat, ALU.add).then_inc(x_added, 1)

            pool.sem_inc(x_added, OPEN_X)
            with steps.loop(0, B // 2, 6) as i:
                stage(i, 0)
                stage(i, 1)
                for u in range(2):
                    centre(2 * i + u)
                    finish(2 * i + u, u)

        @block.scalar
        def _(act):
            def decays(i, k):
                n, u, g4, par = group(i, k)
                act.wait_ge(masked, 2 * i + u + 1)
                act.wait_ge(c_ready, OPEN_C + n - 1)
                for j in range(HG):
                    h = HG * g4 + j
                    nc.scalar.activation(dm[:, par, j, 0:2, :], nm[:, u, h, 0:2, :], ACT.Exp, bias=gst[:, u, 0, h:h + 1])
                    last = nc.scalar.activation(dm[:, par, j, 2, :], nm[:, u, h, 2, :], ACT.Exp, bias=gst[:, u, 1, h:h + 1])
                last.then_inc(d_ready, 1)

            def take(i, k):
                n, u, g4, par = group(i, k)
                if g4 == 0:
                    act.wait_ge(h_read, OPEN_R + 2 * i + u - 1)
                act.wait_ge(pv_ps, OPEN_PV + n + 1)
                nc.scalar.copy(hr[:, u, :, HG * g4:HG * (g4 + 1), :], pvb[par][:]).then_inc(h_sb, 1)

            def square(b):
                act.wait_ge(hc_ready, b + 1)
                nc.scalar.activation(sq[:], hb[:], ACT.Square).then_inc(sq_ready, 1)

            act.sem_inc(d_ready, OPEN_D)
            act.sem_inc(h_sb, OPEN_H)
            with act.Fori(0, B // 2) as i:
                for u in range(2):
                    act.wait_ge(ld[u], LOADS * i + LOADS)
                    for k in range(NG * u, NG * u + NG):
                        decays(i, k)
                        if k:
                            take(i, k - 1)
                        if k == NG + 2:
                            square(2 * i)
                take(i, GR - 1)
                square(2 * i + 1)

        @block.tensor
        def _(pe):
            def scores(i, k):
                n, u, g4, par = group(i, k)
                pe.wait_ge(c_ready, OPEN_C + n)
                for j in range(HG):
                    r = slice(DH * j, DH * (j + 1))
                    nc.tensor.matmul(qk[:, j, 0:S], kt[r, u, g4, 0:P], qt[r, u, g4, :], start=True, stop=True)
                    last = nc.tensor.matmul(qk[:, j, S:S + P], kt[r, u, g4, P:S], qt[r, u, g4, P:S], start=True, stop=True)
                last.then_inc(qk_ps, 1)

            def values(i, k):
                n, u, g4, par = group(i, k)
                pe.wait_ge(c_ready, OPEN_C + n + 1)
                pe.wait_ge(staged, 4 * i + 2 * u + 2)
                pe.wait_ge(h_sb, OPEN_H + n - 1)
                for j in range(HG):
                    h = HG * g4 + j
                    c = cm[:, par, j, :]
                    nc.tensor.matmul(pvb[par][:, 0, j, :], c[:, 0:P], va[:, u, 0, h, :], start=True, stop=True)
                    nc.tensor.matmul(pvb[par][:, 1, j, :], c[:, P:2 * P], va[:, u, 0, h, :], start=True, stop=False)
                    last = nc.tensor.matmul(pvb[par][:, 1, j, :], c[:, 2 * P:3 * P], va[:, u, 1, h, :], start=False, stop=True)
                last.then_inc(pv_ps, 1)

            pe.sem_inc(pv_ps, OPEN_PV)
            with pe.Fori(0, B // 2) as i:
                for k in range(GR):
                    if k % NG == 0:
                        pe.wait_ge(ld[k // NG], LOADS * i + LOADS)
                    scores(i, k)
                    if k:
                        values(i, k - 1)
                values(i, GR - 1)

        @block.vector
        def _(dve):
            steps = Steps(dve, dve_step)
            dve.wait_ge(cst_in, 32)

            def weigh(i, k):
                n, u, g4, par = group(i, k)
                dve.wait_ge(d_ready, OPEN_D + n + 1)
                dve.wait_ge(qk_ps, n + 1)
                dve.wait_ge(pv_ps, OPEN_PV + n - 1)
                nc.vector.scalar_tensor_tensor(cm[:, par], qk[:, :, 0:3 * P], float(DH) ** -0.5,
                                               dm[:, par].rearrange("p j c n -> p j (c n)"),
                                               ALU.mult, ALU.mult).then_inc(c_ready, 1)

            def divide(b, u, i):
                dve.wait_ge(h_sb, OPEN_H + GR * i + NG * (u + 1))
                steps.then(nc.vector.scalar_tensor_tensor(nrm[:], hr[:, u, :, :, DH], -1.0, hr[:, u, :, :, DH], ALU.mult, ALU.max))
                steps.then(nc.vector.tensor_tensor(nrm[:], nrm[:], floor_t[:, :, ds(b * NH, NH)], ALU.max))
                steps.then(nc.vector.tensor_scalar(nrm[:], nrm[:], M_EPS, None, ALU.add))
                steps.then(nc.vector.reciprocal(nrm[:], nrm[:]))
                dve.wait_ge(x_added, OPEN_X + b)
                nc.vector.tensor_tensor(hb[:], hr[:, u, :, :, 0:DH], nrm[:].unsqueeze(3).to_broadcast([P, CB, NH, DH]),
                                        ALU.mult).then_inc(h_read, 1)
                dve.wait_ge(h_read, OPEN_R + b + 1)
                steps.then(nc.vector.tensor_reduce(mu[:], hb[:], AX.X, ALU.add))
                nc.vector.tensor_scalar(mu[:], mu[:], 1.0 / DH, None, ALU.mult).then_inc(hc_in, 1)

            def variance(b):
                dve.wait_ge(sq_ready, b + 1)
                steps.then(nc.vector.tensor_reduce(var[:], sq[:], AX.X, ALU.add))
                nc.vector.tensor_scalar(var[:], var[:], 1.0 / DH, M_EPS, ALU.mult, ALU.add).then_inc(var_ready, 1)

            dve.sem_inc(c_ready, OPEN_C)
            dve.sem_inc(h_read, OPEN_R)
            with steps.loop(0, B // 2, 12) as i:
                for k in range(GR):
                    weigh(i, k)
                    if k == NG + 1:
                        divide(2 * i, 0, i)
                    if k == NG + 3:
                        variance(2 * i)
                divide(2 * i + 1, 1, i)
                variance(2 * i + 1)


def experts(nc, st, sem, sbuf, psum, scratch_dram, eo_d, a, x, ident, powers, out):
    r_d = scratch_dram("r_d", [T, D])
    logits = sbuf(st, "logits", [P, NT, NE])
    route = sbuf(st, "route", [P, ROUTES], I32)
    slot = sbuf(st, "slot", [P, NT * TOPK], I32)
    wk = sbuf(st, "wk", [P, NT, TOPK])
    unit_tile = sbuf(st, "unit_tile", [P, ROUTES + 2], I32)
    unit_ends = sbuf(st, "unit_ends", [P, NE], I32)
    rounds = sbuf(st, "rounds", [P, 1], I32)
    carry = sbuf(st, "carry", [P, 2])
    w13 = sbuf(st, "w13", [P, 2, KD, 2 * FI])
    w2 = sbuf(st, "w2", [P, 2, KI, D])
    w13_in = [sem(f"w13_in{u}") for u in range(2)]
    w2_in = [sem(f"w2_in{u}") for u in range(2)]

    def load_w13(eng, e, u):
        eng.dma_start(w13[:, u], a["L1_ffn_w13"][ds(e, 1)].rearrange("e (k p) f -> p (e k) f", p=P)).then_inc(w13_in[u], 16)

    def load_w2(eng, e, u):
        eng.dma_start(w2[:, u], a["L1_ffn_w2"][ds(e, 1)].rearrange("e (k p) f -> p (e k) f", p=P)).then_inc(w2_in[u], 16)

    with ExitStack() as sa:
        nw = sbuf(sa, "norm_w", [P, D])
        gw = sbuf(sa, "gate_w", [NE, D])
        gwt = sbuf(sa, "gate_wt", [P, KD, NE])
        sg = sbuf(sa, "sh_gate", [P, KD, FI])
        su = sbuf(sa, "sh_up", [P, KD, FI])
        sd = sbuf(sa, "sh_down", [P, KI, D])
        xl = sbuf(sa, "e_xl", [P, CB, D])
        sq = sbuf(sa, "e_sq", [P, D])
        ms = sbuf(sa, "e_ms", [P, CB])
        me = sbuf(sa, "e_me", [P, CB])
        rr = sbuf(sa, "e_rr", [P, CB])
        r = sbuf(sa, "e_r", [P, 2, CB, D])
        rt = sbuf(sa, "e_rt", [P, KD, S])
        gsil = sbuf(sa, "e_gsil", [P, KI, S])
        av = sbuf(sa, "e_av", [P, KI, S])
        tbank = [psum(sa, f"e_t{c}", [P, 512]) for c in range(CB)]
        lbank = psum(sa, "e_l", [P, 512])
        gbank = psum(sa, "e_g", [P, KI, S])
        ubank = psum(sa, "e_u", [P, KI, S])
        dbank = [psum(sa, f"e_d{c}", [P, D]) for c in range(CB)]
        norm = Norm(nc, sa, sem, sbuf, "ln3", CB)
        (e_in, w_in, gwt_ps, gwt_sb, dve_step, xl_ready, base_ready, ms_ready, me_ready, rr_ready, r_ready, r_free,
         r_ps, rt_sb, l_ps, l_sb, g_ps, u_ps, sil_ready, av_ready, d_ps, added) = (
            sem("e_" + n) for n in ("in", "w_in", "gwt_ps", "gwt_sb", "dve_step", "xl_ready", "base_ready", "ms_ready",
                                    "me_ready", "rr_ready", "r_ready", "r_free", "r_ps", "rt_sb", "l_ps", "l_sb",
                                    "g_ps", "u_ps", "sil_ready", "av_ready", "d_ps", "added"))
        r_out = [sem(f"e_r_out{u}") for u in range(2)]
        OPEN = 2
        block = sa.enter_context(nc.Block())

        @block.sync
        def _(sp):
            sp.dma_start(nw[:], a["L1_ffn_norm_w"].rearrange("(o d) -> o d", o=1).partition_broadcast(P)
                         .rearrange("p o d -> p (o d)")).then_inc(e_in, 16)
            sp.dma_start(gw[:], a["L1_ffn_gate_w"]).then_inc(e_in, 16)
            sp.dma_start(sg[:], a["L1_ffn_shared_gate_w"].rearrange("(k p) n -> p k n", p=P)).then_inc(w_in, 16)
            sp.dma_start(su[:], a["L1_ffn_shared_up_w"].rearrange("(k p) n -> p k n", p=P)).then_inc(w_in, 16)
            sp.dma_start(sd[:], a["L1_ffn_shared_down_w"].rearrange("(k p) n -> p k n", p=P)).then_inc(w_in, 16)
            for u in range(2):
                load_w13(sp, u, u)
                load_w2(sp, u, u)
            sp.sem_inc(r_free, OPEN)
            with sp.Fori(0, B // 2) as i:
                for u in range(2):
                    b = 2 * i + u
                    sp.wait_ge(r_ready, b + 1)
                    sp.dma_start(r_d[ds(S * b, S), :].rearrange("(c p) d -> p c d", p=P), r[:, u]).then_inc(r_out[u], 16)
                    sp.wait_ge(r_out[u], 16 * i + 16)
                    sp.sem_inc(r_free, 1)

        @block.gpsimd
        def _(pool):
            pool.sem_inc(base_ready, OPEN)
            with pool.Fori(0, B) as b:
                norm.power(pool, powers, b + 1, CB)
                pool.wait_ge(me_ready, b + 1)
                nc.gpsimd.tensor_tensor(rr[:], me[:], powers[:, 0:1].to_broadcast([P, CB]), ALU.pow).then_inc(rr_ready, 1)
                pool.wait_ge(xl_ready, b + 1)
                xb = x[:, ds(CB * b, CB), :]
                nc.gpsimd.tensor_tensor(xb, xb, xl[:], ALU.add).then_inc(base_ready, 1)

        @block.vector
        def _(dve):
            steps = Steps(dve, dve_step)
            dve.sem_inc(av_ready, OPEN)
            dve.wait_ge(gwt_ps, 1)
            nc.vector.tensor_copy(gwt[:], lbank[:, 0:KD * NE].rearrange("p (k n) -> p k n", n=NE)).then_inc(gwt_sb, 1)
            dve.wait_ge(e_in, 32)

            def prepare(b, u):
                norm.stats(steps, [x[:, ds(CB * b + c, 1), :] for c in range(CB)], LN_EPS)
                dve.wait_ge(norm.rstd_ready, b + 1)
                dve.wait_ge(base_ready, OPEN + b)
                for c in range(CB):
                    last = nc.vector.tensor_scalar(xl[:, c, :], x[:, ds(CB * b + c, 1), :], norm.mv[:, c, 0:1],
                                                   norm.rstd[:, c:c + 1], ALU.subtract, ALU.mult)
                last.then_inc(xl_ready, 1)
                dve.wait_ge(ms_ready, CB * b + CB)
                nc.vector.tensor_scalar(me[:], ms[:], 1.0 / D, M_EPS, ALU.mult, ALU.add).then_inc(me_ready, 1)
                dve.wait_ge(rr_ready, b + 1)
                dve.wait_ge(r_free, b + 1)
                dve.wait_ge(r_ps, OPEN + b - 1)
                for c in range(CB):
                    last = nc.vector.scalar_tensor_tensor(r[:, u, c, :], xl[:, c, :], rr[:, c:c + 1], nw[:], ALU.mult, ALU.mult)
                last.then_inc(r_ready, 1)

            def finish(b):
                dve.wait_ge(l_ps, b + 1)
                nc.vector.tensor_copy(logits[:, ds(CB * b, CB), :],
                                      lbank[:, 0:CB * NE].rearrange("p (c n) -> p c n", n=NE)).then_inc(l_sb, 1)
                dve.wait_ge(u_ps, b + 1)
                dve.wait_ge(sil_ready, b + 1)
                dve.wait_ge(d_ps, OPEN + b)
                nc.vector.tensor_tensor(av[:], gsil[:], ubank[:], ALU.mult).then_inc(av_ready, 1)
                dve.wait_ge(d_ps, OPEN + b + 1)
                dve.wait_ge(base_ready, OPEN + b + 1)
                for c in range(CB):
                    xb = x[:, ds(CB * b + c, 1), :]
                    last = nc.vector.tensor_tensor(xb, xb, dbank[c][:], ALU.add)
                last.then_inc(added, 1)

            prepare(0, 0)
            dve.sem_inc(added, 1)
            dve.sem_inc(l_sb, 1)
            with steps.loop(0, B // 2 - 1, 8) as i:
                for u in range(2):
                    prepare(2 * i + u + 1, 1 - u)
                    finish(2 * i + u)
            prepare(B - 1, 1)
            finish(B - 2)
            finish(B - 1)

        @block.scalar
        def _(act):
            def squares(b):
                act.wait_ge(xl_ready, b + 1)
                for c in range(CB):
                    act.wait_ge(ms_ready, CB * b + c) if not (isinstance(b, int) and b == 0 and c == 0) else None
                    nc.scalar.activation(sq[:], xl[:, c, :], ACT.Square, accum_out=ms[:, c:c + 1]).then_inc(ms_ready, 1)

            def silu(b):
                act.wait_ge(r_ps, OPEN + b + 1)
                for c in range(CB):
                    last = nc.scalar.copy(rt[:, :, c * P:(c + 1) * P], tbank[c][:].rearrange("p (k n) -> p k n", n=P))
                last.then_inc(rt_sb, 1)
                act.wait_ge(g_ps, b + 1)
                act.wait_ge(av_ready, OPEN + b)
                nc.scalar.activation(gsil[:], gbank[:], ACT.Silu).then_inc(sil_ready, 1)

            squares(0)
            with act.Fori(0, B - 1) as b:
                squares(b + 1)
                silu(b)
            silu(B - 1)

        @block.tensor
        def _(pe):
            pe.wait_ge(e_in, 32)
            for k in range(KD):
                last = nc.tensor.transpose(lbank[:, k * NE:(k + 1) * NE], gw[:, k * P:(k + 1) * P], ident[0:NE, 0:NE])
            last.then_inc(gwt_ps, 1)
            pe.sem_inc(r_ps, OPEN)
            pe.sem_inc(d_ps, OPEN)
            pe.wait_ge(gwt_sb, 1)
            pe.wait_ge(w_in, 48)

            def batch(b, u):
                pe.wait_ge(r_ready, b + 1)
                for c in range(CB):
                    for k in range(KD):
                        last = nc.tensor.transpose(tbank[c][:, k * P:(k + 1) * P], r[:, u, c, k * P:(k + 1) * P], ident[:])
                last.then_inc(r_ps, 1)
                pe.wait_ge(rt_sb, b + 1)
                pe.wait_ge(l_sb, b + 1)
                for c in range(CB):
                    for k in range(KD):
                        last = nc.tensor.matmul(lbank[:, c * NE:(c + 1) * NE], rt[:, k, c * P:(c + 1) * P], gwt[:, k, :],
                                                start=k == 0, stop=k == KD - 1)
                last.then_inc(l_ps, 1)
                for bank, wgt, done in ((gbank, sg, g_ps), (ubank, su, u_ps)):
                    for f in range(KI):
                        for k in range(KD):
                            last = nc.tensor.matmul(bank[:, f, :], wgt[:, k, f * P:(f + 1) * P], rt[:, k, :],
                                                    start=k == 0, stop=k == KD - 1)
                    last.then_inc(done, 1)
                pe.wait_ge(av_ready, OPEN + b + 1)
                pe.wait_ge(added, b + 1)
                for c in range(CB):
                    for f in range(KI):
                        last = nc.tensor.matmul(dbank[c][:], av[:, f, c * P:(c + 1) * P], sd[:, f, :],
                                                start=f == 0, stop=f == KI - 1)
                last.then_inc(d_ps, 1)

            with pe.Fori(0, B // 2) as i:
                for u in range(2):
                    batch(2 * i + u, u)

    with ExitStack() as sr:
        cst = sbuf(sr, "rt_cst", [P, C_ALL - C_BEF])
        beforeb = sbuf(sr, "rt_before", [P, P], BF16)
        onesb = sbuf(sr, "rt_ones", [P, P], BF16)
        zerob = sbuf(sr, "rt_zero", [P, P], BF16)
        m8 = sbuf(sr, "rt_m8", [P, NT, 8])
        i8 = sbuf(sr, "rt_i8", [P, NT, 8], U32)
        ef = sbuf(sr, "rt_ef", [P, NT, TOPK])
        ex = sbuf(sr, "rt_ex", [P, NT, TOPK])
        es = sbuf(sr, "rt_es", [P, NT])
        oh = sbuf(sr, "rt_oh", [P, TOPK, NT, NE])
        mask = sbuf(sr, "rt_mask", [P, NT, NE])
        maskb = sbuf(sr, "rt_maskb", [P, NT * NE], BF16)
        offs = sbuf(sr, "rt_offs", [P, NT, NE])
        pos = sbuf(sr, "rt_pos", [P, NT, NE])
        prod = sbuf(sr, "rt_prod", [P, TOPK, NT, NE])
        pk = sbuf(sr, "rt_pk", [P, NT, TOPK])
        pi = sbuf(sr, "rt_pi", [P, NT, TOPK], I32)
        li = sbuf(sr, "rt_li", [P, NT, TOPK], I32)
        bi = sbuf(sr, "rt_bi", [P, NT, TOPK], I32)
        lo = sbuf(sr, "rt_lo", [P, NT * TOPK])
        hi = sbuf(sr, "rt_hi", [P, NT * TOPK])
        inb = sbuf(sr, "rt_inb", [P, NT * TOPK])
        sf = sbuf(sr, "rt_sf", [P, NT * TOPK])
        ohlo = sbuf(sr, "rt_ohlo", [P, 2, TOPK, P])
        ohhi = sbuf(sr, "rt_ohhi", [P, 2, TOPK, P])
        rank_bank = psum(sr, "rt_rank", [P, 512])
        cnt_bank = psum(sr, "rt_cnt", [P, 512])
        tab = psum(sr, "rt_tab", [P, P])
        tile_bank = psum(sr, "rt_tile", [P, P])
        tiles = sbuf(sr, "rt_tiles", [P, NE])
        tiles_i = sbuf(sr, "rt_tiles_i", [P, NE], I32)
        ends = sbuf(sr, "rt_ends", [P, NE])
        past = sbuf(sr, "rt_past", [P, NE])
        unit = sbuf(sr, "rt_unit", [P, 1])
        utile = sbuf(sr, "rt_utile", [P, 1])
        utile_w = sbuf(sr, "rt_utile_w", [P, P])
        fill = sbuf(sr, "rt_fill", [P, 2])
        bef, iota, tok = cst[:, 0:P], cst[:, P:2 * P], cst[:, 2 * P:2 * P + NT]
        cst_in, dve_step, step2, ex_in, ex_ready, mask_ready, ranked, hot_ready, hot_used, tile_ps = (
            sem("rt_" + n) for n in ("cst_in", "dve_step", "step2", "ex_in", "ex_ready", "mask_ready", "ranked",
                                     "hot_ready", "hot_used", "tile_ps"))
        fills = sem("rt_fills")
        block = sr.enter_context(nc.Block())

        @block.sync
        def _(sp):
            sp.dma_start(cst[:], a["consts"][:, C_BEF:C_ALL]).then_inc(cst_in, 16)

        @block.gpsimd
        def _(pool):
            nc.gpsimd.memset(onesb[:], 1.0).then_inc(fills, 1)
            nc.gpsimd.memset(zerob[:], 0.0).then_inc(fills, 1)

        @block.scalar
        def _(act):
            act.wait_ge(ex_in, 1)
            nc.scalar.activation(ex[:], ex[:], ACT.Exp).then_inc(ex_ready, 1)

        @block.tensor
        def _(pe):
            pe.sem_inc(hot_used, 2)
            pe.wait_ge(fills, 2)
            nc.tensor.matmul(tab[:], zerob[:], zerob[:], start=True, stop=False, skip_group_check=True)
            pe.wait_ge(mask_ready, 2)
            nc.tensor.matmul(rank_bank[:], beforeb[:], maskb[:], start=True, stop=True)
            nc.tensor.matmul(cnt_bank[:], onesb[:], maskb[:], start=True, stop=True).then_inc(ranked, 1)
            pe.wait_ge(mask_ready, 3)
            nc.tensor.matmul(tile_bank[:], utile_w[:], ident[:], start=True, stop=True).then_inc(tile_ps, 1)
            with pe.Fori(0, NT // 2) as i:
                for u in range(2):
                    pe.wait_ge(hot_ready, 2 * i + u + 1)
                    for k in range(TOPK):
                        last = nc.tensor.matmul(tab[:], ohlo[:, u, k, :], ohhi[:, u, k, :], start=False, stop=False,
                                                skip_group_check=True)
                    last.then_inc(hot_used, 1)

        @block.vector
        def _(dve):
            steps = Steps(dve, dve_step)
            dve.wait_ge(cst_in, 16)
            nc.vector.tensor_copy(beforeb[:], bef).then_inc(mask_ready, 1)
            for t in range(NT):
                steps.did(nc.vector.max(m8[:, t, :], logits[:, t, :]))
            steps.settle()
            for t in range(NT):
                steps.did(nc.vector.max_index(i8[:, t, :], m8[:, t, :], logits[:, t, :]))
            nc.vector.tensor_tensor(ex[:], m8[:, :, 0:TOPK], m8[:, :, 0:1].to_broadcast([P, NT, TOPK]),
                                    ALU.subtract).then_inc(ex_in, 1)
            steps.settle()
            steps.then(nc.vector.tensor_copy(ef[:], i8[:, :, 0:TOPK]))
            for k in range(TOPK):
                steps.did(nc.vector.tensor_tensor(oh[:, k], iota[:, 0:NE].unsqueeze(1).to_broadcast([P, NT, NE]),
                                                  ef[:, :, k:k + 1].to_broadcast([P, NT, NE]), ALU.is_equal))
            steps.settle()
            steps.then(nc.vector.tensor_tensor(mask[:], oh[:, 0], oh[:, 1], ALU.add))
            steps.then(nc.vector.tensor_tensor(mask[:], mask[:], oh[:, 2], ALU.add))
            nc.vector.tensor_tensor(maskb[:].rearrange("p (t n) -> p t n", n=NE), mask[:], oh[:, 3], ALU.add).then_inc(mask_ready, 1)
            steps.then(nc.vector.memset(offs[:, 0, :], 0.0))
            dve.wait_ge(ex_ready, 1)
            steps.then(nc.vector.tensor_reduce(es[:], ex[:], AX.X, ALU.add))
            steps.then(nc.vector.reciprocal(es[:], es[:]))
            steps.did(nc.vector.tensor_tensor(wk[:], ex[:], es[:].unsqueeze(2).to_broadcast([P, NT, TOPK]), ALU.mult))
            dve.wait_ge(ranked, 1)
            for t in range(NT - 1):
                steps.then(nc.vector.tensor_tensor(offs[:, t + 1, :], offs[:, t, :], cnt_bank[:, t * NE:(t + 1) * NE], ALU.add))
            steps.then(nc.vector.tensor_tensor(tiles[:], offs[:, NT - 1, :], cnt_bank[:, (NT - 1) * NE:NT * NE], ALU.add))
            steps.then(nc.vector.tensor_scalar(tiles[:], tiles[:], float(CAP), 1.0, ALU.min, ALU.max))
            steps.then(nc.vector.tensor_copy(tiles_i[:], tiles[:]))
            steps.then(nc.vector.tensor_scalar(tiles_i[:], tiles_i[:], P - 1, None, ALU.add))
            steps.then(nc.vector.tensor_scalar(tiles_i[:], tiles_i[:], P.bit_length() - 1, None, ALU.arith_shift_right))
            steps.then(nc.vector.tensor_copy(tiles[:], tiles_i[:]))
            steps.did(nc.vector.tensor_scalar(unit[:], tok[:, 0:1], float(T), None, ALU.add))
            steps.then(nc.vector.tensor_tensor_scan(ends[:], tiles[:], offs[:, 0, :], 0.0, ALU.add, ALU.add))
            steps.did(nc.vector.tensor_copy(unit_ends[:], ends[:]))
            steps.did(nc.vector.tensor_scalar(past[:], ends[:], unit[:], None, ALU.is_le))
            steps.then(nc.vector.tensor_scalar(tiles[:], tiles[:], -1.0, float(RT), ALU.mult, ALU.add))
            steps.did(nc.vector.tensor_scalar(rounds[:], unit_ends[:, NE - 1:NE], 1, None, ALU.add))
            steps.then(nc.vector.tensor_tensor(past[:], past[:], tiles[:], ALU.mult))
            steps.did(nc.vector.tensor_scalar(rounds[:], rounds[:], 1, None, ALU.arith_shift_right))
            steps.then(nc.vector.tensor_reduce(utile[:], past[:], AX.X, ALU.add))
            steps.then(nc.vector.tensor_scalar(utile[:], utile[:], unit[:], float(ROUTES - 1), ALU.add, ALU.min))
            nc.vector.tensor_copy(utile_w[:], utile[:].to_broadcast([P, P])).then_inc(mask_ready, 1)
            steps.did(nc.vector.memset(fill[:], float(ROUTES - 1)))
            steps.then(nc.vector.tensor_tensor(pos[:], offs[:], rank_bank[:].rearrange("p (t n) -> p t n", n=NE), ALU.add))
            for k in range(TOPK):
                steps.did(nc.vector.tensor_tensor(prod[:, k], oh[:, k], pos[:], ALU.mult))
            steps.settle()
            for k in range(TOPK):
                steps.did(nc.vector.tensor_reduce(pk[:, :, k], prod[:, k], AX.X, ALU.add))
            steps.settle()
            flat = lambda v: v[:].rearrange("p t k -> p (t k)")
            steps.did(nc.vector.tensor_copy(pi[:], pk[:]))
            steps.did(nc.vector.tensor_scalar(sf[:], flat(pk), float(CAP - 1), None, ALU.min))
            steps.then(nc.vector.tensor_scalar(inb[:], flat(pk), float(CAP), None, ALU.is_lt))
            steps.did(nc.vector.tensor_scalar(li[:], pi[:], P - 1, None, ALU.bitwise_and))
            steps.then(nc.vector.tensor_scalar(bi[:], pi[:], P.bit_length() - 1, None, ALU.arith_shift_right))
            steps.did(nc.vector.tensor_copy(lo[:], flat(li)))
            steps.did(nc.vector.scalar_tensor_tensor(slot[:], flat(ef), float(CAP), sf[:], ALU.mult, ALU.add))
            steps.then(nc.vector.tensor_copy(hi[:], flat(bi)))
            steps.then(nc.vector.scalar_tensor_tensor(hi[:], flat(ef), float(RT), hi[:], ALU.mult, ALU.add))
            steps.then(nc.vector.scalar_tensor_tensor(hi[:], hi[:], 1.0, inb[:], ALU.add, ALU.mult))
            steps.then(nc.vector.tensor_scalar(hi[:], hi[:], -1.0, None, ALU.add))
            with dve.Fori(0, NT // 2) as i:
                for u in range(2):
                    t = 2 * i + u
                    dve.wait_ge(hot_used, t + 1)
                    for k in range(TOPK):
                        c = ds(TOPK * t + k, 1)
                        nc.vector.tensor_scalar(ohlo[:, u, k, :], iota, lo[:, c], None, ALU.is_equal)
                        last = nc.vector.tensor_scalar(ohhi[:, u, k, :], iota, hi[:, c], tok[:, ds(t, 1)],
                                                       ALU.is_equal, ALU.mult)
                    last.then_inc(hot_ready, 1)
            dve.wait_ge(tile_ps, 1)
            steps.did(nc.vector.tensor_copy(unit_tile[:, 0:ROUTES], tile_bank[:]))
            steps.did(nc.vector.tensor_copy(unit_tile[:, ROUTES:], fill[:]))
            dve.wait_ge(hot_used, 2 + NT)
            steps.then(nc.vector.tensor_scalar(route[:], tab[:], float(T), None, ALU.add))

    with ExitStack() as se:
        ix = [sbuf(se, f"x_ix{s}", [P, 1], I32) for s in range(2)]
        xg = [sbuf(se, f"x_g{s}", [P, D]) for s in range(2)]
        xt = [sbuf(se, f"x_t{s}", [P, KD, P]) for s in range(2)]
        gs = [sbuf(se, f"x_gs{s}", [P, FI]) for s in range(2)]
        av = [sbuf(se, f"x_av{s}", [P, FI]) for s in range(2)]
        avt = [sbuf(se, f"x_avt{s}", [P, KI, P]) for s in range(2)]
        eo = [sbuf(se, f"x_eo{s}", [P, D]) for s in range(2)]
        xbank = [psum(se, f"x_xb{s}", [P, D]) for s in range(2)]
        hbank = [psum(se, f"x_h{s}", [P, 2 * FI]) for s in range(2)]
        abank = [psum(se, f"x_ab{s}", [P, FI]) for s in range(2)]
        obank = [psum(se, f"x_o{s}", [P, D]) for s in range(2)]
        got = [sem(f"x_got{s}") for s in range(2)]
        eo_out = [sem(f"x_out{s}") for s in range(2)]
        fills, ix_ready, w_ready, xt_ps, xt_sb, h_ps, gs_ready, av_ready, at_ps, at_sb, eo_ps, eo_sb = (
            sem("x_" + n) for n in ("fills", "ix_ready", "w_ready", "xt_ps", "xt_sb", "h_ps", "gs_ready", "av_ready",
                                    "at_ps", "at_sb", "eo_ps", "eo_sb"))
        OPEN = 2
        block = se.enter_context(nc.Block())

        def count(eng):
            return eng.value_load(rounds[0:1, 0:1], min_val=1, max_val=ROUTES // 2)

        def tile_of(eng, j):
            return eng.value_load(unit_tile[0:1, ds(j, 1)], min_val=0, max_val=ROUTES - 1)

        @block.gpsimd
        def _(pool):
            for s in range(2):
                nc.gpsimd.memset(xg[s][:], 0.0).then_inc(fills, 1)
            pool.wait_ge(fills, 2)
            n = count(pool)
            with pool.Fori(0, n + 1) as i:
                for s in range(2):
                    j = 2 * i + s
                    pool.wait_ge(xt_ps, OPEN + j - 1)
                    nc.gpsimd.tensor_copy(ix[s][:], route[:, ds(tile_of(pool, j), 1)]).then_inc(ix_ready, 1)
                    pool.wait_ge(ix_ready, j + 1)
                    nc.gpsimd.tensor_tensor(carry[:, s:s + 1], powers[:, 0:1], powers[:, 0:1], ALU.mult)
                    nc.gpsimd.indirect_dma_start(
                        out=xg[s][:], out_offset=None, in_=r_d,
                        in_offset=bass.IndirectOffsetOnAxis(ap=ix[s][:], axis=0),
                        bounds_check=T - 1, oob_is_err=False).then_inc(got[s], 16)

        @block.sync
        def _(sp):
            def arrived(i, u):
                sp.wait_ge(w13_in[u], 16 * i + 16)
                sp.wait_ge(w2_in[u], 16 * i + 16)
                sp.sem_inc(w_ready, 1)

            arrived(0, 0)
            with sp.Fori(0, NE // 2 - 1) as i:
                for u in range(2):
                    e = 2 * i + u
                    arrived(i + u, 1 - u)
                    sp.wait_ge(eo_ps, OPEN + sp.value_load(unit_ends[0:1, ds(e, 1)], min_val=0, max_val=ROUTES))
                    load_w13(sp, e + 2, u)
                    load_w2(sp, e + 2, u)
            arrived(NE // 2 - 1, 1)

        @block.tensor
        def _(pe):
            def turn(i, s):
                pe.wait_ge(got[s], 16 * i + 16)
                for k in range(KD):
                    last = nc.tensor.transpose(xbank[s][:, k * P:(k + 1) * P], xg[s][:, k * P:(k + 1) * P], ident[:])
                last.then_inc(xt_ps, 1)

            def up(i, s):
                e = tile_of(pe, 2 * i + s) // RT
                pe.wait_ge(w_ready, e + 1)
                pe.wait_ge(xt_sb, 2 * i + s + 1)
                for k in range(KD):
                    last = nc.tensor.matmul(hbank[s][:], xt[s][:, k, :], w13[:, ds(e % 2, 1), k, :],
                                            start=k == 0, stop=k == KD - 1)
                last.then_inc(h_ps, 1)
                return e % 2

            def turn_act(i, s):
                pe.wait_ge(av_ready, OPEN + 2 * i + s + 1)
                for f in range(KI):
                    last = nc.tensor.transpose(abank[s][:, f * P:(f + 1) * P], av[s][:, f * P:(f + 1) * P], ident[:])
                last.then_inc(at_ps, 1)

            def down(i, s, half, between=None):
                pe.wait_ge(at_sb, 2 * i + s + 1)
                pe.wait_ge(eo_sb, OPEN + 2 * i + s - 1)
                for f in range(KI):
                    last = nc.tensor.matmul(obank[s][:], avt[s][:, f, :], w2[:, ds(half, 1), f, :],
                                            start=f == 0, stop=f == KI - 1)
                    if between and f == 0:
                        between()
                last.then_inc(eo_ps, 1)

            for opened in (xt_ps, at_ps, eo_ps):
                pe.sem_inc(opened, OPEN)
            pe.wait_ge(fills, 2)
            turn(0, 0)
            turn(0, 1)
            n = count(pe)
            with pe.Fori(0, n) as i:
                half = [up(i, 0), up(i, 1)]
                turn_act(i, 0)
                turn(i + 1, 0)
                turn(i + 1, 1)
                down(i, 0, half[0], between=lambda: turn_act(i, 1))
                down(i, 1, half[1])

        @block.scalar
        def _(act):
            def turned(i, s):
                act.wait_ge(xt_ps, OPEN + 2 * i + s + 1)
                nc.scalar.copy(xt[s][:], xbank[s][:].rearrange("p (k n) -> p k n", n=P)).then_inc(xt_sb, 1)

            act.sem_inc(eo_sb, OPEN)
            for s in range(2):
                act.sem_inc(eo_out[s], 16)
            turned(0, 0)
            turned(0, 1)
            n = count(act)
            with act.Fori(0, n) as i:
                for s in range(2):
                    act.wait_ge(h_ps, 2 * i + s + 1)
                    act.wait_ge(av_ready, OPEN + 2 * i + s - 1)
                    nc.scalar.activation(gs[s][:], hbank[s][:, 0:FI], ACT.Silu).then_inc(gs_ready, 1)
                for s in range(2):
                    turned(i + 1, s)
                for s in range(2):
                    act.wait_ge(eo_ps, OPEN + 2 * i + s + 1)
                    act.wait_ge(eo_out[s], 16 * i + 16)
                    nc.scalar.copy(eo[s][:], obank[s][:]).then_inc(eo_sb, 1)
                    act.wait_ge(eo_sb, OPEN + 2 * i + s + 1)
                    act.dma_start(eo_d[ds(P * tile_of(act, 2 * i + s), P), :], eo[s][:]).then_inc(eo_out[s], 16)
            for s in range(2):
                act.wait_ge(eo_out[s], 16 * n + 16)
                nc.scalar.copy(eo[s][:, 0:1], xt[s][:, 0, 0:1])

        @block.vector
        def _(dve):
            dve.sem_inc(av_ready, OPEN)
            n = count(dve)
            with dve.Fori(0, n) as i:
                def gated(s):
                    dve.wait_ge(gs_ready, 2 * i + s + 1)
                    dve.wait_ge(at_ps, OPEN + 2 * i + s - 1)
                    nc.vector.tensor_tensor(av[s][:], gs[s][:], hbank[s][:, FI:2 * FI], ALU.mult).then_inc(av_ready, 1)

                def turned_act(s):
                    dve.wait_ge(at_ps, OPEN + 2 * i + s + 1)
                    dve.wait_ge(eo_ps, OPEN + 2 * i + s - 1)
                    nc.vector.tensor_copy(avt[s][:], abank[s][:].rearrange("p (f n) -> p f n", n=P)).then_inc(at_sb, 1)

                gated(0)
                turned_act(0)
                gated(1)
                turned_act(1)

    with ExitStack() as sc:
        sx = [sbuf(sc, f"c_sx{u}", [P, TOPK], I32) for u in range(2)]
        rows = [sbuf(sc, f"c_rows{u}", [P, TOPK, D]) for u in range(2)]
        y = sbuf(sc, "c_y", [P, 2, D])
        got = [sem(f"c_got{u}") for u in range(2)]
        y_out = [sem(f"c_out{u}") for u in range(2)]
        sx_ready, dve_step, y_ready, y_free = (sem("c_" + n) for n in ("sx_ready", "dve_step", "y_ready", "y_free"))
        out_rows = out.rearrange("b (c p) d -> p (b c) d", p=P)
        block = sc.enter_context(nc.Block())

        @block.gpsimd
        def _(pool):
            with pool.Fori(0, NT // 2) as i:
                for u in range(2):
                    t = 2 * i + u
                    pool.wait_ge(y_ready, t + 1)
                    nc.gpsimd.tensor_copy(sx[u][:], slot[:, ds(TOPK * t, TOPK)]).then_inc(sx_ready, 1)
                    pool.wait_ge(sx_ready, t + 1)
                    nc.gpsimd.tensor_tensor(carry[:, u:u + 1], powers[:, 0:1], powers[:, 0:1], ALU.mult)
                    for k in range(TOPK):
                        nc.gpsimd.indirect_dma_start(
                            out=rows[u][:, k, :], out_offset=None, in_=eo_d,
                            in_offset=bass.IndirectOffsetOnAxis(ap=sx[u][:, k:k + 1], axis=0),
                            bounds_check=NE * CAP - 1, oob_is_err=False).then_inc(got[u], 16)

        @block.vector
        def _(dve):
            steps = Steps(dve, dve_step)
            dve.sem_inc(y_ready, 2)
            with steps.loop(0, NT // 2, 2 * (TOPK - 1)) as i:
                for u in range(2):
                    t = 2 * i + u
                    dve.wait_ge(got[u], 16 * TOPK * (i + 1))
                    dve.wait_ge(y_free, t + 1)
                    for k in range(TOPK):
                        ins = nc.vector.scalar_tensor_tensor(
                            y[:, u], rows[u][:, k, :], wk[:].rearrange("p t k -> p (t k)")[:, ds(TOPK * t + k, 1)],
                            x[:, ds(t, 1), :].rearrange("p o d -> p (o d)") if k == 0 else y[:, u], ALU.mult, ALU.add)
                        if k < TOPK - 1:
                            steps.then(ins)
                        else:
                            ins.then_inc(y_ready, 1)

        @block.sync
        def _(sp):
            sp.sem_inc(y_free, 2)
            with sp.Fori(0, NT // 2) as i:
                for u in range(2):
                    t = 2 * i + u
                    sp.wait_ge(y_ready, 2 + t + 1)
                    sp.dma_start(out_rows[:, ds(t, 1), :].rearrange("p o d -> p (o d)"), y[:, u]).then_inc(y_out[u], 16)
                    sp.wait_ge(y_out[u], 16 * i + 16)
                    sp.sem_inc(y_free, 1)


_INS = ["x", "ctx_2048", "L0_xattn_Wh", "L0_xattn_wg_w", "L0_xattn_wo_w", "L0_xattn_gn_gamma", "L0_xattn_gn_beta",
        "L0_ffn_w1", "L0_ffn_w2", "L0_ffn_w3", "L1_xattn_Wi", "L1_xattn_bi", "L1_xattn_Wf", "L1_xattn_bf",
        "L1_xattn_ln_scale", "L1_ffn_norm_w", "L1_ffn_gate_w", "L1_ffn_w13", "L1_ffn_w2", "L1_ffn_shared_gate_w",
        "L1_ffn_shared_up_w", "L1_ffn_shared_down_w"]


def kernel(**inputs):
    import concourse.bacc as bacc
    from concourse.bass_utils import run_bass_kernel_spmd

    nc = bacc.Bacc("TRN2", target_bir_lowering=False, num_devices=1)
    arrays = {f"in_{n}": np.ascontiguousarray(inputs[n]) for n in _INS}
    arrays["in_consts"] = shape_constants()
    a = {n[3:]: nc.dram_tensor(n, v.shape, mybir.dt.from_np(v.dtype), kind="ExternalInput").ap()
         for n, v in arrays.items()}
    out = nc.dram_tensor("out_x", (B, S, D), F32, kind="ExternalOutput").ap()
    program(nc, a, out)
    r = run_bass_kernel_spmd(nc, [arrays], core_ids=[0])
    return r.results[0]["out_x"]
```

```python
from contextlib import ExitStack, contextmanager

import numpy as np

import concourse.bass as bass
from concourse import mybir

ALU = mybir.AluOpType
ACT = mybir.ActivationFunctionType
AX = mybir.AxisListType
F32 = mybir.dt.float32
F32R = mybir.dt.float32r
BF16 = mybir.dt.bfloat16
I32 = mybir.dt.int32
U32 = mybir.dt.uint32
ds = bass.ds

P = 128
B, S, D = 8, 256, 512
KD = D // P
CB = S // P
T = B * S
NT = T // P
LN_EPS = 1e-5
H0 = 4
HD = D // H0
GN_EPS = 1e-3
F0 = 1408
KF = F0 // P
Q_EPS = 1e-5
ROUND = float(1.5 * 2 ** 23)
NH = 16
DH = D // NH
HG = P // DH
NG = NH // HG
M_EPS = 1e-6
MASKED = -1e30
NE, TOPK, FI = 32, 4, 256
CAP = 2 * T * TOPK // NE
RT = CAP // P
KI = FI // P
ROUTES = NE * RT


class Steps:

    def __init__(self, eng, sem):
        self.eng, self.sem, self.n, self.base = eng, sem, 0, 0

    def did(self, ins):
        ins.then_inc(self.sem, 1)
        self.n += 1

    def settle(self):
        self.eng.wait_ge(self.sem, self.base + self.n)

    def then(self, ins):
        self.did(ins)
        self.settle()

    @contextmanager
    def loop(self, lo, hi, per):
        before = self.n
        with self.eng.Fori(lo, hi) as i:
            self.base, self.n = (i - lo) * per + before, 0
            yield i
            assert self.n == per, f"{self.sem}: {self.n} steps in a round"
        self.base, self.n = 0, before + (hi - lo) * per


def shape_constants():
    gam = 1.0 - 2.0 ** (-5.0 - np.arange(H0, dtype=np.float64))
    pos = np.arange(S, dtype=np.float64)
    expo = pos[None, :] - pos[:, None]
    dec = np.where(expo[None] <= 0, gam[:, None, None] ** np.minimum(expo, 0)[None], 0.0)
    dec = dec / np.sqrt(dec.sum(-1))[:, None, :] / np.sqrt(float(HD))
    dect = dec.transpose(2, 0, 1)
    first = dect[:P].reshape(P, H0 * S)
    second = dect[P:, :, P:].reshape(P, H0 * P)
    decay = np.concatenate([first, second], 1).astype(np.float32)
    r = np.arange(P)
    ident = np.eye(P, dtype=np.float32)
    future = np.where(r[:, None] <= r[None, :], 0.0, MASKED).astype(np.float32)
    before = (r[:, None] < r[None, :]).astype(np.float32)
    iota = np.broadcast_to(r.astype(np.float32), (P, P))
    token = (np.arange(NT)[None, :] * P + r[:, None] - T).astype(np.float32)
    return np.concatenate([decay, ident, future, before, iota, token], 1)


C_DEC, C_ID = 0, H0 * (S + P)
C_FUT, C_BEF, C_IOTA, C_TOK = C_ID + P, C_ID + 2 * P, C_ID + 3 * P, C_ID + 4 * P
C_ALL = C_TOK + NT


def program(nc, a, out):
    with ExitStack() as top:
        held = [ExitStack(), []]

        def sem(name):
            held[1].append(held[0].enter_context(nc.semaphore(name)))
            return held[1][-1]

        def clear_semaphores():
            with nc.Block() as block:
                @block.gpsimd
                def _(pool):
                    nums = sorted(s.num for s in held[1])
                    runs = [n for n in nums if n - 1 not in nums]
                    for lo in runs:
                        hi = next(n for n in range(lo, 257) if n not in nums)
                        pool.sem_clear(range(lo, hi))
            held[0].close()
            held[:] = [ExitStack(), []]

        def scratch_dram(name, shape, dt=F32):
            return nc.dram_tensor(name, shape, dt, kind="Internal").ap()

        def psum(st, name, shape, dt=F32):
            return st.enter_context(nc.psum_tensor(name, shape, dt))

        def sbuf(st, name, shape, dt=F32):
            return st.enter_context(nc.sbuf_tensor(name, shape, dt))

        x = sbuf(top, "x_res", [P, NT, D])
        ident = sbuf(top, "ident", [P, P])
        powers = sbuf(top, "powers", [P, 2])
        x_rows = a["x"].rearrange("b (c p) d -> p (b c) d", p=P)
        eo_d = scratch_dram("eo_d", [NE * CAP, D])
        ctx_rows = a["ctx_2048"].rearrange("b (c p) d -> p (b c) d", p=P)

        with ExitStack() as st:
            tern = {n: sbuf(st, f"tern_{n}", [P, KF * D], BF16) for n in ("w1", "w3", "w2")}
            w_mean = sbuf(st, "w_mean", [P, 3])
            raw = sbuf(st, "raw", [P, KF * D])
            with ExitStack() as sr:
                retention(nc, sr, sem, sbuf, psum, a, x, x_rows, ctx_rows, ident, powers, tern, w_mean, raw)
            bit_ffn(nc, st, sem, sbuf, psum, eo_d, x, ident, powers, tern, w_mean)
        clear_semaphores()
        with ExitStack() as st:
            mlstm(nc, st, sem, sbuf, psum, scratch_dram, a, x, ctx_rows, ident, powers)
        with ExitStack() as st:
            experts(nc, st, sem, sbuf, psum, scratch_dram, eo_d, a, x, ident, powers, out)
        held[0].close()


class Norm:

    def __init__(self, nc, st, sem, sbuf, name, lanes):
        self.nc = nc
        self.st6 = sbuf(st, f"{name}_st6", [P, lanes, 6])
        self.mv = sbuf(st, f"{name}_mv", [P, lanes, 2])
        self.ve = sbuf(st, f"{name}_ve", [P, lanes])
        self.rstd = sbuf(st, f"{name}_rstd", [P, lanes])
        self.var_ready = sem(f"{name}_var_ready")
        self.rstd_ready = sem(f"{name}_rstd_ready")

    def stats(self, steps, sources, eps):
        for c, src in enumerate(sources):
            steps.did(self.nc.vector.bn_stats(self.st6[:, c, :], src))
        steps.settle()
        self.nc.vector.tensor_copy(self.ve[:, 0:1], self.st6[:, 0, 0:1])
        for c in range(len(sources)):
            steps.did(self.nc.vector.bn_aggr(self.mv[:, c, :], self.st6[:, c, :]))
        steps.settle()
        self.nc.vector.tensor_scalar(self.ve[:, 0:len(sources)], self.mv[:, 0:len(sources), 1], eps, None,
                                     ALU.add).then_inc(self.var_ready, 1)

    def power(self, pool, powers, n, lanes):
        pool.wait_ge(self.var_ready, n)
        self.nc.gpsimd.tensor_tensor(self.rstd[:, 0:lanes], self.ve[:, 0:lanes],
                                     powers[:, 0:1].to_broadcast([P, lanes]), ALU.pow).then_inc(self.rstd_ready, 1)


def retention(nc, st, sem, sbuf, psum, a, x, x_rows, ctx_rows, ident, powers, tern, w_mean, raw):
    vt = sbuf(st, "v_rows", [P, NT, D])
    wt = sbuf(st, "gate_t", [P, KD, T])
    at = sbuf(st, "a_t", [P, H0 * (S + P)])
    ones = sbuf(st, "ones", [P, P])
    rsum = sbuf(st, "rsum", [P, 3])
    wrec = sbuf(st, "wrec", [P, 3])

    raw_in = [sem(f"raw_in{j}") for j in range(3)]
    abs_done = sem("abs_done")
    pool_step = sem("r_pool_step")
    mean_ready = sem("mean_ready")
    names = ("w1", "w3", "w2")

    def load_raw(eng, j, dst):
        src = a[f"L0_ffn_{names[j]}"].rearrange("(j p) d -> p j d", p=P)
        eng.dma_start(dst[:].rearrange("p (j d) -> p j d", j=src.shape[1]), src).then_inc(raw_in[j], 16)

    def abs_sum(act, j, src):
        act.wait_ge(raw_in[j], 16)
        nc.scalar.activation(tern[names[j]][:], src[:], ACT.Abs, accum_out=rsum[:, j:j + 1]).then_inc(abs_done, 1)

    def mean(pool, steps, j):
        pool.wait_ge(abs_done, j + 1)
        m = w_mean[:, j:j + 1]
        steps.then(nc.gpsimd.partition_all_reduce(m, rsum[:, j:j + 1], P, bass.bass_isa.ReduceOp.add))
        steps.then(nc.gpsimd.tensor_scalar(m, m, 1.0 / (F0 * D), Q_EPS, ALU.mult, ALU.max))
        nc.gpsimd.tensor_tensor(wrec[:, j:j + 1], m, powers[:, 1:2], ALU.pow).then_inc(mean_ready, 1)

    def ternary(steps, weights, start, n):
        cols = ds(start, n)
        for j, src in weights:
            steps.did(nc.vector.tensor_scalar(src[:, cols], src[:, cols], wrec[:, j:j + 1], ROUND, ALU.mult, ALU.add))
        steps.settle()
        for j, src in weights:
            steps.did(nc.vector.tensor_scalar(src[:, cols], src[:, cols], ROUND, 1.0, ALU.subtract, ALU.min))
        steps.settle()
        for j, src in weights:
            steps.did(nc.vector.tensor_scalar(tern[names[j]][:, cols], src[:, cols], -1.0, None, ALU.max))

    with ExitStack() as sa:
        acc = psum(sa, "acc", [P, 3, 512])
        ring = [psum(sa, f"ring{i}", [P, 512]) for i in range(5)]
        decay = sbuf(sa, "decay", [P, H0 * (S + P)])
        wh = sbuf(sa, "wh", [P, H0, HD])
        wht = sbuf(sa, "wht", [P, H0, HD])
        gram = sbuf(sa, "gram", [P, H0, HD])
        wg = sbuf(sa, "wg", [P, KD, D])
        cx = sbuf(sa, "ctx_in", [P, 2, CB, D])
        xn = sbuf(sa, "xn", [P, CB, D])
        xt = sbuf(sa, "xt", [P, KD, S])
        ct = sbuf(sa, "ct", [P, KD, S])
        qt = sbuf(sa, "qt", [P, H0, S])
        zeros = sbuf(sa, "zeros", [P, 512], BF16)
        norm = Norm(nc, sa, sem, sbuf, "ln0", CB)
        x_in = [sem(f"x_in{i}") for i in range(2)]
        c_in = [sem(f"ctx_in{i}") for i in range(2)]
        ident_in, wh_in, wg_in, decay_in = (sem(n) for n in ("ident_in", "wh_in", "wg_in", "decay_in"))
        fill_done, dve_step = sem("fill_done"), sem("r_dve_step")
        setup_ps, setup_sb = sem("setup_ps"), sem("setup_sb")
        xn_ready, xt_ps, ct_ps, xt_sb, ct_sb = (sem(n) for n in ("xn_ready", "xt_ps", "ct_ps", "xt_sb", "ct_sb"))
        q_ps, v_ps, w_ps, q_sb, v_sb, w_sb = (sem(n) for n in ("q_ps", "v_ps", "w_ps", "q_sb", "v_sb", "w_sb"))
        scored, a_ready, ctx_used = sem("scored"), sem("a_ready"), sem("ctx_used")
        block = sa.enter_context(nc.Block())

        @block.sync
        def _(sp):
            sp.dma_start(x[:, 0:CB, :], x_rows[:, 0:CB, :]).then_inc(x_in[0], 16)
            sp.dma_start(ident[:], a["consts"][:, C_ID:C_ID + P]).then_inc(ident_in, 16)
            sp.dma_start(wh[:], a["L0_xattn_Wh"].rearrange("h d e -> d h e")).then_inc(wh_in, 16)
            sp.dma_start(cx[:, 0], ctx_rows[:, 0:CB, :]).then_inc(c_in[0], 16)
            sp.dma_start(wg[:], a["L0_xattn_wg_w"].rearrange("(k p) n -> p k n", p=P)).then_inc(wg_in, 16)
            sp.dma_start(x[:, CB:2 * CB, :], x_rows[:, CB:2 * CB, :]).then_inc(x_in[1], 16)
            sp.dma_start(cx[:, 1], ctx_rows[:, CB:2 * CB, :]).then_inc(c_in[1], 16)
            load_raw(sp, 0, raw)
            with sp.Fori(0, B // 2 - 1) as i:
                for u in range(2):
                    at_b = 2 * CB * i + CB * (2 + u)
                    sp.wait_ge(x_in[u], 16 * i + 16)
                    sp.dma_start(x[:, ds(at_b, CB), :], x_rows[:, ds(at_b, CB), :]).then_inc(x_in[u], 16)
                    sp.wait_ge(ct_ps, 4 * i + 2 * u + 2)
                    sp.dma_start(cx[:, u], ctx_rows[:, ds(at_b, CB), :]).then_inc(c_in[u], 16)
            sp.dma_start(decay[:], a["consts"][:, C_DEC:C_DEC + H0 * (S + P)]).then_inc(decay_in, 16)

        @block.gpsimd
        def _(pool):
            steps = Steps(pool, pool_step)
            nc.gpsimd.memset(zeros[:], 0.0).then_inc(fill_done, 1)
            nc.gpsimd.memset(powers[:, 0:1], -0.5).then_inc(fill_done, 1)
            nc.gpsimd.memset(powers[:, 1:2], -1.0).then_inc(fill_done, 1)
            nc.gpsimd.memset(ones[:], 1.0).then_inc(fill_done, 1)
            pool.wait_ge(fill_done, 4)
            norm.power(pool, powers, 1, CB)
            with pool.Fori(0, B - 4) as b:
                norm.power(pool, powers, b + 2, CB)
            mean(pool, steps, 0)
            for b in range(B - 4, B - 1):
                norm.power(pool, powers, b + 2, CB)

        @block.vector
        def _(dve):
            steps = Steps(dve, dve_step)

            def normalise(b, i, u):
                dve.wait_ge(x_in[u], 16 * i + 16)
                norm.stats(steps, [x[:, CB * b + c, :] if isinstance(b, int) else x[:, ds(CB * b + c, 1), :]
                                   for c in range(CB)], LN_EPS)
                dve.wait_ge(norm.rstd_ready, b + 1)
                for c in range(CB):
                    nc.vector.tensor_scalar(xn[:, c, :], x[:, ds(CB * b + c, 1), :], norm.mv[:, c, 0:1],
                                            norm.rstd[:, c:c + 1], ALU.subtract, ALU.mult).then_inc(xn_ready, 1)

            def copies(b, src_sem, counts, ring_at, dst, done):
                for c in range(CB):
                    dve.wait_ge(src_sem, 2 * b + c + 1)
                    nc.vector.tensor_copy(dst(c), ring[ring_at[c]][:].rearrange("p (k n) -> p k n", n=P)).then_inc(done, 1)

            def batch(b, nxt):
                copies(b, ct_ps, None, (1, 3), lambda c: ct[:, :, c * P:(c + 1) * P], ct_sb)
                if nxt is not None:
                    normalise(b + 1, *nxt)
                for c in range(CB):
                    dve.wait_ge(v_ps, 2 * b + c + 1)
                    nc.vector.tensor_copy(vt[:, ds(CB * b + c, 1), :], ring[1 + c][:]).then_inc(v_sb, 1)

            dve.wait_ge(setup_ps, 1)
            nc.vector.tensor_copy(wht[:], ring[0][:].rearrange("p (h n) -> p h n", n=P)).then_inc(setup_sb, 1)
            dve.wait_ge(setup_ps, 2)
            nc.vector.tensor_copy(gram[:], ring[1][:].rearrange("p (h n) -> p h n", n=P)).then_inc(setup_sb, 1)
            normalise(0, 0, 0)
            with steps.loop(0, B // 2 - 1, 8) as i:
                batch(2 * i, (i, 1))
                batch(2 * i + 1, (i + 1, 0))
            half = KF * D // 2
            dve.wait_ge(mean_ready, 1)
            ternary(steps, [(0, raw)], 0, half)
            batch(B - 2, (B // 2 - 1, 1))
            ternary(steps, [(0, raw)], half, half)
            batch(B - 1, None)
            dve.wait_ge(scored, B)
            dve.wait_ge(decay_in, 16)
            flat = acc[:].rearrange("p n d -> p (n d)")
            steps.then(nc.vector.tensor_tensor(at[:], flat, decay[:], ALU.mult))
            steps.then(nc.vector.scalar_tensor_tensor(at[:], at[:], -1.0, at[:], ALU.mult, ALU.max))
            nc.vector.tensor_scalar(at[:], at[:], 1.0, None, ALU.max).then_inc(a_ready, 1)

        @block.scalar
        def _(act):
            def batch(b):
                for c in range(CB):
                    act.wait_ge(xt_ps, 2 * b + c + 1)
                    nc.scalar.copy(xt[:, :, c * P:(c + 1) * P],
                                   ring[2 * c][:].rearrange("p (k n) -> p k n", n=P)).then_inc(xt_sb, 1)
                for c in range(CB):
                    act.wait_ge(q_ps, 2 * b + c + 1)
                    nc.scalar.copy(qt[:, :, c * P:(c + 1) * P],
                                   ring[(4, 0)[c]][:].rearrange("p (k n) -> p k n", n=P)).then_inc(q_sb, 1)
                for c in range(2):
                    act.wait_ge(w_ps, 2 * b + c + 1)
                    nc.scalar.activation(wt[:, 2 * c:2 * c + 2, ds(S * b, S)],
                                         ring[3 + c][:].rearrange("p (k n) -> p k n", n=S), ACT.Relu).then_inc(w_sb, 1)

            with act.Fori(0, B - 4) as b:
                batch(b)
            abs_sum(act, 0, raw)
            with act.Fori(B - 4, B) as b:
                batch(b)

        @block.tensor
        def _(pe):
            pe.wait_ge(ident_in, 16)
            pe.wait_ge(wh_in, 16)
            pe.wait_ge(fill_done, 4)
            for h in range(H0):
                last = nc.tensor.transpose(ring[0][:, h * P:(h + 1) * P], wh[:, h, :], ident[:])
            last.then_inc(setup_ps, 1)
            for n in range(3):
                nc.tensor.matmul(acc[:, n, :], zeros[:, 0:P], zeros[:], start=True, stop=False, skip_group_check=True)
            pe.wait_ge(setup_sb, 1)
            for h in range(H0):
                last = nc.tensor.matmul(ring[1][:, h * P:(h + 1) * P], wht[:, h, :], wht[:, h, :], start=True, stop=True)
            last.then_inc(setup_ps, 1)
            pe.wait_ge(setup_sb, 2)
            pe.wait_ge(wg_in, 16)

            def turn(dst, src, done):
                for k in range(KD):
                    last = nc.tensor.transpose(dst[:, k * P:(k + 1) * P], src[:, k * P:(k + 1) * P], ident[:])
                last.then_inc(done, 1)

            def batch(b, i, u, first=False):
                for c in range(CB):
                    pe.wait_ge(xn_ready, 2 * b + c + 1)
                    if not first:
                        pe.wait_ge(*((q_sb, 2 * b), (v_sb, 2 * b))[c])
                    turn(ring[2 * c], xn[:, c, :], xt_ps)
                    if c == 0:
                        pe.wait_ge(c_in[u], 16 * i + 16)
                    if not first:
                        pe.wait_ge(*((v_sb, 2 * b - 1), (w_sb, 2 * b - 1))[c])
                    turn(ring[2 * c + 1], cx[:, u, c, :], ct_ps)
                for c in range(CB):
                    pe.wait_ge(xt_sb, 2 * b + c + 1)
                    if c == 0 and not first:
                        pe.wait_ge(w_sb, 2 * b)
                    for h in range(H0):
                        last = nc.tensor.matmul(ring[(4, 0)[c]][:, h * P:(h + 1) * P], gram[:, h, :],
                                                xt[:, h, c * P:(c + 1) * P], start=True, stop=True)
                    last.then_inc(q_ps, 1)
                for c in range(CB):
                    pe.wait_ge(ct_sb, 2 * b + c + 1)
                    for h in range(H0):
                        last = nc.tensor.matmul(ring[1 + c][:, h * P:(h + 1) * P], ct[:, h, c * P:(c + 1) * P],
                                                wh[:, h, :], start=True, stop=True)
                    last.then_inc(v_ps, 1)
                for n in range(2):
                    if n == 1:
                        pe.wait_ge(q_sb, 2 * b + 1)
                    for j in range(2):
                        m = 2 * n + j
                        for k in range(KD):
                            last = nc.tensor.matmul(ring[3 + n][:, j * S:(j + 1) * S], wg[:, k, m * P:(m + 1) * P],
                                                    xt[:, k, :], start=k == 0, stop=k == KD - 1)
                    last.then_inc(w_ps, 1)
                pe.wait_ge(q_sb, 2 * b + 2)
                for h in range(H0):
                    nc.tensor.matmul(acc[:, h // 2, (h % 2) * S:(h % 2 + 1) * S], ct[:, h, 0:P], qt[:, h, :],
                                     start=False, stop=False, skip_group_check=True)
                    last = nc.tensor.matmul(acc[:, 2, h * P:(h + 1) * P], ct[:, h, P:S], qt[:, h, P:S],
                                            start=False, stop=False, skip_group_check=True)
                last.then_inc(scored, 1)

            batch(0, 0, 0, first=True)
            batch(1, 0, 1)
            with pe.Fori(1, B // 2) as i:
                batch(2 * i, i, 0)
                batch(2 * i + 1, i, 1)

    with ExitStack() as sb_:
        wo = sbuf(sb_, "wo", [P, KD, D])
        gam = sbuf(sb_, "gn_gamma", [P, KD])
        bet = sbuf(sb_, "gn_beta", [P, KD])
        y = sbuf(sb_, "gn_y", [P, CB, D])
        zt = sbuf(sb_, "z_t", [P, CB, D])
        raw2 = sbuf(sb_, "raw2", [P, KF * D])
        o_bank = [psum(sb_, f"o_bank{c}", [P, D]) for c in range(CB)]
        y_bank = [psum(sb_, f"y_bank{c}", [P, D]) for c in range(CB)]
        p_bank = [psum(sb_, f"p_bank{c}", [P, D]) for c in range(CB)]
        norm = Norm(nc, sb_, sem, sbuf, "gn", CB)
        wo_in, dve_step = sem("wo_in"), sem("gn_dve_step")
        o_ps, y_ready, y_ps, y_scaled, z_ready, p_ps, x_added = (
            sem(n) for n in ("o_ps", "y_ready", "y_ps", "y_scaled", "z_ready", "p_ps", "x_added"))
        MEAN_STEPS = 2
        QUIET = 3
        block = sb_.enter_context(nc.Block())

        @block.sync
        def _(sp):
            sp.dma_start(wo[:], a["L0_xattn_wo_w"].rearrange("(k p) n -> p k n", p=P)).then_inc(wo_in, 16)
            sp.dma_start(gam[:], a["L0_xattn_gn_gamma"].rearrange("(k p) -> p k", p=P),
                         allow_slow_non_contiguous=True).then_inc(wo_in, 16)
            sp.dma_start(bet[:], a["L0_xattn_gn_beta"].rearrange("(k p) -> p k", p=P),
                         allow_slow_non_contiguous=True).then_inc(wo_in, 16)
            load_raw(sp, 1, raw)
            load_raw(sp, 2, raw2)

        @block.gpsimd
        def _(pool):
            steps = Steps(pool, pool_step)
            steps.n = MEAN_STEPS
            with pool.Fori(0, QUIET + 1) as b:
                norm.power(pool, powers, b + 1, CB)
            mean(pool, steps, 1)
            mean(pool, steps, 2)
            with pool.Fori(QUIET + 1, B) as b:
                norm.power(pool, powers, b + 1, CB)

        def pv(b):
            for c in range(CB):
                for h in range(H0):
                    col = c * P
                    nc.tensor.matmul(o_bank[c][:, h * P:(h + 1) * P], at[:, h * S + col:h * S + col + P],
                                     vt[:, ds(CB * b, 1), h * P:(h + 1) * P], start=True, stop=False)
                    second = ones[:] if c == 0 else at[:, H0 * S + h * P:H0 * S + (h + 1) * P]
                    last = nc.tensor.matmul(o_bank[c][:, h * P:(h + 1) * P], second,
                                            vt[:, ds(CB * b + 1, 1), h * P:(h + 1) * P], start=False, stop=True)
                last.then_inc(o_ps, 1)

        @block.tensor
        def _(pe):
            def batch(b, first=False, final=False):
                for c in range(CB):
                    pe.wait_ge(y_ready, 2 * b + c + 1)
                    if not first:
                        pe.wait_ge(y_scaled, 2 * b + c - 1)
                    for k in range(KD):
                        last = nc.tensor.transpose(y_bank[c][:, k * P:(k + 1) * P], y[:, c, k * P:(k + 1) * P], ident[:])
                    last.then_inc(y_ps, 1)
                if not final:
                    pv(b + 1)
                for c in range(CB):
                    pe.wait_ge(z_ready, 2 * b + c + 1)
                    if not first:
                        pe.wait_ge(x_added, 2 * b + c - 1)
                    for k in range(KD):
                        last = nc.tensor.matmul(p_bank[c][:], zt[:, c, k * P:(k + 1) * P], wo[:, k, :],
                                                start=k == 0, stop=k == KD - 1)
                    last.then_inc(p_ps, 1)

            pv(0)
            pe.wait_ge(wo_in, 48)
            batch(0, first=True)
            with pe.Fori(1, B - 1) as b:
                batch(b)
            batch(B - 1, final=True)

        @block.scalar
        def _(act):
            def batch(b):
                for c in range(CB):
                    act.wait_ge(y_ps, 2 * b + c + 1)
                    for k in range(KD):
                        last = nc.scalar.activation(zt[:, c, k * P:(k + 1) * P], y_bank[c][:, k * P:(k + 1) * P],
                                                    ACT.Identity, bias=bet[:, k:k + 1], scale=gam[:, k:k + 1])
                    last.then_inc(y_scaled, 1)

            act.wait_ge(wo_in, 48)
            batch(0)

            def rest(lo, hi):
                with act.Fori(lo, hi) as b:
                    act.wait_ge(p_ps, 2 * b)
                    batch(b)

            rest(1, QUIET)
            abs_sum(act, 1, raw)
            abs_sum(act, 2, raw2)
            rest(QUIET, B)

        @block.vector
        def _(dve):
            steps = Steps(dve, dve_step)

            def normalise(b):
                dve.wait_ge(o_ps, 2 * b + CB)
                norm.stats(steps, [o_bank[c][:] for c in range(CB)], GN_EPS)
                dve.wait_ge(norm.rstd_ready, b + 1)
                for c in range(CB):
                    nc.vector.tensor_scalar(y[:, c, :], o_bank[c][:], norm.mv[:, c, 0:1], norm.rstd[:, c:c + 1],
                                            ALU.subtract, ALU.mult).then_inc(y_ready, 1)

            def gate(b):
                for c in range(CB):
                    dve.wait_ge(y_scaled, 2 * b + c + 1)
                    z = zt[:, c, :].rearrange("p (k n) -> p k n", n=P)
                    nc.vector.tensor_tensor(z, z, wt[:, :, ds(S * b + c * P, P)], ALU.mult).then_inc(z_ready, 1)

            def residual(b):
                for c in range(CB):
                    dve.wait_ge(p_ps, 2 * b + c + 1)
                    nc.vector.tensor_tensor(x[:, ds(CB * b + c, 1), :], x[:, ds(CB * b + c, 1), :], p_bank[c][:],
                                            ALU.add).then_inc(x_added, 1)

            def batch(b):
                gate(b)
                normalise(b + 1)
                residual(b)

            normalise(0)
            with steps.loop(0, QUIET, 4) as b:
                batch(b)
            dve.wait_ge(mean_ready, 3)
            part = KF * D // (B - 1 - QUIET)
            with steps.loop(QUIET, B - 1, 10) as b:
                batch(b)
                ternary(steps, [(1, raw), (2, raw2)], (b - QUIET) * part, part)
            gate(B - 1)
            residual(B - 1)


def bit_ffn(nc, st, sem, sbuf, psum, eo_d, x, ident, powers, tern, w_mean):
    w1t = sbuf(st, "w1t", [P, KD, F0], BF16)
    w3t = sbuf(st, "w3t", [P, KD, F0], BF16)
    w2t = sbuf(st, "w2t", [P, KF, D], BF16)
    identb = sbuf(st, "identb", [P, P], BF16)
    xn = sbuf(st, "f_xn", [P, D])
    big = sbuf(st, "f_big", [P, 1])
    deq = sbuf(st, "f_deq", [P, 2])
    scl = sbuf(st, "f_scl", [P, 1])
    d13 = sbuf(st, "f_d13", [P, 2, 2])
    xq = sbuf(st, "f_xq", [P, D], BF16)
    xqt = sbuf(st, "f_xqt", [P, KD, P], BF16)
    sil = sbuf(st, "f_silu", [P, F0])
    hid = sbuf(st, "f_hid", [P, F0])
    hq = sbuf(st, "f_hq", [P, F0], BF16)
    hqt = sbuf(st, "f_hqt", [P, KF, P], BF16)
    hbig = sbuf(st, "f_hbig", [P, 1])
    hscl = sbuf(st, "f_hscl", [P, 1])
    hdeq = sbuf(st, "f_hdeq", [P, 2])
    hd2 = sbuf(st, "f_hd2", [P, 2])
    g_bank = psum(st, "g_bank", [P, 3, 512])
    u_bank = psum(st, "u_bank", [P, 3, 512])
    ta = psum(st, "turn_a", [P, 512])
    tb = psum(st, "turn_b", [P, 512])
    tab, tbb = (t[:].bitcast(BF16).rearrange("p (k n) -> p k n", n=P) for t in (ta, tb))
    KA = 8
    norm = Norm(nc, st, sem, sbuf, "ln1", 1)
    dve_step, act_step = sem("f_dve_step"), sem("f_act_step")
    idb_ready = sem("f_identb")
    wt_ps = sem("f_wt_ps")
    wt_sb = [sem("f_wt_sb_even"), sem("f_wt_sb_odd")]
    xq_ready, xqt_ps, xqt_sb, g_ps, u_ps, sil_ready, u_used, hq_ready, hta_ps, htb_ps, hta_sb, htb_sb, o_ps, x_added = (
        sem("f_" + n) for n in ("xq_ready", "xqt_ps", "xqt_sb", "g_ps", "u_ps", "sil_ready", "u_used", "hq_ready",
                                "hta_ps", "htb_ps", "hta_sb", "htb_sb", "o_ps", "x_added"))
    jobs = []
    for src, dst in (("w1", w1t), ("w3", w3t)):
        for k in range(KD):
            for j0 in range(0, KF, KA):
                n = min(KA, KF - j0)
                jobs.append(([tern[src][:, (j0 + j) * D + k * P:(j0 + j) * D + (k + 1) * P] for j in range(n)],
                             dst[:, k, j0 * P:(j0 + n) * P].rearrange("p (j n) -> p j n", n=P)))
    for f0 in range(0, KF, 2):
        n = min(2, KF - f0)
        jobs.append(([tern["w2"][:, m * F0 + (f0 + j) * P:m * F0 + (f0 + j + 1) * P] for j in range(n) for m in range(KD)],
                     w2t[:, f0:f0 + n, :].rearrange("p f (m n) -> p (f m) n", n=P)))
    zero_row = sbuf(st, "f_zero_row", [P, D])
    zero_ready, zeroed = sem("f_zero_ready"), sem("f_zeroed")
    FILLS = 8
    block = st.enter_context(nc.Block())

    @block.sync
    def _(sp):
        sp.wait_ge(zero_ready, 1)
        per = NE * CAP // FILLS
        for n in range(FILLS):
            sp.dma_start(eo_d[n * per:(n + 1) * per, :].rearrange("(p q) d -> p q d", p=P),
                         zero_row[:].unsqueeze(1).to_broadcast([P, per // P, D])).then_inc(zeroed, 16)
        sp.wait_ge(zeroed, 16 * FILLS)

    @block.gpsimd
    def _(pool):
        nc.gpsimd.memset(zero_row[:], 0.0).then_inc(zero_ready, 1)
        norm.power(pool, powers, 1, 1)
        with pool.Fori(1, NT) as t:
            norm.power(pool, powers, t + 1, 1)

    @block.tensor
    def _(pe):
        pe.wait_ge(idb_ready, 1)
        for n, (pieces, _) in enumerate(jobs):
            if n >= 2:
                pe.wait_ge(wt_sb[n % 2], n // 2)
            for j, piece in enumerate(pieces):
                last = nc.tensor.transpose((tab, tbb)[n % 2][:, j, :], piece, identb[:])
            last.then_inc(wt_ps, 1)
        for e in range(2):
            pe.wait_ge(wt_sb[e], (len(jobs) + 1 - e) // 2)

        def turn_x(t):
            pe.wait_ge(xq_ready, t + 1)
            for k in range(KD):
                last = nc.tensor.transpose(tbb[:, k, :], xq[:, k * P:(k + 1) * P], identb[:])
            last.then_inc(xqt_ps, 1)

        def up(t, first=False):
            pe.wait_ge(xqt_sb, t + 1)
            for bank, wgt, done, freed in ((g_bank, w1t, g_ps, sil_ready), (u_bank, w3t, u_ps, u_used)):
                if not first:
                    pe.wait_ge(freed, t)
                for n in range(3):
                    lo, hi = 512 * n, min(512 * n + 512, F0)
                    for k in range(KD):
                        last = nc.tensor.matmul(bank[:, n, 0:hi - lo], xqt[:, k, :], wgt[:, k, lo:hi],
                                                start=k == 0, stop=k == KD - 1)
                last.then_inc(done, 1)

        def down(t):
            pe.wait_ge(hq_ready, t + 1)
            for k in range(KF):
                last = nc.tensor.transpose(tab[:, k, :] if k < KA else tbb[:, k - KA, :], hq[:, k * P:(k + 1) * P], identb[:])
                if k == KA - 1:
                    last.then_inc(hta_ps, 1)
            last.then_inc(htb_ps, 1)
            pe.wait_ge(hta_sb, t + 1)
            pe.wait_ge(htb_sb, t + 1)
            for k in range(KF):
                last = nc.tensor.matmul(ta[:], hqt[:, k, :], w2t[:, k, :], start=k == 0, stop=k == KF - 1)
            last.then_inc(o_ps, 1)

        turn_x(0)
        up(0, first=True)
        turn_x(1)
        up(1)
        down(0)
        turn_x(2)
        with pe.Fori(2, NT - 1) as t:
            up(t)
            pe.wait_ge(x_added, t - 1)
            down(t - 1)
            turn_x(t + 1)
        up(NT - 1)
        for t in (NT - 2, NT - 1):
            pe.wait_ge(x_added, t)
            down(t)

    @block.scalar
    def _(act):
        for n, (pieces, dst) in enumerate(jobs):
            if n % 2:
                act.wait_ge(wt_ps, n + 1)
                nc.scalar.copy(dst, (tab, tbb)[n % 2][:, 0:len(pieces), :]).then_inc(wt_sb[n % 2], 1)

        def copy_x(t):
            act.wait_ge(xqt_ps, t + 1)
            nc.scalar.copy(xqt[:], tbb[:, 0:KD, :]).then_inc(xqt_sb, 1)

        def silu(t, d):
            act.wait_ge(g_ps, t + 1)
            if not isinstance(t, int) or t:
                act.wait_ge(u_used, t)
            nc.scalar.activation(sil[:], g_bank[:].rearrange("p n f -> p (n f)")[:, 0:F0], ACT.Silu,
                                 scale=d).then_inc(sil_ready, 1)

        def copy_h(t):
            act.wait_ge(hta_ps, t + 1)
            nc.scalar.copy(hqt[:, 0:KA, :], tab[:, 0:KA, :]).then_inc(hta_sb, 1)
            act.wait_ge(htb_ps, t + 1)
            nc.scalar.copy(hqt[:, KA:KF, :], tbb[:, 0:KF - KA, :]).then_inc(htb_sb, 1)

        copy_x(0)
        silu(0, d13[:, 0, 0:1])
        copy_x(1)
        with act.Fori(0, NT // 2 - 1) as i:
            for u in range(2):
                t = 2 * i + 1 + u
                silu(t, d13[:, (1 + u) % 2, 0:1])
                copy_h(t - 1)
                copy_x(t + 1)
        silu(NT - 1, d13[:, (NT - 1) % 2, 0:1])
        copy_h(NT - 2)
        copy_h(NT - 1)

    @block.vector
    def _(dve):
        steps = Steps(dve, dve_step)
        nc.vector.tensor_copy(identb[:], ident[:]).then_inc(idb_ready, 1)
        for n, (pieces, dst) in enumerate(jobs):
            if n % 2 == 0:
                dve.wait_ge(wt_ps, n + 1)
                nc.vector.tensor_copy(dst, (tab, tbb)[n % 2][:, 0:len(pieces), :]).then_inc(wt_sb[n % 2], 1)

        def quantise(src, bigs, scale, step, products, dst, done):
            steps.then(nc.vector.tensor_reduce(bigs[:], src[:], AX.X, ALU.max, apply_absolute_value=True))
            steps.then(nc.vector.tensor_scalar(bigs[:], bigs[:], Q_EPS, None, ALU.max))
            steps.did(nc.vector.tensor_scalar(step, bigs[:], 1.0 / 127.0, None, ALU.mult))
            steps.then(nc.vector.reciprocal(scale[:], bigs[:]))
            steps.did(nc.vector.tensor_scalar(scale[:], scale[:], 127.0, None, ALU.mult))
            for dst_p, mean in products:
                steps.did(nc.vector.tensor_scalar(dst_p, step, mean, None, ALU.mult))
            steps.settle()
            steps.then(nc.vector.tensor_scalar(src[:], src[:], scale[:], ROUND, ALU.mult, ALU.add))
            nc.vector.tensor_scalar(dst[:], src[:], ROUND, 127.0, ALU.subtract, ALU.min).then_inc(done, 1)

        def prepare(t, par):
            row = x[:, ds(t, 1), :]
            norm.stats(steps, [row], LN_EPS)
            dve.wait_ge(norm.rstd_ready, t + 1)
            steps.then(nc.vector.tensor_scalar(xn[:], row, norm.mv[:, 0, 0:1], norm.rstd[:, 0:1],
                                               ALU.subtract, ALU.mult))
            if not isinstance(t, int) or t:
                dve.wait_ge(xqt_ps, t)
            quantise(xn, big, scl, deq[:, par:par + 1],
                     [(d13[:, par, 0:1], w_mean[:, 0:1]), (d13[:, par, 1:2], w_mean[:, 1:2])], xq, xq_ready)

        def hidden(t, par):
            dve.wait_ge(u_ps, t + 1)
            dve.wait_ge(sil_ready, t + 1)
            if not isinstance(t, int) or t:
                dve.wait_ge(hq_ready, t)
            nc.vector.scalar_tensor_tensor(hid[:], u_bank[:].rearrange("p n f -> p (n f)")[:, 0:F0],
                                           d13[:, par, 1:2], sil[:], ALU.mult, ALU.mult).then_inc(u_used, 1)
            dve.wait_ge(u_used, t + 1)
            if not isinstance(t, int) or t:
                dve.wait_ge(htb_ps, t)
            quantise(hid, hbig, hscl, hdeq[:, par:par + 1], [(hd2[:, par:par + 1], w_mean[:, 2:3])], hq, hq_ready)

        def residual(t, par):
            dve.wait_ge(o_ps, t + 1)
            row = x[:, ds(t, 1), :]
            nc.vector.scalar_tensor_tensor(row, ta[:], hd2[:, par:par + 1], row, ALU.mult, ALU.add).then_inc(x_added, 1)

        prepare(0, 0)
        prepare(1, 1)
        hidden(0, 0)
        with steps.loop(0, NT // 2 - 1, 36) as i:
            for u in range(2):
                t = 2 * i + 1 + u
                prepare(t + 1, u)
                hidden(t, 1 - u)
                residual(t - 1, u)
        hidden(NT - 1, 1)
        residual(NT - 2, 0)
        residual(NT - 1, 1)


def mlstm(nc, st, sem, sbuf, psum, scratch_dram, a, x, ctx_rows, ident, powers):
    BH = B * NH
    W = DH + 1
    gate_d = scratch_dram("gate_d", [2, B, NH, S])
    negm_d = scratch_dram("negm_d", [BH, S])
    qt_d = scratch_dram("qt_d", [B, P, KD * S])
    kt_d = scratch_dram("kt_d", [B, P, KD * S])
    g_t = sbuf(st, "g_t", [P, CB, BH])
    floor_t = sbuf(st, "floor_t", [P, CB, BH])

    with ExitStack() as sa:
        wraw = sbuf(sa, "m_wraw", [P, 3 * KD, 2 * NH])
        bias = sbuf(sa, "m_bias", [2 * NH, 1])
        cx = sbuf(sa, "m_cx", [P, 2, CB, D])
        xn = sbuf(sa, "m_xn", [P, CB, D])
        qt = sbuf(sa, "m_qt", [P, 2, KD, S])
        kt = sbuf(sa, "m_kt", [P, 2, KD, S])
        gts = sbuf(sa, "m_gts", [2 * NH, 2, S])
        ring = [psum(sa, f"m_ring{i}", [P, 512]) for i in range(5)]
        norm = Norm(nc, sa, sem, sbuf, "ln2", CB)
        w_in, w_sum = sem("m_w_in"), sem("m_w_sum")
        c_in = [sem(f"m_c_in{u}") for u in range(2)]
        stored = [sem(f"m_stored{u}") for u in range(2)]
        dve_step, xn_ready, xt_ps, ct_ps, xt_sb, ct_sb, g_ps, g_sb = (
            sem("m_" + n) for n in ("dve_step", "xn_ready", "xt_ps", "ct_ps", "xt_sb", "ct_sb", "g_ps", "g_sb"))
        block = sa.enter_context(nc.Block())

        @block.sync
        def _(sp):
            for u in range(2):
                sp.dma_start(cx[:, u], ctx_rows[:, CB * u:CB * u + CB, :]).then_inc(c_in[u], 16)
            for k, n in enumerate(("Wi", "Wf")):
                sp.dma_start(wraw[:, :, k * NH:(k + 1) * NH],
                             a["L1_xattn_" + n].rearrange("(k p) n -> p k n", p=P)).then_inc(w_in, 16)
            for k, n in enumerate(("bi", "bf")):
                sp.dma_start(bias[k * NH:(k + 1) * NH, :],
                             a["L1_xattn_" + n].rearrange("(p o) -> p o", o=1)).then_inc(w_in, 16)

            def store(b, u):
                sp.wait_ge(xt_sb, 2 * b + 2)
                sp.dma_start(qt_d[ds(b, 1)].rearrange("b p n -> p (b n)"),
                             qt[:, u].rearrange("p k n -> p (k n)")).then_inc(stored[u], 16)
                sp.wait_ge(ct_sb, 2 * b + 2)
                sp.dma_start(kt_d[ds(b, 1)].rearrange("b p n -> p (b n)"),
                             kt[:, u].rearrange("p k n -> p (k n)")).then_inc(stored[u], 16)
                sp.wait_ge(g_sb, b + 1)
                for k in range(2):
                    sp.dma_start(gate_d[k, ds(b, 1)].rearrange("b h s -> (b h) s"),
                                 gts[k * NH:(k + 1) * NH, u, :]).then_inc(stored[u], 16)

            with sp.Fori(0, B // 2 - 1) as i:
                for u in range(2):
                    sp.wait_ge(ct_ps, 4 * i + 2 * u + 2)
                    sp.dma_start(cx[:, u], ctx_rows[:, ds(2 * CB * i + CB * (2 + u), CB), :]).then_inc(c_in[u], 16)
                    store(2 * i + u, u)
            for u in range(2):
                store(B - 2 + u, u)
            for u in range(2):
                sp.wait_ge(stored[u], 64 * (B // 2))

        @block.gpsimd
        def _(pool):
            with pool.Fori(0, B) as b:
                norm.power(pool, powers, b + 1, CB)

        @block.vector
        def _(dve):
            steps = Steps(dve, dve_step)
            dve.wait_ge(w_in, 64)
            nc.vector.tensor_tensor(wraw[:, KD:2 * KD, :], wraw[:, KD:2 * KD, :], wraw[:, 2 * KD:3 * KD, :],
                                    ALU.add).then_inc(w_sum, 1)

            def normalise(b):
                norm.stats(steps, [x[:, ds(CB * b + c, 1), :] for c in range(CB)], LN_EPS)
                dve.wait_ge(norm.rstd_ready, b + 1)
                if not isinstance(b, int) or b:
                    dve.wait_ge(xt_ps, 2 * b)
                for c in range(CB):
                    nc.vector.tensor_scalar(xn[:, c, :], x[:, ds(CB * b + c, 1), :], norm.mv[:, c, 0:1],
                                            norm.rstd[:, c:c + 1], ALU.subtract, ALU.mult).then_inc(xn_ready, 1)

            def copies(b, u, i):
                if not isinstance(i, int) or i:
                    dve.wait_ge(stored[u], 64 * i)
                for c in range(CB):
                    dve.wait_ge(ct_ps, 2 * b + c + 1)
                    nc.vector.tensor_copy(kt[:, u, :, c * P:(c + 1) * P],
                                          ring[2 * c + 1][:].rearrange("p (k n) -> p k n", n=P)).then_inc(ct_sb, 1)

            normalise(0)
            for u in range(2):
                copies(u, u, 0)
                normalise(u + 1)
            with steps.loop(1, B // 2 - 1, 8) as i:
                for u in range(2):
                    copies(2 * i + u, u, i)
                    normalise(2 * i + u + 1)
            copies(B - 2, 0, B // 2 - 1)
            normalise(B - 1)
            copies(B - 1, 1, B // 2 - 1)

        @block.scalar
        def _(act):
            def batch(b, u, i):
                if not isinstance(i, int) or i:
                    act.wait_ge(stored[u], 64 * i)
                for c in range(CB):
                    act.wait_ge(xt_ps, 2 * b + c + 1)
                    nc.scalar.copy(qt[:, u, :, c * P:(c + 1) * P],
                                   ring[2 * c][:].rearrange("p (k n) -> p k n", n=P)).then_inc(xt_sb, 1)
                act.wait_ge(g_ps, b + 1)
                nc.scalar.activation(gts[:, u, :], ring[4][0:2 * NH, 0:S], ACT.Identity, bias=bias[:]).then_inc(g_sb, 1)

            act.wait_ge(w_in, 64)
            for u in range(2):
                batch(u, u, 0)
            with act.Fori(1, B // 2) as i:
                for u in range(2):
                    batch(2 * i + u, u, i)

        @block.tensor
        def _(pe):
            def batch(b, u, i, first=False):
                for c in range(CB):
                    pe.wait_ge(xn_ready, 2 * b + c + 1)
                    if not first:
                        pe.wait_ge(xt_sb, 2 * b + c - 1)
                    for k in range(KD):
                        last = nc.tensor.transpose(ring[2 * c][:, k * P:(k + 1) * P], xn[:, c, k * P:(k + 1) * P], ident[:])
                    last.then_inc(xt_ps, 1)
                    if c == 0:
                        pe.wait_ge(c_in[u], 16 * i + 16)
                    if not first:
                        pe.wait_ge(ct_sb, 2 * b + c - 1)
                    for k in range(KD):
                        last = nc.tensor.transpose(ring[2 * c + 1][:, k * P:(k + 1) * P], cx[:, u, c, k * P:(k + 1) * P], ident[:])
                    last.then_inc(ct_ps, 1)
                pe.wait_ge(xt_sb, 2 * b + 2)
                pe.wait_ge(ct_sb, 2 * b + 2)
                if not first:
                    pe.wait_ge(g_sb, b)
                for k in range(2 * KD):
                    last = nc.tensor.matmul(ring[4][0:2 * NH, 0:S], wraw[:, k, :],
                                            qt[:, u, k, :] if k < KD else kt[:, u, k - KD, :],
                                            start=k == 0, stop=k == 2 * KD - 1)
                last.then_inc(g_ps, 1)

            pe.wait_ge(w_sum, 1)
            batch(0, 0, 0, first=True)
            batch(1, 1, 0)
            with pe.Fori(1, B // 2) as i:
                for u in range(2):
                    batch(2 * i + u, u, i)

    with ExitStack() as sg:
        names = ("ig", "fg", "soft", "cum", "g", "m", "negm", "fl", "zero")
        ig, fg, soft, cum, g, m, negm, fl, zero = (sbuf(sg, "d_" + n, [BH, S]) for n in names)
        tg = psum(sg, "d_tg", [P, 512])
        i_in, soft_ready, fl_in, dve_step, act_step, g_ready, fl_ready, t_ps, t_sb, negm_ready, negm_out = (
            sem("d_" + n) for n in ("i_in", "soft_ready", "fl_in", "dve_step", "act_step", "g_ready", "fl_ready",
                                    "t_ps", "t_sb", "negm_ready", "negm_out"))
        block = sg.enter_context(nc.Block())

        @block.sync
        def _(sp):
            sp.dma_start(fg[:], gate_d[1].rearrange("b h s -> (b h) s")).then_inc(i_in, 16)
            sp.dma_start(ig[:], gate_d[0].rearrange("b h s -> (b h) s")).then_inc(i_in, 16)
            sp.wait_ge(negm_ready, 1)
            sp.dma_start(negm_d, negm[:]).then_inc(negm_out, 16)
            sp.wait_ge(negm_out, 16)

        @block.scalar
        def _(act):
            steps = Steps(act, act_step)
            act.wait_ge(i_in, 32)
            steps.then(nc.scalar.activation(soft[:], fg[:], ACT.Abs))
            steps.then(nc.scalar.activation(soft[:], soft[:], ACT.Exp, scale=-1.0))
            nc.scalar.activation(soft[:], soft[:], ACT.Ln, bias=1.0).then_inc(soft_ready, 1)
            act.wait_ge(fl_in, 1)
            nc.scalar.activation(fl[:], fl[:], ACT.Exp, scale=-1.0).then_inc(fl_ready, 1)

        @block.vector
        def _(dve):
            steps = Steps(dve, dve_step)
            steps.did(nc.vector.memset(zero[:], 0.0))
            dve.wait_ge(soft_ready, 1)
            steps.then(nc.vector.scalar_tensor_tensor(soft[:], fg[:], 0.0, soft[:], ALU.min, ALU.subtract))
            steps.then(nc.vector.tensor_tensor_scan(cum[:], soft[:], zero[:], 0.0, ALU.add, ALU.add))
            nc.vector.tensor_tensor(g[:], ig[:], cum[:], ALU.subtract).then_inc(g_ready, 1)
            dve.wait_ge(g_ready, 1)
            steps.then(nc.vector.tensor_tensor_scan(m[:], g[:], g[:], -3e38, ALU.max, ALU.max))
            nc.vector.tensor_scalar(negm[:], m[:], -1.0, None, ALU.mult).then_inc(negm_ready, 1)
            nc.vector.tensor_tensor(fl[:], cum[:], m[:], ALU.add).then_inc(fl_in, 1)
            dve.wait_ge(t_ps, 2)
            nc.vector.tensor_copy(g_t[:], tg[:, 0:2 * P].rearrange("p (c n) -> p c n", n=P)).then_inc(t_sb, 1)
            nc.vector.tensor_copy(floor_t[:], tg[:, 2 * P:4 * P].rearrange("p (c n) -> p c n", n=P)).then_inc(t_sb, 1)

        @block.tensor
        def _(pe):
            for n, (src, ready) in enumerate(((g, g_ready), (fl, fl_ready))):
                pe.wait_ge(ready, 1)
                for c in range(CB):
                    last = nc.tensor.transpose(tg[:, (2 * n + c) * P:(2 * n + c + 1) * P], src[:, c * P:(c + 1) * P], ident[:])
                last.then_inc(t_ps, 1)

    with ExitStack() as sh:
        lns = sbuf(sh, "ln_scale", [P, D])
        future = sbuf(sh, "future", [P, P])
        qt = sbuf(sh, "h_qt", [P, 2, KD, S])
        kt = sbuf(sh, "h_kt", [P, 2, KD, S])
        cx = sbuf(sh, "h_cx", [P, 2, CB, D])
        nm = sbuf(sh, "h_negm", [P, 2, NH, 3, P])
        gst = sbuf(sh, "h_g", [P, 2, CB, NH])
        va = sbuf(sh, "h_v", [P, 2, CB, NH, W])
        dm = sbuf(sh, "h_d", [P, 2, HG, 3, P])
        cm = sbuf(sh, "h_c", [P, 2, HG, 3 * P])
        hr = sbuf(sh, "h_raw", [P, 2, CB, NH, W])
        hb = sbuf(sh, "h_b", [P, 2, CB, NH, DH])
        sq = sbuf(sh, "h_sq", [P, CB, NH, DH])
        nrm = sbuf(sh, "h_nrm", [P, CB, NH])
        mu = sbuf(sh, "h_mu", [P, CB, NH])
        var = sbuf(sh, "h_var", [P, CB, NH])
        rs = sbuf(sh, "h_rs", [P, CB, NH])
        qk = psum(sh, "h_qk", [P, HG, 512])
        pvb = [psum(sh, f"h_pv{i}", [P, CB, HG, W]) for i in range(2)]
        cst_in = sem("h_cst_in")
        ld = [sem(f"h_ld{u}") for u in range(2)]
        (fills, dve_step, g_staged, v_staged, masked, d_ready, qk_ps, c_ready, pv_ps, h_sb, h_read, hc_in, hc_ready,
         sq_ready, var_ready, rs_ready, pool_step, x_added) = (
            sem("h_" + n) for n in ("fills", "dve_step", "g_staged", "v_staged", "masked", "d_ready", "qk_ps",
                                    "c_ready", "pv_ps", "h_sb", "h_read", "hc_in", "hc_ready", "sq_ready",
                                    "var_ready", "rs_ready", "pool_step", "x_added"))
        block = sh.enter_context(nc.Block())
        LOADS = 5 * 16
        OPEN = 2
        HH = HG // 2

        def after(eng, semaphore, value):
            if not isinstance(value, int) or value > 0:
                eng.wait_ge(semaphore, value)

        def batches(eng, first, middle, last):
            first(0, 0, 0)
            with eng(0, B // 2 - 1) as i:
                middle(2 * i + 1, i, 1)
                middle(2 * i + 2, i + 1, 0)
            last(B - 1, B // 2 - 1, 1)

        @block.sync
        def _(sp):
            sp.dma_start(lns[:], a["L1_xattn_ln_scale"].rearrange("(o d) -> o d", o=1).partition_broadcast(P)
                         .rearrange("p o d -> p (o d)")).then_inc(cst_in, 16)
            sp.dma_start(future[:], a["consts"][:, C_FUT:C_FUT + P]).then_inc(cst_in, 16)

            def load(b, u):
                sp.dma_start(qt[:, u].rearrange("p k n -> p (k n)"),
                             qt_d[ds(b, 1)].rearrange("b p n -> p (b n)")).then_inc(ld[u], 16)
                sp.dma_start(kt[:, u].rearrange("p k n -> p (k n)"),
                             kt_d[ds(b, 1)].rearrange("b p n -> p (b n)")).then_inc(ld[u], 16)
                for half in range(2):
                    sp.dma_start(nm[:, u, :, half, :],
                                 negm_d[ds(b * NH, NH), half * P:(half + 1) * P].rearrange("(o h) s -> o h s", o=1)
                                 .partition_broadcast(P).rearrange("p o h s -> p (o h) s")).then_inc(ld[u], 16)
                sp.dma_start(cx[:, u], ctx_rows[:, ds(CB * b, CB), :]).then_inc(ld[u], 16)

            for u in range(2):
                load(u, u)
            with sp.Fori(0, B // 2 - 1) as i:
                for u in range(2):
                    sp.wait_ge(pv_ps, NG * (2 * i + u) + NG)
                    load(2 * i + 2 + u, u)

        @block.gpsimd
        def _(pool):
            steps = Steps(pool, pool_step)
            nc.gpsimd.memset(va[:], 1.0).then_inc(fills, 1)
            pool.wait_ge(cst_in, 32)

            def centre(b, u):
                pool.wait_ge(hc_in, b + 1)
                nc.gpsimd.tensor_tensor(hb[:, u], hb[:, u], mu[:].unsqueeze(3).to_broadcast([P, CB, NH, DH]),
                                        ALU.subtract).then_inc(hc_ready, 1)

            def finish(b, u):
                h = hb[:, u]
                flat = h.rearrange("p c h e -> p c (h e)")
                pool.wait_ge(hc_ready, OPEN + b + 1)
                pool.wait_ge(sq_ready, b + 1)
                for c in range(CB):
                    steps.did(nc.gpsimd.tensor_tensor(flat[:, c], flat[:, c], lns[:], ALU.mult))
                pool.wait_ge(var_ready, OPEN + b + 1)
                nc.gpsimd.tensor_tensor(rs[:].rearrange("p c h -> p (c h)"), var[:].rearrange("p c h -> p (c h)"),
                                        powers[:, 0:1].to_broadcast([P, CB * NH]), ALU.pow).then_inc(rs_ready, 1)
                pool.wait_ge(rs_ready, OPEN + b + 1)
                steps.settle()
                steps.then(nc.gpsimd.tensor_tensor(h, h, rs[:].unsqueeze(3).to_broadcast([P, CB, NH, DH]), ALU.mult))
                nc.gpsimd.tensor_tensor(x[:, ds(CB * b, CB), :], x[:, ds(CB * b, CB), :], flat, ALU.add).then_inc(x_added, 1)

            for opened in (hc_ready, rs_ready, x_added):
                pool.sem_inc(opened, OPEN)
            with steps.loop(0, B // 2, 6) as i:
                for u in range(2):
                    centre(2 * i + u, u)
                    finish(2 * i + u, u)

        @block.scalar
        def _(act):
            def stage_g(b, m, u):
                act.wait_ge(ld[u], LOADS * m + LOADS)
                after(act, c_ready, 2 * NG * (b - 1))
                nc.scalar.copy(gst[:, u], g_t[:, :, ds(b * NH, NH)]).then_inc(g_staged, 1)

            def stage_v(b, u):
                nc.scalar.copy(va[:, u, :, :, 0:DH], cx[:, u].rearrange("p c (h e) -> p c h e", e=DH)).then_inc(v_staged, 1)

            def decays(b, k, u):
                n = NG * b + k
                if k == 0:
                    act.wait_ge(g_staged, b + 1)
                act.wait_ge(masked, n + 1)
                after(act, c_ready, 2 * (n - 1))
                for j in range(HG):
                    h = HG * k + j
                    nc.scalar.activation(dm[:, k % 2, j, 0:2, :], nm[:, u, h, 0:2, :], ACT.Exp, bias=gst[:, u, 0, h:h + 1])
                    last = nc.scalar.activation(dm[:, k % 2, j, 2, :], nm[:, u, h, 2, :], ACT.Exp, bias=gst[:, u, 1, h:h + 1])
                last.then_inc(d_ready, 1)

            def take(b, k, u):
                if k == 0:
                    act.wait_ge(h_read, OPEN + b - 1)
                act.wait_ge(pv_ps, NG * b + k + 1)
                nc.scalar.copy(hr[:, u, :, HG * k:HG * (k + 1), :], pvb[k % 2][:]).then_inc(h_sb, 1)

            def square(b, u):
                act.wait_ge(hc_ready, OPEN + b + 1)
                act.wait_ge(var_ready, OPEN + b)
                nc.scalar.activation(sq[:], hb[:, u], ACT.Square).then_inc(sq_ready, 1)

            def batch(b, m, u, first=False, final=False):
                for k in range(NG):
                    if k < NG - 1:
                        decays(b, k + 1, u)
                    elif not final:
                        stage_g(b + 1, m + u, 1 - u)
                        decays(b + 1, 0, 1 - u)
                    if k:
                        take(b, k - 1, u)
                    elif not first:
                        take(b - 1, NG - 1, 1 - u)
                    if k == 1 and not first:
                        square(b - 1, 1 - u)
                if not final:
                    stage_v(b + 1, 1 - u)

            act.wait_ge(fills, 1)
            stage_g(0, 0, 0)
            stage_v(0, 0)
            decays(0, 0, 0)
            batches(act.Fori, lambda *v: batch(*v, first=True), batch, lambda *v: batch(*v, final=True))
            take(B - 1, NG - 1, 1)
            square(B - 1, 1)

        @block.tensor
        def _(pe):
            def scores(b, k, u):
                n = NG * b + k
                for j in range(HG):
                    if j % HH == 0:
                        after(pe, c_ready, 2 * n - 1 + j // HH)
                    r = slice(DH * j, DH * (j + 1))
                    nc.tensor.matmul(qk[:, j, 0:S], kt[r, u, k, 0:P], qt[r, u, k, :], start=True, stop=True)
                    last = nc.tensor.matmul(qk[:, j, S:S + P], kt[r, u, k, P:S], qt[r, u, k, P:S], start=True, stop=True)
                    if j % HH == HH - 1:
                        last.then_inc(qk_ps, 1)

            def values(b, k, u):
                n = NG * b + k
                pe.wait_ge(c_ready, 2 * n + 2)
                pe.wait_ge(v_staged, b + 1)
                after(pe, h_sb, n - 1)
                for j in range(HG):
                    h = HG * k + j
                    c = cm[:, k % 2, j, :]
                    pv = pvb[k % 2]
                    nc.tensor.matmul(pv[:, 0, j, :], c[:, 0:P], va[:, u, 0, h, :], start=True, stop=True)
                    nc.tensor.matmul(pv[:, 1, j, :], c[:, P:2 * P], va[:, u, 0, h, :], start=True, stop=False)
                    last = nc.tensor.matmul(pv[:, 1, j, :], c[:, 2 * P:3 * P], va[:, u, 1, h, :], start=False, stop=True)
                last.then_inc(pv_ps, 1)

            def batch(b, m, u, first=False):
                pe.wait_ge(ld[u], LOADS * m + LOADS)
                for k in range(NG):
                    scores(b, k, u)
                    if k:
                        values(b, k - 1, u)
                    elif not first:
                        values(b - 1, NG - 1, 1 - u)

            batches(pe.Fori, lambda *v: batch(*v, first=True), batch, batch)
            values(B - 1, NG - 1, 1)

        @block.vector
        def _(dve):
            steps = Steps(dve, dve_step)
            dve.wait_ge(cst_in, 32)

            def mask(m, k, u):
                heads = slice(HG * k, HG * (k + 1))
                dve.wait_ge(ld[u], LOADS * m + LOADS)
                nc.vector.tensor_tensor(nm[:, u, heads, 0::2, :], nm[:, u, heads, 0:2, :],
                                        future[:].unsqueeze(1).unsqueeze(1).to_broadcast([P, HG, 2, P]),
                                        ALU.add).then_inc(masked, 1)

            def weigh(b, k):
                n = NG * b + k
                dve.wait_ge(d_ready, n + 1)
                after(dve, pv_ps, n - 1)
                for f in range(2):
                    heads = slice(HH * f, HH * (f + 1))
                    dve.wait_ge(qk_ps, 2 * n + f + 1)
                    nc.vector.scalar_tensor_tensor(cm[:, k % 2, heads], qk[:, heads, 0:3 * P], float(DH) ** -0.5,
                                                   dm[:, k % 2, heads].rearrange("p j c n -> p j (c n)"),
                                                   ALU.mult, ALU.mult).then_inc(c_ready, 1)

            def divide(b, u):
                dve.wait_ge(h_sb, NG * b + NG)
                steps.then(nc.vector.scalar_tensor_tensor(nrm[:], hr[:, u, :, :, DH], -1.0, hr[:, u, :, :, DH], ALU.mult, ALU.max))
                steps.then(nc.vector.tensor_tensor(nrm[:], nrm[:], floor_t[:, :, ds(b * NH, NH)], ALU.max))
                steps.then(nc.vector.tensor_scalar(nrm[:], nrm[:], M_EPS, None, ALU.add))
                steps.then(nc.vector.reciprocal(nrm[:], nrm[:]))
                dve.wait_ge(x_added, OPEN + b - 1)
                nc.vector.tensor_tensor(hb[:, u], hr[:, u, :, :, 0:DH], nrm[:].unsqueeze(3).to_broadcast([P, CB, NH, DH]),
                                        ALU.mult).then_inc(h_read, 1)
                dve.wait_ge(h_read, OPEN + b + 1)
                dve.wait_ge(hc_ready, OPEN + b)
                steps.then(nc.vector.tensor_reduce(mu[:], hb[:, u], AX.X, ALU.add))
                nc.vector.tensor_scalar(mu[:], mu[:], 1.0 / DH, None, ALU.mult).then_inc(hc_in, 1)

            def variance(b):
                dve.wait_ge(sq_ready, b + 1)
                dve.wait_ge(rs_ready, OPEN + b)
                steps.then(nc.vector.tensor_reduce(var[:], sq[:], AX.X, ALU.add))
                nc.vector.tensor_scalar(var[:], var[:], 1.0 / DH, M_EPS, ALU.mult, ALU.add).then_inc(var_ready, 1)

            def batch(b, m, u, first=False, final=False):
                for k in range(NG):
                    weigh(b, k)
                    if k < NG - 2:
                        mask(m, k + 2, u)
                    elif not final:
                        mask(m + u, k + 2 - NG, 1 - u)
                    if k == 0 and not first:
                        divide(b - 1, 1 - u)
                    if k == 2 and not first:
                        variance(b - 1)

            dve.sem_inc(h_read, OPEN)
            dve.sem_inc(var_ready, OPEN)
            mask(0, 0, 0)
            mask(0, 1, 0)
            batches(lambda lo, hi: steps.loop(lo, hi, 12), lambda *v: batch(*v, first=True), batch,
                    lambda *v: batch(*v, final=True))
            divide(B - 1, 1)
            variance(B - 1)


def experts(nc, st, sem, sbuf, psum, scratch_dram, eo_d, a, x, ident, powers, out):
    r_d = scratch_dram("r_d", [T, D])
    logits = sbuf(st, "logits", [P, NT, NE])
    route = sbuf(st, "route", [P, ROUTES], I32)
    slot = sbuf(st, "slot", [P, NT * TOPK], I32)
    wk = sbuf(st, "wk", [P, NT, TOPK])
    unit_tile = sbuf(st, "unit_tile", [P, ROUTES + 4], I32)
    last_round = sbuf(st, "last_round", [P, 1], I32)
    carry = sbuf(st, "carry", [P, 2])
    w13 = sbuf(st, "w13", [P, 2, KD, 2 * FI])
    w2 = sbuf(st, "w2", [P, 2, KI, D])
    w13_in = [sem(f"w13_in{u}") for u in range(2)]
    w2_in = [sem(f"w2_in{u}") for u in range(2)]

    def load_w13(eng, e, u):
        eng.dma_start(w13[:, u], a["L1_ffn_w13"][ds(e, 1)].rearrange("e (k p) f -> p (e k) f", p=P)).then_inc(w13_in[u], 16)

    def load_w2(eng, e, u):
        eng.dma_start(w2[:, u], a["L1_ffn_w2"][ds(e, 1)].rearrange("e (k p) f -> p (e k) f", p=P)).then_inc(w2_in[u], 16)

    with ExitStack() as sa:
        nw = sbuf(sa, "norm_w", [P, D])
        gw = sbuf(sa, "gate_w", [NE, D])
        gwt = sbuf(sa, "gate_wt", [P, KD, NE])
        sg = sbuf(sa, "sh_gate", [P, KD, FI])
        su = sbuf(sa, "sh_up", [P, KD, FI])
        sd = sbuf(sa, "sh_down", [P, KI, D])
        xl = sbuf(sa, "e_xl", [P, CB, D])
        sq = sbuf(sa, "e_sq", [P, D])
        ms = sbuf(sa, "e_ms", [P, CB])
        me = sbuf(sa, "e_me", [P, CB])
        rr = sbuf(sa, "e_rr", [P, CB])
        r = sbuf(sa, "e_r", [P, 2, CB, D])
        rt = sbuf(sa, "e_rt", [P, 2, KD, S])
        gsil = sbuf(sa, "e_gsil", [P, KI, S])
        av = sbuf(sa, "e_av", [P, 2, KI, S])
        tbank = [psum(sa, f"e_t{c}", [P, 512]) for c in range(CB)]
        lbank = psum(sa, "e_l", [P, 512])
        gbank = psum(sa, "e_g", [P, KI, S])
        ubank = psum(sa, "e_u", [P, KI, S])
        dbank = [psum(sa, f"e_d{c}", [P, D]) for c in range(CB)]
        norm = Norm(nc, sa, sem, sbuf, "ln3", CB)
        (e_in, w_in, gwt_ps, gwt_sb, dve_step, xl_ready, base_ready, ms_ready, me_ready, rr_ready, r_ready, r_free,
         r_ps, rt_sb, l_ps, l_sb, g_ps, u_ps, sil_ready, av_ready, d_ps, added) = (
            sem("e_" + n) for n in ("in", "w_in", "gwt_ps", "gwt_sb", "dve_step", "xl_ready", "base_ready", "ms_ready",
                                    "me_ready", "rr_ready", "r_ready", "r_free", "r_ps", "rt_sb", "l_ps", "l_sb",
                                    "g_ps", "u_ps", "sil_ready", "av_ready", "d_ps", "added"))
        r_out = [sem(f"e_r_out{u}") for u in range(2)]
        OPEN = 2
        block = sa.enter_context(nc.Block())

        @block.sync
        def _(sp):
            sp.dma_start(nw[:], a["L1_ffn_norm_w"].rearrange("(o d) -> o d", o=1).partition_broadcast(P)
                         .rearrange("p o d -> p (o d)")).then_inc(e_in, 16)
            sp.dma_start(gw[:], a["L1_ffn_gate_w"]).then_inc(e_in, 16)
            sp.dma_start(sg[:], a["L1_ffn_shared_gate_w"].rearrange("(k p) n -> p k n", p=P)).then_inc(w_in, 16)
            sp.dma_start(su[:], a["L1_ffn_shared_up_w"].rearrange("(k p) n -> p k n", p=P)).then_inc(w_in, 16)
            sp.dma_start(sd[:], a["L1_ffn_shared_down_w"].rearrange("(k p) n -> p k n", p=P)).then_inc(w_in, 16)
            for u in range(2):
                load_w13(sp, u, u)
                load_w2(sp, u, u)
            sp.sem_inc(r_free, OPEN)
            with sp.Fori(0, B // 2) as i:
                for u in range(2):
                    b = 2 * i + u
                    sp.wait_ge(r_ready, b + 1)
                    sp.dma_start(r_d[ds(S * b, S), :].rearrange("(c p) d -> p c d", p=P), r[:, u]).then_inc(r_out[u], 16)
                    sp.wait_ge(r_out[u], 16 * i + 16)
                    sp.sem_inc(r_free, 1)

        @block.gpsimd
        def _(pool):
            pool.sem_inc(base_ready, OPEN)
            with pool.Fori(0, B) as b:
                norm.power(pool, powers, b + 1, CB)
                pool.wait_ge(me_ready, b + 1)
                nc.gpsimd.tensor_tensor(rr[:], me[:], powers[:, 0:1].to_broadcast([P, CB]), ALU.pow).then_inc(rr_ready, 1)
                pool.wait_ge(xl_ready, b + 1)
                xb = x[:, ds(CB * b, CB), :]
                nc.gpsimd.tensor_tensor(xb, xb, xl[:], ALU.add).then_inc(base_ready, 1)

        @block.vector
        def _(dve):
            steps = Steps(dve, dve_step)
            dve.sem_inc(av_ready, OPEN)
            dve.wait_ge(gwt_ps, 1)
            nc.vector.tensor_copy(gwt[:], lbank[:, 0:KD * NE].rearrange("p (k n) -> p k n", n=NE)).then_inc(gwt_sb, 1)
            dve.wait_ge(e_in, 32)

            def prepare(b, u):
                norm.stats(steps, [x[:, ds(CB * b + c, 1), :] for c in range(CB)], LN_EPS)
                dve.wait_ge(norm.rstd_ready, b + 1)
                dve.wait_ge(base_ready, OPEN + b)
                for c in range(CB):
                    last = nc.vector.tensor_scalar(xl[:, c, :], x[:, ds(CB * b + c, 1), :], norm.mv[:, c, 0:1],
                                                   norm.rstd[:, c:c + 1], ALU.subtract, ALU.mult)
                last.then_inc(xl_ready, 1)
                dve.wait_ge(ms_ready, CB * b + CB)
                nc.vector.tensor_scalar(me[:], ms[:], 1.0 / D, M_EPS, ALU.mult, ALU.add).then_inc(me_ready, 1)
                dve.wait_ge(rr_ready, b + 1)
                dve.wait_ge(r_free, b + 1)
                dve.wait_ge(r_ps, OPEN + b - 1)
                for c in range(CB):
                    last = nc.vector.scalar_tensor_tensor(r[:, u, c, :], xl[:, c, :], rr[:, c:c + 1], nw[:], ALU.mult, ALU.mult)
                last.then_inc(r_ready, 1)

            def middle(b, u):
                dve.wait_ge(l_ps, b + 1)
                nc.vector.tensor_copy(logits[:, ds(CB * b, CB), :],
                                      lbank[:, 0:CB * NE].rearrange("p (c n) -> p c n", n=NE)).then_inc(l_sb, 1)
                dve.wait_ge(u_ps, OPEN + b + 1)
                dve.wait_ge(sil_ready, OPEN + b + 1)
                dve.wait_ge(d_ps, OPEN + b - 1)
                nc.vector.tensor_tensor(av[:, u], gsil[:], ubank[:], ALU.mult).then_inc(av_ready, 1)

            def residual(b):
                dve.wait_ge(d_ps, OPEN + b + 1)
                dve.wait_ge(base_ready, OPEN + b + 1)
                for c in range(CB):
                    xb = x[:, ds(CB * b + c, 1), :]
                    last = nc.vector.tensor_tensor(xb, xb, dbank[c][:], ALU.add)
                last.then_inc(added, 1)

            dve.sem_inc(added, 1)
            dve.sem_inc(l_sb, 1)
            prepare(0, 0)
            prepare(1, 1)
            middle(0, 0)
            with steps.loop(0, B // 2 - 1, 8) as i:
                for u in range(2):
                    b = 2 * i + 1 + u
                    prepare(b + 1, u)
                    middle(b, 1 - u)
                    residual(b - 1)
            middle(B - 1, 1)
            residual(B - 2)
            residual(B - 1)

        @block.scalar
        def _(act):
            def squares(b):
                act.wait_ge(xl_ready, b + 1)
                for c in range(CB):
                    act.wait_ge(ms_ready, CB * b + c) if not (isinstance(b, int) and b == 0 and c == 0) else None
                    nc.scalar.activation(sq[:], xl[:, c, :], ACT.Square, accum_out=ms[:, c:c + 1]).then_inc(ms_ready, 1)

            def turned(b, u):
                act.wait_ge(r_ps, OPEN + b + 1)
                act.wait_ge(u_ps, OPEN + b - 1)
                for c in range(CB):
                    last = nc.scalar.copy(rt[:, u, :, c * P:(c + 1) * P], tbank[c][:].rearrange("p (k n) -> p k n", n=P))
                last.then_inc(rt_sb, 1)

            def silu(b):
                act.wait_ge(g_ps, b + 1)
                act.wait_ge(av_ready, OPEN + b)
                nc.scalar.activation(gsil[:], gbank[:], ACT.Silu).then_inc(sil_ready, 1)

            act.sem_inc(sil_ready, OPEN)
            squares(0)
            turned(0, 0)
            squares(1)
            silu(0)
            turned(1, 1)
            with act.Fori(0, B // 2 - 1) as i:
                for u in range(2):
                    b = 2 * i + 1 + u
                    squares(b + 1)
                    silu(b)
                    turned(b + 1, u)
            silu(B - 1)

        @block.tensor
        def _(pe):
            pe.wait_ge(e_in, 32)
            for k in range(KD):
                last = nc.tensor.transpose(lbank[:, k * NE:(k + 1) * NE], gw[:, k * P:(k + 1) * P], ident[0:NE, 0:NE])
            last.then_inc(gwt_ps, 1)
            for opened in (r_ps, d_ps, u_ps):
                pe.sem_inc(opened, OPEN)
            pe.wait_ge(gwt_sb, 1)
            pe.wait_ge(w_in, 48)

            def turn(b, u):
                pe.wait_ge(r_ready, b + 1)
                for c in range(CB):
                    for k in range(KD):
                        last = nc.tensor.transpose(tbank[c][:, k * P:(k + 1) * P], r[:, u, c, k * P:(k + 1) * P], ident[:])
                last.then_inc(r_ps, 1)

            def up(b, u):
                pe.wait_ge(rt_sb, b + 1)
                pe.wait_ge(l_sb, b + 1)
                for c in range(CB):
                    for k in range(KD):
                        last = nc.tensor.matmul(lbank[:, c * NE:(c + 1) * NE], rt[:, u, k, c * P:(c + 1) * P], gwt[:, k, :],
                                                start=k == 0, stop=k == KD - 1)
                last.then_inc(l_ps, 1)
                for bank, wgt, done, freed in ((gbank, sg, g_ps, sil_ready), (ubank, su, u_ps, av_ready)):
                    pe.wait_ge(freed, OPEN + b)
                    for f in range(KI):
                        for k in range(KD):
                            last = nc.tensor.matmul(bank[:, f, :], wgt[:, k, f * P:(f + 1) * P], rt[:, u, k, :],
                                                    start=k == 0, stop=k == KD - 1)
                    last.then_inc(done, 1)

            def down(b, u):
                pe.wait_ge(av_ready, OPEN + b + 1)
                pe.wait_ge(added, b + 1)
                for c in range(CB):
                    for f in range(KI):
                        last = nc.tensor.matmul(dbank[c][:], av[:, u, f, c * P:(c + 1) * P], sd[:, f, :],
                                                start=f == 0, stop=f == KI - 1)
                last.then_inc(d_ps, 1)

            turn(0, 0)
            up(0, 0)
            turn(1, 1)
            with pe.Fori(0, B // 2 - 1) as i:
                for u in range(2):
                    b = 2 * i + 1 + u
                    up(b, 1 - u)
                    turn(b + 1, u)
                    down(b - 1, u)
            up(B - 1, 1)
            down(B - 2, 0)
            down(B - 1, 1)

    with ExitStack() as sr:
        cst = sbuf(sr, "rt_cst", [P, C_ALL - C_BEF])
        beforeb = sbuf(sr, "rt_before", [P, P], BF16)
        onesb = sbuf(sr, "rt_ones", [P, P], BF16)
        zerob = sbuf(sr, "rt_zero", [P, P], BF16)
        m8 = sbuf(sr, "rt_m8", [P, NT, 8])
        i8 = sbuf(sr, "rt_i8", [P, NT, 8], U32)
        ef = sbuf(sr, "rt_ef", [P, NT, TOPK])
        ex = sbuf(sr, "rt_ex", [P, NT, TOPK])
        es = sbuf(sr, "rt_es", [P, NT])
        oh = sbuf(sr, "rt_oh", [P, TOPK, NT, NE])
        mask = sbuf(sr, "rt_mask", [P, NT, NE])
        maskb = sbuf(sr, "rt_maskb", [P, NT * NE], BF16)
        offs = sbuf(sr, "rt_offs", [P, NT, NE])
        pos = sbuf(sr, "rt_pos", [P, NT, NE])
        prod = sbuf(sr, "rt_prod", [P, TOPK, NT, NE])
        pk = sbuf(sr, "rt_pk", [P, NT, TOPK])
        pi = sbuf(sr, "rt_pi", [P, NT, TOPK], I32)
        li = sbuf(sr, "rt_li", [P, NT, TOPK], I32)
        bi = sbuf(sr, "rt_bi", [P, NT, TOPK], I32)
        lo = sbuf(sr, "rt_lo", [P, NT * TOPK])
        hi = sbuf(sr, "rt_hi", [P, NT * TOPK])
        inb = sbuf(sr, "rt_inb", [P, NT * TOPK])
        sf = sbuf(sr, "rt_sf", [P, NT * TOPK])
        ohlo = sbuf(sr, "rt_ohlo", [P, 2, TOPK, P])
        ohhi = sbuf(sr, "rt_ohhi", [P, 2, TOPK, P])
        rank_bank = psum(sr, "rt_rank", [P, 512])
        cnt_bank = psum(sr, "rt_cnt", [P, 512])
        tab = psum(sr, "rt_tab", [P, P])
        tile_bank = psum(sr, "rt_tile", [P, P])
        tiles = sbuf(sr, "rt_tiles", [P, NE])
        tiles_i = sbuf(sr, "rt_tiles_i", [P, NE], I32)
        ends = sbuf(sr, "rt_ends", [P, NE])
        past = sbuf(sr, "rt_past", [P, NE])
        unit = sbuf(sr, "rt_unit", [P, 1])
        utile = sbuf(sr, "rt_utile", [P, 1])
        utile_w = sbuf(sr, "rt_utile_w", [P, P])
        fill = sbuf(sr, "rt_fill", [P, 4])
        bef, iota, tok = cst[:, 0:P], cst[:, P:2 * P], cst[:, 2 * P:2 * P + NT]
        cst_in, dve_step, step2, ex_in, ex_ready, mask_ready, ranked, hot_ready, hot_used, tile_ps = (
            sem("rt_" + n) for n in ("cst_in", "dve_step", "step2", "ex_in", "ex_ready", "mask_ready", "ranked",
                                     "hot_ready", "hot_used", "tile_ps"))
        fills = sem("rt_fills")
        block = sr.enter_context(nc.Block())

        @block.sync
        def _(sp):
            sp.dma_start(cst[:], a["consts"][:, C_BEF:C_ALL]).then_inc(cst_in, 16)

        @block.gpsimd
        def _(pool):
            nc.gpsimd.memset(onesb[:], 1.0).then_inc(fills, 1)
            nc.gpsimd.memset(zerob[:], 0.0).then_inc(fills, 1)

        @block.scalar
        def _(act):
            act.wait_ge(ex_in, 1)
            nc.scalar.activation(ex[:], ex[:], ACT.Exp).then_inc(ex_ready, 1)

        @block.tensor
        def _(pe):
            pe.sem_inc(hot_used, 2)
            pe.wait_ge(fills, 2)
            nc.tensor.matmul(tab[:], zerob[:], zerob[:], start=True, stop=False, skip_group_check=True)
            pe.wait_ge(mask_ready, 2)
            nc.tensor.matmul(rank_bank[:], beforeb[:], maskb[:], start=True, stop=True)
            nc.tensor.matmul(cnt_bank[:], onesb[:], maskb[:], start=True, stop=True).then_inc(ranked, 1)
            pe.wait_ge(mask_ready, 3)
            nc.tensor.matmul(tile_bank[:], utile_w[:], ident[:], start=True, stop=True).then_inc(tile_ps, 1)
            with pe.Fori(0, NT // 2) as i:
                for u in range(2):
                    pe.wait_ge(hot_ready, 2 * i + u + 1)
                    for k in range(TOPK):
                        last = nc.tensor.matmul(tab[:], ohlo[:, u, k, :], ohhi[:, u, k, :], start=False, stop=False,
                                                skip_group_check=True)
                    last.then_inc(hot_used, 1)

        @block.vector
        def _(dve):
            steps = Steps(dve, dve_step)
            dve.wait_ge(cst_in, 16)
            nc.vector.tensor_copy(beforeb[:], bef).then_inc(mask_ready, 1)
            for t in range(NT):
                steps.did(nc.vector.max(m8[:, t, :], logits[:, t, :]))
            steps.settle()
            for t in range(NT):
                steps.did(nc.vector.max_index(i8[:, t, :], m8[:, t, :], logits[:, t, :]))
            nc.vector.tensor_tensor(ex[:], m8[:, :, 0:TOPK], m8[:, :, 0:1].to_broadcast([P, NT, TOPK]),
                                    ALU.subtract).then_inc(ex_in, 1)
            steps.settle()
            steps.then(nc.vector.tensor_copy(ef[:], i8[:, :, 0:TOPK]))
            for k in range(TOPK):
                steps.did(nc.vector.tensor_tensor(oh[:, k], iota[:, 0:NE].unsqueeze(1).to_broadcast([P, NT, NE]),
                                                  ef[:, :, k:k + 1].to_broadcast([P, NT, NE]), ALU.is_equal))
            steps.settle()
            steps.then(nc.vector.tensor_tensor(mask[:], oh[:, 0], oh[:, 1], ALU.add))
            steps.then(nc.vector.tensor_tensor(mask[:], mask[:], oh[:, 2], ALU.add))
            nc.vector.tensor_tensor(maskb[:].rearrange("p (t n) -> p t n", n=NE), mask[:], oh[:, 3], ALU.add).then_inc(mask_ready, 1)
            steps.then(nc.vector.memset(offs[:, 0, :], 0.0))
            dve.wait_ge(ex_ready, 1)
            steps.then(nc.vector.tensor_reduce(es[:], ex[:], AX.X, ALU.add))
            steps.then(nc.vector.reciprocal(es[:], es[:]))
            steps.did(nc.vector.tensor_tensor(wk[:], ex[:], es[:].unsqueeze(2).to_broadcast([P, NT, TOPK]), ALU.mult))
            dve.wait_ge(ranked, 1)
            for t in range(NT - 1):
                steps.then(nc.vector.tensor_tensor(offs[:, t + 1, :], offs[:, t, :], cnt_bank[:, t * NE:(t + 1) * NE], ALU.add))
            steps.then(nc.vector.tensor_tensor(tiles[:], offs[:, NT - 1, :], cnt_bank[:, (NT - 1) * NE:NT * NE], ALU.add))
            steps.then(nc.vector.tensor_scalar(tiles[:], tiles[:], float(CAP), 1.0, ALU.min, ALU.max))
            steps.then(nc.vector.tensor_copy(tiles_i[:], tiles[:]))
            steps.then(nc.vector.tensor_scalar(tiles_i[:], tiles_i[:], P - 1, None, ALU.add))
            steps.then(nc.vector.tensor_scalar(tiles_i[:], tiles_i[:], P.bit_length() - 1, None, ALU.arith_shift_right))
            steps.then(nc.vector.tensor_copy(tiles[:], tiles_i[:]))
            steps.did(nc.vector.tensor_scalar(unit[:], tok[:, 0:1], float(T), None, ALU.add))
            steps.then(nc.vector.tensor_tensor_scan(ends[:], tiles[:], offs[:, 0, :], 0.0, ALU.add, ALU.add))
            steps.did(nc.vector.tensor_scalar(utile[:], ends[:, NE - 1:NE], -1.0, None, ALU.add))
            steps.did(nc.vector.tensor_scalar(past[:], ends[:], unit[:], None, ALU.is_le))
            steps.then(nc.vector.tensor_scalar(tiles[:], tiles[:], -1.0, float(RT), ALU.mult, ALU.add))
            steps.did(nc.vector.tensor_copy(last_round[:], utile[:]))
            steps.then(nc.vector.tensor_tensor(past[:], past[:], tiles[:], ALU.mult))
            steps.did(nc.vector.tensor_scalar(last_round[:], last_round[:], 1, None, ALU.arith_shift_right))
            steps.then(nc.vector.tensor_reduce(utile[:], past[:], AX.X, ALU.add))
            steps.then(nc.vector.tensor_scalar(utile[:], utile[:], unit[:], float(ROUTES - 1), ALU.add, ALU.min))
            nc.vector.tensor_copy(utile_w[:], utile[:].to_broadcast([P, P])).then_inc(mask_ready, 1)
            steps.did(nc.vector.memset(fill[:], float(ROUTES - 1)))
            steps.then(nc.vector.tensor_tensor(pos[:], offs[:], rank_bank[:].rearrange("p (t n) -> p t n", n=NE), ALU.add))
            for k in range(TOPK):
                steps.did(nc.vector.tensor_tensor(prod[:, k], oh[:, k], pos[:], ALU.mult))
            steps.settle()
            for k in range(TOPK):
                steps.did(nc.vector.tensor_reduce(pk[:, :, k], prod[:, k], AX.X, ALU.add))
            steps.settle()
            flat = lambda v: v[:].rearrange("p t k -> p (t k)")
            steps.did(nc.vector.tensor_copy(pi[:], pk[:]))
            steps.did(nc.vector.tensor_scalar(sf[:], flat(pk), float(CAP - 1), None, ALU.min))
            steps.then(nc.vector.tensor_scalar(inb[:], flat(pk), float(CAP), None, ALU.is_lt))
            steps.did(nc.vector.tensor_scalar(li[:], pi[:], P - 1, None, ALU.bitwise_and))
            steps.then(nc.vector.tensor_scalar(bi[:], pi[:], P.bit_length() - 1, None, ALU.arith_shift_right))
            steps.did(nc.vector.tensor_copy(lo[:], flat(li)))
            steps.did(nc.vector.scalar_tensor_tensor(slot[:], flat(ef), float(CAP), sf[:], ALU.mult, ALU.add))
            steps.then(nc.vector.tensor_copy(hi[:], flat(bi)))
            steps.then(nc.vector.scalar_tensor_tensor(hi[:], flat(ef), float(RT), hi[:], ALU.mult, ALU.add))
            steps.then(nc.vector.scalar_tensor_tensor(hi[:], hi[:], 1.0, inb[:], ALU.add, ALU.mult))
            steps.then(nc.vector.tensor_scalar(hi[:], hi[:], -1.0, None, ALU.add))
            with dve.Fori(0, NT // 2) as i:
                for u in range(2):
                    t = 2 * i + u
                    dve.wait_ge(hot_used, t + 1)
                    for k in range(TOPK):
                        c = ds(TOPK * t + k, 1)
                        nc.vector.tensor_scalar(ohlo[:, u, k, :], iota, lo[:, c], None, ALU.is_equal)
                        last = nc.vector.tensor_scalar(ohhi[:, u, k, :], iota, hi[:, c], tok[:, ds(t, 1)],
                                                       ALU.is_equal, ALU.mult)
                    last.then_inc(hot_ready, 1)
            dve.wait_ge(tile_ps, 1)
            steps.did(nc.vector.tensor_copy(unit_tile[:, 0:ROUTES], tile_bank[:]))
            steps.did(nc.vector.tensor_copy(unit_tile[:, ROUTES:], fill[:]))
            dve.wait_ge(hot_used, 2 + NT)
            steps.then(nc.vector.tensor_scalar(route[:], tab[:], float(T), None, ALU.add))

    with ExitStack() as se:
        SPLIT = 3
        w13p = [sbuf(se, f"x_w13_{p}", [P, SPLIT, KD, 2 * FI], F32R) for p in ("hi", "lo")]
        w2p = [sbuf(se, f"x_w2_{p}", [P, SPLIT, KI, D], F32R) for p in ("hi", "lo")]
        ix = [sbuf(se, f"x_ix{s}", [P, 1], I32) for s in range(2)]
        xg = [sbuf(se, f"x_g{s}", [P, D]) for s in range(2)]
        xt = [[sbuf(se, f"x_t{s}_{p}", [P, KD, P], F32R) for p in ("hi", "lo")] for s in range(2)]
        gs = [sbuf(se, f"x_gs{s}", [P, FI]) for s in range(2)]
        av = [sbuf(se, f"x_av{s}", [P, FI]) for s in range(2)]
        avt = [[sbuf(se, f"x_avt{s}_{p}", [P, KI, P], F32R) for p in ("hi", "lo")] for s in range(2)]
        eo = [sbuf(se, f"x_eo{s}", [P, D]) for s in range(2)]
        xbank = [psum(se, f"x_xb{s}", [P, D]) for s in range(2)]
        hbank = [psum(se, f"x_h{s}", [P, 2 * FI]) for s in range(2)]
        abank = [psum(se, f"x_ab{s}", [P, FI]) for s in range(2)]
        obank = [psum(se, f"x_o{s}", [P, D]) for s in range(2)]
        got = [sem(f"x_got{s}") for s in range(2)]
        eo_out = [sem(f"x_out{s}") for s in range(2)]
        (fills, ix_ready, w_ready, w13_hi, w13_lo, w2_hi, w2_lo, xt_ps, xt_hi, xt_lo, h_ps, gs_ready, av_ready,
         at_ps, at_hi, at_lo, eo_ps, eo_sb) = (
            sem("x_" + n) for n in ("fills", "ix_ready", "w_ready", "w13_hi", "w13_lo", "w2_hi", "w2_lo", "xt_ps",
                                    "xt_hi", "xt_lo", "h_ps", "gs_ready", "av_ready", "at_ps", "at_hi", "at_lo",
                                    "eo_ps", "eo_sb"))
        OPEN = 2
        block = se.enter_context(nc.Block())

        def last_of(eng):
            return eng.value_load(last_round[0:1, 0:1], min_val=0, max_val=ROUTES // 2 - 1)

        def tile_of(eng, j):
            return eng.value_load(unit_tile[0:1, ds(j, 1)], min_val=0, max_val=ROUTES - 1)

        @block.gpsimd
        def _(pool):
            for s in range(2):
                nc.gpsimd.memset(xg[s][:], 0.0).then_inc(fills, 1)
            pool.wait_ge(fills, 2)

            def gather(j, s):
                pool.wait_ge(xt_ps, OPEN + j - 1)
                nc.gpsimd.tensor_copy(ix[s][:], route[:, ds(tile_of(pool, j), 1)]).then_inc(ix_ready, 1)
                pool.wait_ge(ix_ready, j + 1)
                nc.gpsimd.tensor_tensor(carry[:, s:s + 1], powers[:, 0:1], powers[:, 0:1], ALU.mult)
                nc.gpsimd.indirect_dma_start(
                    out=xg[s][:], out_offset=None, in_=r_d,
                    in_offset=bass.IndirectOffsetOnAxis(ap=ix[s][:], axis=0),
                    bounds_check=T - 1, oob_is_err=False).then_inc(got[s], 16)

            for j in range(4):
                gather(j, j % 2)
            with pool.Fori(0, last_of(pool)) as i:
                for s in range(2):
                    gather(2 * i + 4 + s, s)

        @block.sync
        def _(sp):
            def arrived(i, u):
                sp.wait_ge(w13_in[u], 16 * i + 16)
                sp.wait_ge(w2_in[u], 16 * i + 16)
                sp.sem_inc(w_ready, 1)

            with sp.Fori(0, NE // 2 - 1) as i:
                for u in range(2):
                    e = 2 * i + u
                    arrived(i, u)
                    sp.wait_ge(w13_lo, e + 1)
                    load_w13(sp, e + 2, u)
                    sp.wait_ge(w2_lo, e + 1)
                    load_w2(sp, e + 2, u)
            for u in range(2):
                arrived(NE // 2 - 1, u)

        @block.tensor
        def _(pe):
            def turn(i, s):
                pe.wait_ge(got[s], 16 * i + 16)
                for k in range(KD):
                    last = nc.tensor.transpose(xbank[s][:, k * P:(k + 1) * P], xg[s][:, k * P:(k + 1) * P], ident[:])
                last.then_inc(xt_ps, 1)

            def up(i, s, e):
                at = ds(e % SPLIT, 1)
                hi, lo = xt[s]
                pe.wait_ge(w13_lo, e + 1)
                pe.wait_ge(xt_lo, 2 * i + s + 1)
                for k in range(KD):
                    nc.tensor.matmul(hbank[s][:], hi[:, k, :], w13p[0][:, at, k, :], start=k == 0, stop=False)
                    nc.tensor.matmul(hbank[s][:], hi[:, k, :], w13p[1][:, at, k, :], start=False, stop=False)
                    last = nc.tensor.matmul(hbank[s][:], lo[:, k, :], w13p[0][:, at, k, :], start=False, stop=k == KD - 1)
                last.then_inc(h_ps, 1)

            def turn_act(i, s):
                pe.wait_ge(av_ready, OPEN + 2 * i + s + 1)
                for f in range(KI):
                    last = nc.tensor.transpose(abank[s][:, f * P:(f + 1) * P], av[s][:, f * P:(f + 1) * P], ident[:])
                last.then_inc(at_ps, 1)

            def down(i, s, e, between=None):
                at = ds(e % SPLIT, 1)
                hi, lo = avt[s]
                pe.wait_ge(w2_lo, e + 1)
                pe.wait_ge(at_hi, 2 * i + s + 1)
                pe.wait_ge(eo_sb, OPEN + 2 * i + s - 1)
                for f in range(KI):
                    nc.tensor.matmul(obank[s][:], hi[:, f, :], w2p[0][:, at, f, :], start=f == 0, stop=False)
                    nc.tensor.matmul(obank[s][:], hi[:, f, :], w2p[1][:, at, f, :], start=False, stop=False)
                    if between and f == 0:
                        between()
                pe.wait_ge(at_lo, 2 * i + s + 1)
                for f in range(KI):
                    last = nc.tensor.matmul(obank[s][:], lo[:, f, :], w2p[0][:, at, f, :], start=False, stop=f == KI - 1)
                last.then_inc(eo_ps, 1)

            for opened in (xt_ps, at_ps, eo_ps):
                pe.sem_inc(opened, OPEN)
            pe.wait_ge(fills, 2)
            turn(0, 0)
            turn(0, 1)
            def experts_of(i):
                return [tile_of(pe, 2 * i + s) // RT for s in range(2)]

            def rest(i, e, following=None):
                turn_act(i, 0)
                turn(i + 1, 0)
                turn(i + 1, 1)
                down(i, 0, e[0], between=lambda: turn_act(i, 1))
                down(i, 1, e[1])
                if following:
                    for s in range(2):
                        up(i + 1, s, following[s])

            n = last_of(pe)
            first = experts_of(0)
            for s in range(2):
                up(0, s, first[s])
            with pe.Fori(0, n) as i:
                rest(i, experts_of(i), experts_of(i + 1))
            rest(n, experts_of(n))

        @block.scalar
        def _(act):
            def turned(i, s):
                act.wait_ge(xt_ps, OPEN + 2 * i + s + 1)
                nc.scalar.copy(xt[s][0][:], xbank[s][:].rearrange("p (k n) -> p k n", n=P)).then_inc(xt_hi, 1)

            def silu(i, s):
                act.wait_ge(h_ps, 2 * i + s + 1)
                act.wait_ge(av_ready, OPEN + 2 * i + s - 1)
                nc.scalar.activation(gs[s][:], hbank[s][:, 0:FI], ACT.Silu).then_inc(gs_ready, 1)

            def turned_act(i, s):
                act.wait_ge(at_ps, OPEN + 2 * i + s + 1)
                act.wait_ge(eo_ps, OPEN + 2 * i + s - 1)
                nc.scalar.copy(avt[s][0][:], abank[s][:].rearrange("p (f n) -> p f n", n=P)).then_inc(at_hi, 1)

            act.sem_inc(eo_sb, OPEN)
            for s in range(2):
                act.sem_inc(eo_out[s], 16)
            turned(0, 0)
            turned(0, 1)
            n = last_of(act)
            with act.Fori(0, n + 1) as i:
                silu(i, 0)
                silu(i, 1)
                turned_act(i, 0)
                turned(i + 1, 0)
                turned(i + 1, 1)
                turned_act(i, 1)
                for s in range(2):
                    act.wait_ge(eo_ps, OPEN + 2 * i + s + 1)
                    act.wait_ge(eo_out[s], 16 * i + 16)
                    nc.scalar.copy(eo[s][:], obank[s][:]).then_inc(eo_sb, 1)
                    act.wait_ge(eo_sb, OPEN + 2 * i + s + 1)
                    act.dma_start(eo_d[ds(P * tile_of(act, 2 * i + s), P), :], eo[s][:]).then_inc(eo_out[s], 16)
            for s in range(2):
                act.wait_ge(eo_out[s], 16 * n + 32)
                nc.scalar.copy(eo[s][:, 0:1], gs[s][:, 0:1])

        @block.vector
        def _(dve):
            def lo_part(dst, src, hi):
                return nc.vector.tensor_tensor(dst, src, hi.bitcast(F32), ALU.subtract)

            def turned(i, s):
                dve.wait_ge(xt_hi, 2 * i + s + 1)
                lo_part(xt[s][1][:], xbank[s][:].rearrange("p (k n) -> p k n", n=P), xt[s][0][:]).then_inc(xt_lo, 1)

            def split(e):
                at, raw = ds(e % SPLIT, 1), ds(e % 2, 1)
                dve.wait_ge(w_ready, e + 1)
                nc.vector.tensor_copy(w13p[0][:, at], w13[:, raw]).then_inc(w13_hi, 1)
                nc.vector.tensor_copy(w2p[0][:, at], w2[:, raw]).then_inc(w2_hi, 1)
                dve.wait_ge(w13_hi, e + 1)
                lo_part(w13p[1][:, at], w13[:, raw], w13p[0][:, at]).then_inc(w13_lo, 1)
                dve.wait_ge(w2_hi, e + 1)
                lo_part(w2p[1][:, at], w2[:, raw], w2p[0][:, at]).then_inc(w2_lo, 1)

            def at_first_unit(j, tile):
                with dve.If(tile < ROUTES - 2 * RT):
                    with dve.If(tile % RT == 0):
                        dve.wait_ge(eo_ps, OPEN + j)
                        split(tile // RT + 2)

            def gated(i, s):
                dve.wait_ge(gs_ready, 2 * i + s + 1)
                dve.wait_ge(at_ps, OPEN + 2 * i + s - 1)
                nc.vector.tensor_tensor(av[s][:], gs[s][:], hbank[s][:, FI:2 * FI], ALU.mult).then_inc(av_ready, 1)

            def turned_act(i, s):
                dve.wait_ge(at_hi, 2 * i + s + 1)
                lo_part(avt[s][1][:], abank[s][:].rearrange("p (f n) -> p f n", n=P), avt[s][0][:]).then_inc(at_lo, 1)

            dve.sem_inc(av_ready, OPEN)
            split(0)
            turned(0, 0)
            turned(0, 1)
            split(1)
            at_first_unit(0, tile_of(dve, 0))
            with dve.Fori(0, last_of(dve) + 1) as i:
                tiles_next = [tile_of(dve, 2 * i + 1), tile_of(dve, 2 * i + 2)]
                gated(i, 0)
                turned_act(i, 0)
                gated(i, 1)
                turned(i + 1, 0)
                turned_act(i, 1)
                turned(i + 1, 1)
                for s in range(2):
                    at_first_unit(2 * i + 1 + s, tiles_next[s])

    with ExitStack() as sc:
        sx = [sbuf(sc, f"c_sx{u}", [P, TOPK], I32) for u in range(2)]
        rows = [sbuf(sc, f"c_rows{u}", [P, TOPK, D]) for u in range(2)]
        y = sbuf(sc, "c_y", [P, 2, D])
        got = [sem(f"c_got{u}") for u in range(2)]
        y_out = [sem(f"c_out{u}") for u in range(2)]
        sx_ready, dve_step, y_ready, y_free = (sem("c_" + n) for n in ("sx_ready", "dve_step", "y_ready", "y_free"))
        out_rows = out.rearrange("b (c p) d -> p (b c) d", p=P)
        block = sc.enter_context(nc.Block())

        @block.gpsimd
        def _(pool):
            with pool.Fori(0, NT // 2) as i:
                for u in range(2):
                    t = 2 * i + u
                    pool.wait_ge(y_ready, t + 1)
                    nc.gpsimd.tensor_copy(sx[u][:], slot[:, ds(TOPK * t, TOPK)]).then_inc(sx_ready, 1)
                    pool.wait_ge(sx_ready, t + 1)
                    nc.gpsimd.tensor_tensor(carry[:, u:u + 1], powers[:, 0:1], powers[:, 0:1], ALU.mult)
                    for k in range(TOPK):
                        nc.gpsimd.indirect_dma_start(
                            out=rows[u][:, k, :], out_offset=None, in_=eo_d,
                            in_offset=bass.IndirectOffsetOnAxis(ap=sx[u][:, k:k + 1], axis=0),
                            bounds_check=NE * CAP - 1, oob_is_err=False).then_inc(got[u], 16)

        @block.vector
        def _(dve):
            steps = Steps(dve, dve_step)
            dve.sem_inc(y_ready, 2)
            with steps.loop(0, NT // 2, 2 * (TOPK - 1)) as i:
                for u in range(2):
                    t = 2 * i + u
                    dve.wait_ge(got[u], 16 * TOPK * (i + 1))
                    dve.wait_ge(y_free, t + 1)
                    for k in range(TOPK):
                        ins = nc.vector.scalar_tensor_tensor(
                            y[:, u], rows[u][:, k, :], wk[:].rearrange("p t k -> p (t k)")[:, ds(TOPK * t + k, 1)],
                            x[:, ds(t, 1), :].rearrange("p o d -> p (o d)") if k == 0 else y[:, u], ALU.mult, ALU.add)
                        if k < TOPK - 1:
                            steps.then(ins)
                        else:
                            ins.then_inc(y_ready, 1)

        @block.sync
        def _(sp):
            sp.sem_inc(y_free, 2)
            with sp.Fori(0, NT // 2) as i:
                for u in range(2):
                    t = 2 * i + u
                    sp.wait_ge(y_ready, 2 + t + 1)
                    sp.dma_start(out_rows[:, ds(t, 1), :].rearrange("p o d -> p (o d)"), y[:, u]).then_inc(y_out[u], 16)
                    sp.wait_ge(y_out[u], 16 * i + 16)
                    sp.sem_inc(y_free, 1)


_INS = ["x", "ctx_2048", "L0_xattn_Wh", "L0_xattn_wg_w", "L0_xattn_wo_w", "L0_xattn_gn_gamma", "L0_xattn_gn_beta",
        "L0_ffn_w1", "L0_ffn_w2", "L0_ffn_w3", "L1_xattn_Wi", "L1_xattn_bi", "L1_xattn_Wf", "L1_xattn_bf",
        "L1_xattn_ln_scale", "L1_ffn_norm_w", "L1_ffn_gate_w", "L1_ffn_w13", "L1_ffn_w2", "L1_ffn_shared_gate_w",
        "L1_ffn_shared_up_w", "L1_ffn_shared_down_w"]


def kernel(**inputs):
    import concourse.bacc as bacc
    from concourse.bass_utils import run_bass_kernel_spmd

    nc = bacc.Bacc("TRN2", target_bir_lowering=False, num_devices=1)
    arrays = {f"in_{n}": np.ascontiguousarray(inputs[n]) for n in _INS}
    arrays["in_consts"] = shape_constants()
    a = {n[3:]: nc.dram_tensor(n, v.shape, mybir.dt.from_np(v.dtype), kind="ExternalInput").ap()
         for n, v in arrays.items()}
    out = nc.dram_tensor("out_x", (B, S, D), F32, kind="ExternalOutput").ap()
    program(nc, a, out)
    r = run_bass_kernel_spmd(nc, [arrays], core_ids=[0])
    return r.results[0]["out_x"]
```
